# Optimizing a Trainium2 kernel written in Bass

```python
import numpy as np
import jax
import jax.numpy as jnp

def _softmax(x, axis=-1):
    return jax.nn.softmax(x, axis=axis)

def _gelu(x):
    return jax.nn.gelu(x, approximate=True)

def _silu(x):
    return jax.nn.silu(x)

def _sigmoid(x):
    return jax.nn.sigmoid(x)

def _layernorm(x, axis=-1, eps=1e-05):
    m = jnp.mean(x, axis=axis, keepdims=True)
    v = jnp.var(x, axis=axis, keepdims=True)
    return (x - m) / jnp.sqrt(v + eps)

def _scatter_add(tgt, idx, src, axis=0):
    return tgt.at[idx].add(src)

def _segment_sum(src, seg, n):
    return jax.ops.segment_sum(src, seg, n)
kernel_name = 'mk_macaron_d2_jaxref_r8_e0b0c8'

def setup_inputs(seed: int=0):
    np.random.seed(seed)
    _w = jnp.asarray

    def _L0_attn_setup():
        import jax, jax.numpy as jnp
        import numpy as np
        import math
        D_MODEL = 128
        N_HEADS = 16
        HEAD_DIM = D_MODEL // N_HEADS

        def _apply_rope_full(x):
            B, S, D = x.shape
            half = D // 2
            pos = jnp.arange(S, dtype=jnp.float32)[:, None]
            freqs = 1.0 / 10000.0 ** (jnp.arange(half, dtype=jnp.float32) / half)
            ang = pos * freqs[None, :]
            sin, cos = (jnp.sin(ang), jnp.cos(ang))
            x1, x2 = (x[..., :half], x[..., half:])
            return jnp.concatenate([x1 * cos - x2 * sin, x1 * sin + x2 * cos], axis=-1)

        def _alibi_slopes(n_heads):
            return jnp.array([2.0 ** (-8.0 * (i + 1) / n_heads) for i in range(n_heads)], dtype=jnp.float32)
        key = jax.random.key(seed)
        ks = jax.random.split(key, 5)
        B, S, D = (2, 256, D_MODEL)
        scale = 1.0 / math.sqrt(D)
        return {'x': jax.random.normal(ks[0], (B, S, D), dtype=jnp.float32), 'wq': jax.random.normal(ks[1], (D, D), dtype=jnp.float32) * scale, 'wk': jax.random.normal(ks[2], (D, D), dtype=jnp.float32) * scale, 'wv': jax.random.normal(ks[3], (D, D), dtype=jnp.float32) * scale, 'out_w': jax.random.normal(ks[4], (D, D), dtype=jnp.float32) * scale, 'out_b': jnp.zeros((D,), dtype=jnp.float32)}
    _L0_attn_in = _L0_attn_setup()

    def _L0_ffn_setup():
        import jax, jax.numpy as jnp
        import numpy as np
        LATENT = 128
        LEAF_W = 64
        DEPTH = 4
        N_LEAVES = 2 ** DEPTH
        N_NODES = 2 ** DEPTH - 1
        B, S = (4, 256)

        def _fff_params(key, prefix):
            ks = jax.random.split(key, 4)
            d, h, l, n = (LATENT, LEAF_W, N_LEAVES, N_NODES)
            s_in = 1.0 / np.sqrt(d).astype(np.float32)
            s_h = 1.0 / np.sqrt(h).astype(np.float32)
            return {f'{prefix}_node_w': jax.random.normal(ks[0], (n, d), jnp.float32) * s_in, f'{prefix}_node_b': jax.random.normal(ks[1], (n,), jnp.float32) * s_in, f'{prefix}_w1': jax.random.normal(ks[2], (l, d, h), jnp.float32) * s_in, f'{prefix}_b1': jnp.zeros((l, h), jnp.float32), f'{prefix}_w2': jax.random.normal(ks[3], (l, h, d), jnp.float32) * s_h, f'{prefix}_b2': jnp.zeros((l, d), jnp.float32)}

        def _fff(x, node_w, node_b, w1, b1, w2, b2):
            Bx, Sx, D = x.shape
            xf = x.reshape(-1, D)
            N = xf.shape[0]
            cur = jnp.zeros((N,), jnp.int32)
            for _ in range(DEPTH):
                pw = node_w[cur]
                score = jnp.einsum('nd,nd->n', xf, pw) + node_b[cur]
                cur = 2 * cur + 1 + (score >= 0).astype(jnp.int32)
            leaf = cur - N_NODES
            sel = jax.nn.one_hot(leaf, N_LEAVES, dtype=xf.dtype)
            hidden_all = jax.nn.relu(jnp.einsum('nd,ldh->lnh', xf, w1) + b1[:, None, :])
            hidden = hidden_all * sel.T[:, :, None]
            out = jnp.einsum('lnh,lho->no', hidden, w2) + sel @ b2
            return out.reshape(Bx, Sx, D)
        key = jax.random.key(seed)
        kx, kq, kk, kv = jax.random.split(key, 4)
        inp = {'x': jax.random.normal(kx, (B, S, LATENT), jnp.float32)}
        inp.update(_fff_params(kq, 'q'))
        inp.update(_fff_params(kk, 'k'))
        inp.update(_fff_params(kv, 'v'))
        return inp
    _L0_ffn_in = _L0_ffn_setup()

    def _L1_attn_setup():
        import jax, jax.numpy as jnp
        import numpy as np
        D_MODEL, D_INNER, D_STATE, D_CONV, DT_RANK = (128, 256, 16, 4, 64)
        EPS = 1e-05

        def _rmsnorm(x, w):
            x = x.astype(jnp.float32)
            return x * jax.lax.rsqrt(jnp.mean(x * x, axis=-1, keepdims=True) + EPS) * w

        def _mamba_block(residual, norm_w, W_in, conv_w, conv_b, W_x, W_dt, b_dt, A_log, D, W_out):
            B, L, _ = residual.shape
            hidden = _rmsnorm(residual, norm_w)
            residual = residual.astype(jnp.float32)
            xz = hidden @ W_in
            x, z = jnp.split(xz, 2, axis=-1)
            xc = jax.lax.conv_general_dilated(x.transpose(0, 2, 1), conv_w[:, None, :], (1,), [(D_CONV - 1, 0)], dimension_numbers=('NCH', 'OIH', 'NCH'), feature_group_count=D_INNER)
            x = jax.nn.silu((xc + conv_b[None, :, None]).transpose(0, 2, 1))
            x_dbl = x @ W_x
            dt = jax.nn.softplus(x_dbl[..., :DT_RANK] @ W_dt + b_dt)
            Bm = x_dbl[..., DT_RANK:DT_RANK + D_STATE]
            Cm = x_dbl[..., DT_RANK + D_STATE:]
            A = -jnp.exp(A_log)

            def step(h, inp):
                x_t, dt_t, B_t, C_t = inp
                dA = jnp.exp(dt_t[..., None] * A)
                h = dA * h + (dt_t * x_t)[..., None] * B_t[:, None, :]
                y = jnp.einsum('bdn,bn->bd', h, C_t)
                return (h, y)
            h0 = jnp.zeros((B, D_INNER, D_STATE), jnp.float32)
            xs = (x.transpose(1, 0, 2), dt.transpose(1, 0, 2), Bm.transpose(1, 0, 2), Cm.transpose(1, 0, 2))
            _, ys = jax.lax.scan(step, h0, xs)
            y = ys.transpose(1, 0, 2) + x * D
            y = y * jax.nn.silu(z)
            out = y @ W_out
            return residual + out
        key = jax.random.key(seed)
        ks = jax.random.split(key, 10)
        s = 0.02
        residual = jax.random.normal(ks[0], (2, 256, D_MODEL), dtype=jnp.float32)
        norm_w = jnp.ones((D_MODEL,), jnp.float32)
        W_in = jax.random.normal(ks[1], (D_MODEL, 2 * D_INNER), jnp.float32) * s
        conv_w = jax.random.normal(ks[2], (D_INNER, D_CONV), jnp.float32) * s
        conv_b = jnp.zeros((D_INNER,), jnp.float32)
        W_x = jax.random.normal(ks[3], (D_INNER, DT_RANK + 2 * D_STATE), jnp.float32) * s
        W_dt = jax.random.normal(ks[4], (DT_RANK, D_INNER), jnp.float32) * s
        b_dt = jax.random.uniform(ks[5], (D_INNER,), jnp.float32, -4.0, -2.0)
        A_log = jnp.log(jnp.broadcast_to(jnp.arange(1, D_STATE + 1, dtype=jnp.float32), (D_INNER, D_STATE)))
        D = jnp.ones((D_INNER,), jnp.float32)
        W_out = jax.random.normal(ks[6], (D_INNER, D_MODEL), jnp.float32) * s
        return dict(residual=residual, norm_w=norm_w, W_in=W_in, conv_w=conv_w, conv_b=conv_b, W_x=W_x, W_dt=W_dt, b_dt=b_dt, A_log=A_log, D=D, W_out=W_out)
    _L1_attn_in = _L1_attn_setup()

    def _L1_ffn_setup():
        import jax, jax.numpy as jnp
        import numpy as np
        DIM = 128
        INTER = 256
        E = 8
        TOPK = 2
        ROUTE_SCALE = 1.0

        def _mlp(x, w1, w2, w3):
            h = jax.nn.silu(x @ w1.T) * (x @ w3.T)
            return h @ w2.T
        key = jax.random.key(seed)
        ks = jax.random.split(key, 10)
        s_in = 0.02
        return {'x': jax.random.normal(ks[0], (4, 256, DIM), dtype=jnp.float32), 'gate_w': jax.random.normal(ks[1], (E, DIM), dtype=jnp.float32) * s_in, 'gate_bias': jax.random.normal(ks[2], (E,), dtype=jnp.float32) * 0.01, 'w1': jax.random.normal(ks[3], (E, INTER, DIM), dtype=jnp.float32) * s_in, 'w2': jax.random.normal(ks[4], (E, DIM, INTER), dtype=jnp.float32) * s_in, 'w3': jax.random.normal(ks[5], (E, INTER, DIM), dtype=jnp.float32) * s_in, 'sw1': jax.random.normal(ks[6], (INTER, DIM), dtype=jnp.float32) * s_in, 'sw2': jax.random.normal(ks[7], (DIM, INTER), dtype=jnp.float32) * s_in, 'sw3': jax.random.normal(ks[8], (INTER, DIM), dtype=jnp.float32) * s_in}
    _L1_ffn_in = _L1_ffn_setup()
    _d = {'L0_attn_x': _L0_attn_in['x'], 'L0_attn_wq': _L0_attn_in['wq'], 'L0_attn_wk': _L0_attn_in['wk'], 'L0_attn_wv': _L0_attn_in['wv'], 'L0_attn_out_w': _L0_attn_in['out_w'], 'L0_attn_out_b': _L0_attn_in['out_b'], 'L0_ffn_q_node_w': _L0_ffn_in['q_node_w'], 'L0_ffn_q_node_b': _L0_ffn_in['q_node_b'], 'L0_ffn_q_w1': _L0_ffn_in['q_w1'], 'L0_ffn_q_b1': _L0_ffn_in['q_b1'], 'L0_ffn_q_w2': _L0_ffn_in['q_w2'], 'L0_ffn_q_b2': _L0_ffn_in['q_b2'], 'L0_ffn_k_node_w': _L0_ffn_in['k_node_w'], 'L0_ffn_k_node_b': _L0_ffn_in['k_node_b'], 'L0_ffn_k_w1': _L0_ffn_in['k_w1'], 'L0_ffn_k_b1': _L0_ffn_in['k_b1'], 'L0_ffn_k_w2': _L0_ffn_in['k_w2'], 'L0_ffn_k_b2': _L0_ffn_in['k_b2'], 'L0_ffn_v_node_w': _L0_ffn_in['v_node_w'], 'L0_ffn_v_node_b': _L0_ffn_in['v_node_b'], 'L0_ffn_v_w1': _L0_ffn_in['v_w1'], 'L0_ffn_v_b1': _L0_ffn_in['v_b1'], 'L0_ffn_v_w2': _L0_ffn_in['v_w2'], 'L0_ffn_v_b2': _L0_ffn_in['v_b2'], 'L1_attn_norm_w': _L1_attn_in['norm_w'], 'L1_attn_W_in': _L1_attn_in['W_in'], 'L1_attn_conv_w': _L1_attn_in['conv_w'], 'L1_attn_conv_b': _L1_attn_in['conv_b'], 'L1_attn_W_x': _L1_attn_in['W_x'], 'L1_attn_W_dt': _L1_attn_in['W_dt'], 'L1_attn_b_dt': _L1_attn_in['b_dt'], 'L1_attn_A_log': _L1_attn_in['A_log'], 'L1_attn_D': _L1_attn_in['D'], 'L1_attn_W_out': _L1_attn_in['W_out'], 'L1_ffn_gate_w': _L1_ffn_in['gate_w'], 'L1_ffn_gate_bias': _L1_ffn_in['gate_bias'], 'L1_ffn_w1': _L1_ffn_in['w1'], 'L1_ffn_w2': _L1_ffn_in['w2'], 'L1_ffn_w3': _L1_ffn_in['w3'], 'L1_ffn_sw1': _L1_ffn_in['sw1'], 'L1_ffn_sw2': _L1_ffn_in['sw2'], 'L1_ffn_sw3': _L1_ffn_in['sw3']}
    _x0 = _d['L0_attn_x']
    _d['L0_attn_x'] = jax.random.normal(jax.random.fold_in(jax.random.key(seed), 1), (4, 512, 128), dtype=_x0.dtype)
    del _x0
    return _d

def reference(L0_attn_x, L0_attn_wq, L0_attn_wk, L0_attn_wv, L0_attn_out_w, L0_attn_out_b, L0_ffn_q_node_w, L0_ffn_q_node_b, L0_ffn_q_w1, L0_ffn_q_b1, L0_ffn_q_w2, L0_ffn_q_b2, L0_ffn_k_node_w, L0_ffn_k_node_b, L0_ffn_k_w1, L0_ffn_k_b1, L0_ffn_k_w2, L0_ffn_k_b2, L0_ffn_v_node_w, L0_ffn_v_node_b, L0_ffn_v_w1, L0_ffn_v_b1, L0_ffn_v_w2, L0_ffn_v_b2, L1_attn_norm_w, L1_attn_W_in, L1_attn_conv_w, L1_attn_conv_b, L1_attn_W_x, L1_attn_W_dt, L1_attn_b_dt, L1_attn_A_log, L1_attn_D, L1_attn_W_out, L1_ffn_gate_w, L1_ffn_gate_bias, L1_ffn_w1, L1_ffn_w2, L1_ffn_w3, L1_ffn_sw1, L1_ffn_sw2, L1_ffn_sw3):

    def _L0_attn_ref(x, wq, wk, wv, out_w, out_b):
        import jax, jax.numpy as jnp
        import numpy as np
        import math
        D_MODEL = 128
        N_HEADS = 16
        HEAD_DIM = D_MODEL // N_HEADS

        def _apply_rope_full(x):
            B, S, D = x.shape
            half = D // 2
            pos = jnp.arange(S, dtype=jnp.float32)[:, None]
            freqs = 1.0 / 10000.0 ** (jnp.arange(half, dtype=jnp.float32) / half)
            ang = pos * freqs[None, :]
            sin, cos = (jnp.sin(ang), jnp.cos(ang))
            x1, x2 = (x[..., :half], x[..., half:])
            return jnp.concatenate([x1 * cos - x2 * sin, x1 * sin + x2 * cos], axis=-1)

        def _alibi_slopes(n_heads):
            return jnp.array([2.0 ** (-8.0 * (i + 1) / n_heads) for i in range(n_heads)], dtype=jnp.float32)
        B, S, D = x.shape
        H, Dh = (N_HEADS, HEAD_DIM)
        q = x @ wq.T
        k = x @ wk.T
        v = x @ wv.T
        q = _apply_rope_full(q)
        k = _apply_rope_full(k)
        q = q.reshape(B, S, H, Dh).transpose(0, 2, 1, 3)
        k = k.reshape(B, S, H, Dh).transpose(0, 2, 1, 3)
        v = v.reshape(B, S, H, Dh).transpose(0, 2, 1, 3)
        scores = jnp.einsum('bhqd,bhkd->bhqk', q, k) / math.sqrt(Dh)
        pos = jnp.arange(S, dtype=jnp.float32)
        rel = pos[None, :] - pos[:, None]
        scores = scores + _alibi_slopes(H)[None, :, None, None] * rel[None, None]
        causal = jnp.triu(jnp.ones((S, S), dtype=bool), k=1)
        scores = jnp.where(causal[None, None], jnp.float32(-1000000000.0), scores)
        attn = jax.nn.softmax(scores, axis=-1)
        out = jnp.einsum('bhqk,bhkd->bhqd', attn, v)
        out = out.transpose(0, 2, 1, 3).reshape(B, S, D)
        return out @ out_w.T + out_b

    def _L0_ffn_ref(x, q_node_w, q_node_b, q_w1, q_b1, q_w2, q_b2, k_node_w, k_node_b, k_w1, k_b1, k_w2, k_b2, v_node_w, v_node_b, v_w1, v_b1, v_w2, v_b2):
        import jax, jax.numpy as jnp
        import numpy as np
        LATENT = 128
        LEAF_W = 64
        DEPTH = 4
        N_LEAVES = 2 ** DEPTH
        N_NODES = 2 ** DEPTH - 1
        B, S = (4, 256)

        def _fff_params(key, prefix):
            ks = jax.random.split(key, 4)
            d, h, l, n = (LATENT, LEAF_W, N_LEAVES, N_NODES)
            s_in = 1.0 / np.sqrt(d).astype(np.float32)
            s_h = 1.0 / np.sqrt(h).astype(np.float32)
            return {f'{prefix}_node_w': jax.random.normal(ks[0], (n, d), jnp.float32) * s_in, f'{prefix}_node_b': jax.random.normal(ks[1], (n,), jnp.float32) * s_in, f'{prefix}_w1': jax.random.normal(ks[2], (l, d, h), jnp.float32) * s_in, f'{prefix}_b1': jnp.zeros((l, h), jnp.float32), f'{prefix}_w2': jax.random.normal(ks[3], (l, h, d), jnp.float32) * s_h, f'{prefix}_b2': jnp.zeros((l, d), jnp.float32)}

        def _fff(x, node_w, node_b, w1, b1, w2, b2):
            Bx, Sx, D = x.shape
            xf = x.reshape(-1, D)
            N = xf.shape[0]
            cur = jnp.zeros((N,), jnp.int32)
            for _ in range(DEPTH):
                pw = node_w[cur]
                score = jnp.einsum('nd,nd->n', xf, pw) + node_b[cur]
                cur = 2 * cur + 1 + (score >= 0).astype(jnp.int32)
            leaf = cur - N_NODES
            sel = jax.nn.one_hot(leaf, N_LEAVES, dtype=xf.dtype)
            hidden_all = jax.nn.relu(jnp.einsum('nd,ldh->lnh', xf, w1) + b1[:, None, :])
            hidden = hidden_all * sel.T[:, :, None]
            out = jnp.einsum('lnh,lho->no', hidden, w2) + sel @ b2
            return out.reshape(Bx, Sx, D)
        q = _fff(x, q_node_w, q_node_b, q_w1, q_b1, q_w2, q_b2)
        k = _fff(x, k_node_w, k_node_b, k_w1, k_b1, k_w2, k_b2)
        v = _fff(x, v_node_w, v_node_b, v_w1, v_b1, v_w2, v_b2)
        scale = 1.0 / np.sqrt(LATENT).astype(np.float32)
        attn = jax.nn.softmax(jnp.einsum('bqd,bkd->bqk', q, k) * scale, axis=-1)
        return jnp.einsum('bqk,bkd->bqd', attn, v)

    def _L1_attn_ref(residual, norm_w, W_in, conv_w, conv_b, W_x, W_dt, b_dt, A_log, D, W_out):
        import jax, jax.numpy as jnp
        import numpy as np
        D_MODEL, D_INNER, D_STATE, D_CONV, DT_RANK = (128, 256, 16, 4, 64)
        EPS = 1e-05

        def _rmsnorm(x, w):
            x = x.astype(jnp.float32)
            return x * jax.lax.rsqrt(jnp.mean(x * x, axis=-1, keepdims=True) + EPS) * w

        def _mamba_block(residual, norm_w, W_in, conv_w, conv_b, W_x, W_dt, b_dt, A_log, D, W_out):
            B, L, _ = residual.shape
            hidden = _rmsnorm(residual, norm_w)
            residual = residual.astype(jnp.float32)
            xz = hidden @ W_in
            x, z = jnp.split(xz, 2, axis=-1)
            xc = jax.lax.conv_general_dilated(x.transpose(0, 2, 1), conv_w[:, None, :], (1,), [(D_CONV - 1, 0)], dimension_numbers=('NCH', 'OIH', 'NCH'), feature_group_count=D_INNER)
            x = jax.nn.silu((xc + conv_b[None, :, None]).transpose(0, 2, 1))
            x_dbl = x @ W_x
            dt = jax.nn.softplus(x_dbl[..., :DT_RANK] @ W_dt + b_dt)
            Bm = x_dbl[..., DT_RANK:DT_RANK + D_STATE]
            Cm = x_dbl[..., DT_RANK + D_STATE:]
            A = -jnp.exp(A_log)

            def step(h, inp):
                x_t, dt_t, B_t, C_t = inp
                dA = jnp.exp(dt_t[..., None] * A)
                h = dA * h + (dt_t * x_t)[..., None] * B_t[:, None, :]
                y = jnp.einsum('bdn,bn->bd', h, C_t)
                return (h, y)
            h0 = jnp.zeros((B, D_INNER, D_STATE), jnp.float32)
            xs = (x.transpose(1, 0, 2), dt.transpose(1, 0, 2), Bm.transpose(1, 0, 2), Cm.transpose(1, 0, 2))
            _, ys = jax.lax.scan(step, h0, xs)
            y = ys.transpose(1, 0, 2) + x * D
            y = y * jax.nn.silu(z)
            out = y @ W_out
            return residual + out
        return _mamba_block(residual, norm_w, W_in, conv_w, conv_b, W_x, W_dt, b_dt, A_log, D, W_out)

    def _L1_ffn_ref(x, gate_w, gate_bias, w1, w2, w3, sw1, sw2, sw3):
        import jax, jax.numpy as jnp
        import numpy as np
        DIM = 128
        INTER = 256
        E = 8
        TOPK = 2
        ROUTE_SCALE = 1.0

        def _mlp(x, w1, w2, w3):
            h = jax.nn.silu(x @ w1.T) * (x @ w3.T)
            return h @ w2.T
        shape = x.shape
        xt = x.reshape(-1, DIM)
        T = xt.shape[0]
        logits = xt @ gate_w.T
        scores = jax.nn.softmax(logits.astype(jnp.float32), axis=-1)
        original_scores = scores
        biased = scores + gate_bias
        _, indices = jax.lax.top_k(biased, TOPK)
        weights = jnp.take_along_axis(original_scores, indices, axis=1)
        weights = (weights * ROUTE_SCALE).astype(x.dtype)
        combine = (jax.nn.one_hot(indices, E, dtype=weights.dtype) * weights[..., None]).sum(axis=1)
        y = jnp.zeros_like(xt)
        for e in range(E):
            y = y + _mlp(xt, w1[e], w2[e], w3[e]) * combine[:, e:e + 1]
        z = _mlp(xt, sw1, sw2, sw3)
        return (y + z).reshape(shape)
    x = L0_attn_x
    x = x + 0.5 * _L0_ffn_ref(_layernorm(x, axis=-1), L0_ffn_q_node_w, L0_ffn_q_node_b, L0_ffn_q_w1, L0_ffn_q_b1, L0_ffn_q_w2, L0_ffn_q_b2, L0_ffn_k_node_w, L0_ffn_k_node_b, L0_ffn_k_w1, L0_ffn_k_b1, L0_ffn_k_w2, L0_ffn_k_b2, L0_ffn_v_node_w, L0_ffn_v_node_b, L0_ffn_v_w1, L0_ffn_v_b1, L0_ffn_v_w2, L0_ffn_v_b2)
    x = x + _L0_attn_ref(_layernorm(x, axis=-1), L0_attn_wq, L0_attn_wk, L0_attn_wv, L0_attn_out_w, L0_attn_out_b)
    x = x + 0.5 * _L0_ffn_ref(_layernorm(x, axis=-1), L0_ffn_q_node_w, L0_ffn_q_node_b, L0_ffn_q_w1, L0_ffn_q_b1, L0_ffn_q_w2, L0_ffn_q_b2, L0_ffn_k_node_w, L0_ffn_k_node_b, L0_ffn_k_w1, L0_ffn_k_b1, L0_ffn_k_w2, L0_ffn_k_b2, L0_ffn_v_node_w, L0_ffn_v_node_b, L0_ffn_v_w1, L0_ffn_v_b1, L0_ffn_v_w2, L0_ffn_v_b2)
    x = x + 0.5 * _L1_ffn_ref(_layernorm(x, axis=-1), L1_ffn_gate_w, L1_ffn_gate_bias, L1_ffn_w1, L1_ffn_w2, L1_ffn_w3, L1_ffn_sw1, L1_ffn_sw2, L1_ffn_sw3)
    x = x + _L1_attn_ref(_layernorm(x, axis=-1), L1_attn_norm_w, L1_attn_W_in, L1_attn_conv_w, L1_attn_conv_b, L1_attn_W_x, L1_attn_W_dt, L1_attn_b_dt, L1_attn_A_log, L1_attn_D, L1_attn_W_out)
    x = x + 0.5 * _L1_ffn_ref(_layernorm(x, axis=-1), L1_ffn_gate_w, L1_ffn_gate_bias, L1_ffn_w1, L1_ffn_w2, L1_ffn_w3, L1_ffn_sw1, L1_ffn_sw2, L1_ffn_sw3)
    return x

_drawn_inputs = setup_inputs


def setup_inputs(seed=0):
    import zlib

    import numpy as np

    out = dict(_drawn_inputs(seed))
    spreads = {'L0_attn_out_b': (0.0, 0.1),
     'L0_ffn_q_b1': (0.0, 0.8),
     'L0_ffn_q_b2': (0.0, 0.8),
     'L0_ffn_k_b1': (0.0, 0.8),
     'L0_ffn_k_b2': (0.0, 0.8),
     'L0_ffn_v_b1': (0.0, 0.53),
     'L0_ffn_v_b2': (0.0, 0.272),
     'L1_attn_norm_w': (1.0, 0.6),
     'L1_attn_conv_b': (0.0, 0.8),
     'L1_attn_D': (1.0, 0.6)}
    factors = {'L0_ffn_q_node_w': 4.391,
     'L0_ffn_q_node_b': 8.0,
     'L0_ffn_q_w1': 5.101,
     'L0_ffn_q_w2': 4.245,
     'L0_ffn_k_node_w': 4.227,
     'L0_ffn_k_node_b': 8.0,
     'L0_ffn_k_w1': 4.983,
     'L0_ffn_k_w2': 4.282,
     'L0_ffn_v_node_b': 2.698,
     'L1_attn_W_in': 8.0,
     'L1_attn_conv_w': 8.0,
     'L1_attn_W_x': 8.0,
     'L1_attn_W_dt': 8.0,
     'L1_attn_b_dt': 8.0,
     'L1_attn_A_log': 8.0,
     'L1_attn_W_out': 8.0,
     'L1_ffn_gate_w': 8.0,
     'L1_ffn_gate_bias': 8.0,
     'L1_ffn_w1': 8.0,
     'L1_ffn_w2': 8.0,
     'L1_ffn_w3': 8.0,
     'L1_ffn_sw1': 8.0,
     'L1_ffn_sw2': 8.0,
     'L1_ffn_sw3': 8.0}
    for name, (base, spread) in spreads.items():
        noise = np.random.default_rng([zlib.crc32(name.encode()), seed]).standard_normal(out[name].shape)
        drawn = base * np.exp(spread * noise) if base else spread * noise
        out[name] = jnp.asarray(drawn.astype(out[name].dtype))
    for name, factor in factors.items():
        out[name] = (out[name] * factor).astype(out[name].dtype)
    return out
```

```python
from contextlib import ExitStack

import numpy as np
import concourse.bass as bass
from concourse import mybir

F32 = mybir.dt.float32
F32R = mybir.dt.float32r
BF16 = mybir.dt.bfloat16
ALU = mybir.AluOpType
ACT = mybir.ActivationFunctionType
AX_X = mybir.AxisListType.X

P = 128
T = 512
NT = T // P
BATCHES = 4
PAIRS = BATCHES // 2
LEAVES, LEAF_W, TREES = 16, 64, 3
M1 = LEAVES * LEAF_W // P
STEPS = TREES * M1
EXPERTS, MLPS = 8, 9
MSTEPS = MLPS * 2
HEADS, DH, SLOTS = 16, 8, 6
NSTATE, NHALF = 16, 2
EPS = 1e-5
LEAF_SCALE = float(np.float32(1.0) / np.sqrt(P).astype(np.float32))
HEAD_SCALE = float(1.0 / np.sqrt(np.float32(DH)))

LAYERS = ["ffn", "mha", "ffn", "moe", "mamba", "moe"]
UNITS = [(kind, batch) for kind in LAYERS for batch in range(2)]
COUNT = {kind: sum(1 for u in UNITS if u[0] == kind) for kind in LAYERS}
COUNT["unit"] = len(UNITS)
Q_PARTS = [0, 0, 1, 0, 2, 1]
K_PARTS = [0, 1, 0, 2, 0, 1]
DVE_STAGES = {1: "stats", 3: "rows", 5: "rms", 8: "low", 10: "first", 12: "second", 14: "third", 16: "fourth"}
ACT_STAGES = {2: "guess", 4: "rms", 7: "high", 11: "exp"}
PE_STAGES = {6: "turn", 9: "first", 11: "second", 13: "third", 15: "fourth"}

MAX_ROW = SLOTS * DH


class Signal:

    def __init__(self, sem, kind, per, step=1):
        self.sem, self.kind, self.per, self.step = sem, kind, per, step
        self.made = 0

    def by(self, instruction):
        self.made += 1
        instruction.then_inc(self.sem, self.step)

    def at(self, k, i):
        assert 0 <= i < self.per and 0 <= k < COUNT[self.kind]
        return (k * self.per + i + 1) * self.step

    def whole(self):
        assert self.made == self.per * COUNT[self.kind], (self.made, self.per, self.kind)


def program(nc, A, out):
    with ExitStack() as ctx:
        def sb(name, shape, dt=F32, stack=ctx):
            return stack.enter_context(nc.sbuf_tensor(name, shape, dt))

        def sem(name):
            return ctx.enter_context(nc.semaphore(name))

        bank = ctx.enter_context(nc.psum_tensor("bank", [P, 8, T], F32))

        fw1 = [sb(f"fw1_{s}", [P, TREES, M1 * P], F32R) for s in "hl"]
        fw2 = [sb(f"fw2_{s}", [P, TREES, M1, P], F32R) for s in "hl"]
        mw = [sb(f"mw_{s}", [P, MLPS, 6, P], F32R) for s in "hl"]
        aw = [sb(f"aw_{s}", [P, 5, P], F32R) for s in "hl"]
        win = [sb(f"win_{s}", [P, 4, P], F32R) for s in "hl"]
        rw = [sb(f"rw_{s}", [P, 96 + EXPERTS], F32R) for s in "hl"]
        biasw = sb("biasw", [P, TREES * (M1 * P + P)], BF16)
        b1w = biasw[:, 0:TREES * M1 * P].rearrange("p (t n) -> p t n", t=TREES)
        b2w = biasw[:, TREES * M1 * P:].rearrange("p (t n) -> p t n", t=TREES)
        owT = sb("owT", [P, 4, P])
        wx = sb("wx", [P, NHALF, 160])
        wdt = sb("wdt", [64, NHALF, P])
        wout = sb("wout", [P, NHALF, P])
        col = sb("col", [P, 20])
        leaf_thr, node_b, norm_w, eps, out_b = (col[:, i:i + 1] for i in range(5))
        conv_w = col[:, 5:13].rearrange("p (m c) -> p m c", m=NHALF)
        conv_b, b_dt, d_skip = col[:, 13:15], col[:, 15:17], col[:, 17:19]
        amat = sb("amat", [P, NHALF, NSTATE])
        gate_b = sb("gate_b", [P, EXPERTS])
        tri = sb("tri", [P, EXPERTS, EXPERTS])
        ident = sb("ident", [P, P])
        spread = sb("spread", [P, P])
        cbf = sb("cbf", [P, 3, P], BF16)
        identb, mask_qk, mask_kq = cbf[:, 0, :], cbf[:, 1, :], cbf[:, 2, :]
        tree = sb("tree", [96, TREES, P], BF16)
        pick = sb("pick", [96, 32], BF16)

        X = sb("X", [P, 2, NT, P])
        xn = sb("xn", [P, 2, NT, P])
        xT = [sb(f"xT_{s}", [P, 2, T], F32R) for s in "hl"]
        R = sb("R", [P, 2, TREES, T], BF16)
        xm = [R[:, p, 0:2, :].rearrange("p a t -> p (a t)").bitcast(F32).rearrange("p (t d) -> p t d", t=NT)
              for p in range(2)]
        cmp = [R[:, p, 1:3, :].rearrange("p a t -> p (a t)").bitcast(F32)
               .rearrange("p (c t a b) -> p c t a b", c=2, t=NT, a=EXPERTS) for p in range(2)]
        dbit = sb("dbit", [96, T], BF16)
        st = sb("st", [P, NT, 6])
        mv = sb("mv", [P, NT, 2])
        small = sb("small", [P, 8, NT])
        lnv, y0, ve, y2, rstd, gmax, gsum, grec = (small[:, i, :] for i in range(8))
        gbuf = sb("gbuf", [P, 8, NT, EXPERTS])
        glog, gexp, gsc, gbi, grank, gcmb, gr1, gr2 = (gbuf[:, i] for i in range(8))
        cparts = sb("cparts", [P, NT, 96], BF16)

        lo_stack = ExitStack()
        stage_w = [sb("stage_fw1", [P, TREES, M1 * P], stack=lo_stack),
                   sb("stage_fw2", [P, TREES, M1, P], stack=lo_stack),
                   X[:].rearrange("p a t d -> p (a t) d")[:, 0:5],
                   xn[:, 0], xn[:, 1, 0, 0:96 + EXPERTS],
                   sb("stage_mw", [P, MLPS, 6, P], stack=lo_stack)]
        lo_stack.close()
        lo_stack = ExitStack()
        stage_b = sb("stage_b", [P, TREES * (M1 * P + P)], stack=lo_stack)
        rest_b = sb("rest_b", [P, TREES * (M1 * P + P)], stack=lo_stack)
        lo_stack.close()

        s = ExitStack()
        f_h = [sb(f"f_h{c}", [P, 4, T], F32R, s) for c in "hl"]
        f_q = [sb(f"f_q{c}", [P, T], F32R, s) for c in "hl"]
        f_k = [sb(f"f_k{c}", [P, T], F32R, s) for c in "hl"]
        f_vT = sb("f_vT", [P, T], F32, s)
        f_v = sb("f_v", [P, NT, P], F32, s)
        f_p = sb("f_p", [P, 2, T], F32, s)
        f_pT = sb("f_pT", [P, NT, T], F32, s)
        f_s = sb("f_s", [P, 5, NT], F32, s)
        s.close()

        s = ExitStack()
        m_sl = sb("m_sl", [P, 2, T], F32, s)
        m_t = sb("m_t", [P, 2, T], F32, s)
        m_h = sb("m_h", [P, 3, T], F32, s)
        m_hh = [sb(f"m_hh{c}", [P, 3, T], F32R, s) for c in "hl"]
        m_yT = sb("m_yT", [P, T], F32, s)
        s.close()

        s = ExitStack()
        a_q = sb("a_q", [P, HEADS // 2, T], BF16, s)
        a_k = sb("a_k", [P, HEADS, T], BF16, s)
        a_v = sb("a_v", [P, NT, HEADS, 32], F32, s)
        a_p = sb("a_p", [P, 4, 2, T], F32, s)
        a_o = sb("a_o", [P, T], F32, s)
        rope = sb("rope", [P, 2, T], F32, s)
        a_mx = sb("a_mx", [P, NT, HEADS], F32, s)
        a_mr = sb("a_mr", [P, NT, HEADS], F32, s)
        a_mp = sb("a_mp", [P, NT, 3, HEADS], BF16, s)
        a_mT = sb("a_mT", [48, T], BF16, s)
        s.close()
        a_rec, a_on = rope[:, 0, :], rope[:, 1, :]
        a_yT = a_rec
        a_rot = [[a_p[:, side, 0, :], a_p[:, side, 1, :]] for side in range(2)]
        a_part = [[a_p[:, 2 + side, c // 2, :].bitcast(BF16)[:, (c % 2) * T:(c % 2 + 1) * T] for c in range(3)]
                  for side in range(2)]

        s = ExitStack()
        n_xp = sb("n_xp", [P, NHALF, T + 4], F32, s)
        n_xc = sb("n_xc", [P, NHALF, T], F32, s)
        n_sz = sb("n_sz", [P, NHALF, T], F32, s)
        n_dtr = sb("n_dtr", [64, T], F32, s)
        n_dt = sb("n_dt", [P, NHALF, T], F32, s)
        n_dtx = sb("n_dtx", [P, NHALF, T], F32, s)
        n_da = sb("n_da", [P, NHALF, T], F32, s)
        n_db = sb("n_db", [P, NHALF, T], F32, s)
        n_h = sb("n_h", [P, NHALF, T], F32, s)
        n_hc = sb("n_hc", [P, NHALF, T], F32, s)
        n_cs = sb("n_cs", [P, 2, T], F32, s)
        n_bc = sb("n_bc", [96, T], BF16, s)
        n_r = sb("n_r", [96, T], F32, s)
        s.close()
        n_cv = n_cor = n_hc
        n_abs, n_u, n_ln, n_low, n_pos = n_db, n_h, n_da, n_cs, n_dtx
        n_yT = n_cs[:, 0, :]

        parts_dram = nc.dram_tensor("parts_dram", [2, 3, P, T], BF16, kind="Internal").ap()
        max_dram = nc.dram_tensor("max_dram", [48, T], BF16, kind="Internal").ap()

        signals = []

        def sig(name, kind, per, step=1):
            signals.append(Signal(sem(name), kind, per, step))
            return signals[-1]

        loaded = sem("loaded")
        split_done = sem("split_done")
        setup_done = sem("setup_done")
        pair_done = sem("pair_done")
        dve_set = sem("dve_set")
        unit_done = sem("unit_done")
        x_in = sem("x_in")
        x_out = sem("x_out")
        dve_step = sem("dve_step")
        act_step = sem("act_step")

        g_var = sig("g_var", "unit", 1)
        g_rsq = sig("g_rsq", "unit", 1)
        r_var = sig("r_var", "mamba", 1)
        r_rsq = sig("r_rsq", "mamba", 1)
        g_xn = sig("g_xn", "unit", 1)
        g_tr = sig("g_tr", "unit", 1)
        g_xh = sig("g_xh", "unit", 1)
        g_xl = sig("g_xl", "unit", 1)
        t_sc = sig("t_sc", "ffn", 1)
        t_bit = sig("t_bit", "ffn", 1)
        t_cnt = sig("t_cnt", "ffn", TREES)
        t_sel = sig("t_sel", "ffn", TREES)
        e_log = sig("e_log", "moe", 1)
        e_sub = sig("e_sub", "moe", 1)
        e_exp = sig("e_exp", "moe", 1)
        e_prt = sig("e_prt", "moe", 1)
        e_tr = sig("e_tr", "moe", 1)
        e_row = sig("e_row", "moe", 1)
        f_s1 = sig("f_s1", "ffn", STEPS)
        f_hi = sig("f_hi", "ffn", STEPS)
        f_lo = sig("f_lo", "ffn", STEPS)
        f_s2 = sig("f_s2", "ffn", STEPS)
        f_evh = sig("f_evh", "ffn", TREES)
        f_evl = sig("f_evl", "ffn", 2)
        f_vtr = sig("f_vtr", "ffn", 1)
        f_vok = sig("f_vok", "ffn", 1)
        f_sco = sig("f_sco", "ffn", NT)
        f_max = sig("f_max", "ffn", NT)
        f_prob = sig("f_prob", "ffn", NT)
        f_ptr = sig("f_ptr", "ffn", NT)
        f_pok = sig("f_pok", "ffn", NT)
        f_pv = sig("f_pv", "ffn", NT)
        m_a = sig("m_a", "moe", MSTEPS)
        m_b = sig("m_b", "moe", MSTEPS)
        m_cr = sig("m_cr", "moe", EXPERTS)
        m_silu = sig("m_silu", "moe", MSTEPS)
        m_ts = sig("m_ts", "moe", 2 * EXPERTS)
        m_hs = sig("m_hs", "moe", MSTEPS)
        m_hi = sig("m_hi", "moe", MSTEPS)
        m_lo = sig("m_lo", "moe", MSTEPS)
        m_s2 = sig("m_s2", "moe", MSTEPS)
        m_y = sig("m_y", "moe", 1)
        m_ytr = sig("m_ytr", "moe", 1)
        SLOT1 = [(0, 8 * i, 8) for i in range(2)] + [(1, 4 * i, 4) for i in range(4)] + \
                [(qt, 2 * i, 2) for qt in (2, 3) for i in range(8)]
        a_proj = sig("a_proj", "mha", 5)
        a_rotd = sig("a_rotd", "mha", 2)
        a_prt = sig("a_prt", "mha", 6)
        a_res = sig("a_res", "mha", 4)
        a_fill = sig("a_fill", "mha", 3)
        a_vok = sig("a_vok", "mha", 1)
        a_wr = sig("a_wr", "mha", 6, 16)
        a_ld = sig("a_ld", "mha", 4 * SLOTS, 16)
        a_cst = sig("a_cst", "mha", 5, 16)
        a_s1 = sig("a_s1", "mha", len(SLOT1))
        a_m1 = sig("a_m1", "mha", len(SLOT1))
        a_mpt = sig("a_mpt", "mha", 1)
        a_mtr = sig("a_mtr", "mha", 1)
        a_mok = sig("a_mok", "mha", 1)
        a_mwr = sig("a_mwr", "mha", 1, 16)
        a_mld = sig("a_mld", "mha", 2, 16)
        NS2 = 4 * NT * 2
        a_s2 = sig("a_s2", "mha", NS2)
        a_e2 = sig("a_e2", "mha", NS2)
        a_pv = sig("a_pv", "mha", 4 * NT)
        a_osb = sig("a_osb", "mha", 4)
        a_rep = sig("a_rep", "mha", 4)
        a_norm = sig("a_norm", "mha", 4)
        a_out = sig("a_out", "mha", 4)
        a_y = sig("a_y", "mha", 1)
        a_ytr = sig("a_ytr", "mha", 1)
        n_in = sig("n_in", "mamba", 4)
        n_fill = sig("n_fill", "mamba", 1)
        n_xps = sig("n_xps", "mamba", 2)
        n_cvs = sig("n_cvs", "mamba", 2)
        n_sil = sig("n_sil", "mamba", 4)
        n_xdb = sig("n_xdb", "mamba", 2)
        n_dtc = sig("n_dtc", "mamba", 1)
        n_bc1 = sig("n_bc1", "mamba", 1)
        n_bcp = sig("n_bcp", "mamba", 1)
        n_dtp = sig("n_dtp", "mamba", 2)
        n_abss = sig("n_abss", "mamba", 2)
        n_us = sig("n_us", "mamba", 1)
        n_lns = sig("n_lns", "mamba", 1)
        n_a1 = sig("n_a1", "mamba", 1)
        n_lows = sig("n_lows", "mamba", 1)
        n_poss = sig("n_poss", "mamba", 1)
        n_dts = sig("n_dts", "mamba", 1)
        n_dtxs = sig("n_dtxs", "mamba", 1)
        n_br = sig("n_br", "mamba", NSTATE)
        n_cr = sig("n_cr", "mamba", NSTATE)
        n_das = sig("n_das", "mamba", 2 * NSTATE)
        n_csc = sig("n_csc", "mamba", NSTATE)
        n_dbs = sig("n_dbs", "mamba", 2 * NSTATE)
        n_scan = sig("n_scan", "mamba", 2 * NSTATE)
        n_hcs = sig("n_hcs", "mamba", 2 * NSTATE)
        n_ya = sig("n_ya", "mamba", 2 * NSTATE)
        n_y = sig("n_y", "mamba", 1)
        n_o = sig("n_o", "mamba", 1)
        n_oc = sig("n_oc", "mamba", 1)
        n_otr = sig("n_otr", "mamba", 1)

        kth = [sum(1 for v in UNITS[:u] if v[0] == UNITS[u][0]) for u in range(len(UNITS))]
        NU = len(UNITS)

        def unit_end(eng, j, u):
            eng.drain().then_inc(unit_done, 1)
            if u < NU - 1:
                eng.wait_ge(unit_done, 4 * (u + 1))
            else:
                eng.wait_ge(pair_done, j + 1)

        def flat(ap):
            return ap.rearrange("p a b -> p (a b)")

        numbers = [x.num for x in (unit_done, x_in, x_out, dve_step, act_step)] + [x.sem.num for x in signals]
        assert numbers == list(range(unit_done.num, unit_done.num + len(numbers)))
        block = ctx.enter_context(nc.Block())

        @block.sync
        def _(sp):
            weights = [(stage_w[0], "fw1"), (stage_w[1], "fw2"), (stage_w[2], "aw"), (stage_w[3], "win"),
                       (stage_w[4], "rw"), (stage_w[5], "mw")]
            rest = [(owT, "owT"), (wx, "wx"), (wdt, "wdt"), (wout, "wout"), (col, "col"), (amat, "a_log"),
                    (gate_b, "gate_b"), (tri, "tri"), (ident, "ident"), (spread, "spread"),
                    (cbf, "cbf"), (tree, "tree"), (pick, "pick")]
            for dst, name in weights + rest:
                sp.dma_start(dst[:], A[name]).then_inc(loaded, 16)
            sp.dma_start(biasw[0:32, :], A["leaf_mask"]).then_inc(loaded, 16)
            sp.wait_ge(split_done, 7)
            sp.wait_ge(dve_set, 6)
            sp.dma_start(stage_b[:], A["bias"]).then_inc(loaded, 16)
            with sp.Fori(0, PAIRS) as j:
                for p in range(2):
                    sp.dma_start(X[:, p], A["x"][bass.ds(j * 2 + p, 1)].rearrange("o t p d -> p (o t) d")) \
                        .then_inc(x_in, 16)
                for u, (kind, p) in enumerate(UNITS):
                    k = kth[u]
                    if kind == "mha":
                        sp.wait_ge(unit_done, 4 * u)
                        a_cst.by(sp.dma_start(rope[:], A["rope"]))
                        for odd in range(2):
                            r = 64 * odd + MAX_ROW
                            a_cst.by(sp.dma_start(a_q[r:r + 16], A["q_rows"][:, odd]))
                            a_cst.by(sp.dma_start(a_k[r:r + 16, odd::2], A["k_rows"][:, odd]))
                        for side in range(2):
                            for c in range(3):
                                sp.wait_ge(a_prt.sem, a_prt.at(k, 3 * side + c))
                                a_wr.by(sp.dma_start(parts_dram[side, c], a_part[side][c]))
                            sp.wait_ge(a_wr.sem, a_wr.at(k, 3 * side + 2))
                            for slot in range(SLOTS):
                                which = (Q_PARTS, K_PARTS)[side][slot]
                                src = parts_dram[side, which].rearrange("(h o d) t -> o d h t", o=2, d=DH)
                                for odd in range(2):
                                    r = 64 * odd + DH * slot
                                    dst = a_q[r:r + DH] if side == 0 else a_k[r:r + DH, odd::2]
                                    a_ld.by(sp.dma_start(dst, src[odd]))
                        sp.wait_ge(a_mok.sem, a_mok.at(k, 0))
                        a_mwr.by(sp.dma_start(max_dram, a_mT[:]))
                        sp.wait_ge(a_mwr.sem, a_mwr.at(k, 0))
                        for odd in range(2):
                            r = 64 * odd + MAX_ROW
                            a_mld.by(sp.dma_start(a_q[r:r + 3],
                                                  max_dram.rearrange("(c h o) t -> o c h t", c=3, o=2)[odd]))
                sp.wait_ge(unit_done, 4 * NU)
                for p in range(2):
                    sp.dma_start(out[bass.ds(j * 2 + p, 1)].rearrange("o t p d -> p (o t) d"), X[:, p]).then_inc(x_out, 16)
                sp.wait_ge(x_out, 32)
                sp.sem_clear(range(numbers[0], numbers[-1] + 1))
                sp.sem_inc(pair_done, 1)

        NLOAD = 20

        @block.gpsimd
        def _(pool):
            with ExitStack():
                pool.memset(cparts[:], 0.0).then_inc(setup_done, 1)
            with pool.Fori(0, PAIRS) as j:
                for u, (kind, p) in enumerate(UNITS):
                    k = kth[u]
                    if kind == "moe":
                        for i in range(MSTEPS):
                            pool.wait_ge(m_hi.sem, m_hi.at(k, i))
                            m_lo.by(nc.gpsimd.tensor_tensor(m_hh[1][:, i % 3, :], m_h[:, i % 3, :],
                                                            m_hh[0][:, i % 3, :].bitcast(F32), ALU.subtract))
                    if kind == "mha":
                        a_fill.by(nc.gpsimd.memset(a_v[:, :, :, DH:32], 1.0))
                        for odd in (1, 0):
                            pool.wait_ge(a_fill.sem, a_fill.at(k, 1 - odd))
                            other = a_k[64 * (1 - odd):64 * (1 - odd) + 64, odd::2]
                            a_fill.by(nc.gpsimd.memset(other.bitcast(F32), 0.0))
                        pool.wait_ge(a_fill.sem, a_fill.at(k, 2))
                        for side in range(2):
                            for c in range(2):
                                pool.wait_ge(a_prt.sem, a_prt.at(k, 3 * side + c))
                                full = a_rot[side][0]
                                a_res.by(nc.gpsimd.tensor_tensor(full, full, a_part[side][c], ALU.subtract))
                    if kind == "mamba":
                        n_fill.by(nc.gpsimd.memset(n_xp[:, :, 0:3], 0.0))
                        pool.wait_ge(n_us.sem, n_us.at(k, 0))
                        n_a1.by(nc.gpsimd.tensor_scalar(n_low[:], n_u[:], -0.5, 1.0, ALU.mult, ALU.add))
                        pool.wait_ge(n_a1.sem, n_a1.at(k, 0))
                        n_lows.by(nc.gpsimd.tensor_tensor(n_low[:], n_low[:], n_u[:], ALU.mult))
                        for n in range(2 * NSTATE):
                            m = n % 2
                            pool.wait_ge(n_scan.sem, n_scan.at(k, n))
                            pool.wait_ge(n_csc.sem, n_csc.at(k, n // 2))
                            if n >= 2:
                                pool.wait_ge(n_ya.sem, n_ya.at(k, n - 2))
                            n_hcs.by(nc.gpsimd.tensor_tensor(n_hc[:, m, :], n_h[:, m, :], n_cs[:, n // 2 % 2, :],
                                                             ALU.mult))
                    unit_end(pool, j, u)

        @block.scalar
        def _(act):
            act.wait_ge(loaded, 16 * NLOAD)
            for dst, src in ((fw1, stage_w[0]), (fw2, stage_w[1]), (aw, stage_w[2]), (win, stage_w[3]),
                             (rw, stage_w[4]), (mw, stage_w[5])):
                nc.scalar.activation(dst[0][:], src[:], ACT.Copy).then_inc(split_done, 1)
            nc.scalar.activation(amat[:], amat[:], ACT.Exp).then_inc(split_done, 1)
            act.wait_ge(split_done, 7)
            nc.scalar.mul(amat[:], amat[:], -1.0).then_inc(split_done, 1)
            act.wait_ge(split_done, 8)
            nc.scalar.activation(amat[:], amat[:], ACT.Copy).then_inc(setup_done, 1)
            act.wait_ge(setup_done, 3)

            def prologue(j, u, stage):
                if u == NU:
                    return
                kind, p = UNITS[u]
                k = kth[u]
                if stage == "guess":
                    act.wait_ge(g_var.sem, g_var.at(u, 0))
                    act.activation(lnv, mv[:, :, 1], ACT.Ln, bias=eps).then_inc(act_step, 1)
                    chain_act(j)
                    g_rsq.by(act.activation(y0, lnv, ACT.Exp, scale=-0.5))
                if stage == "rms" and kind == "mamba":
                    act.wait_ge(r_var.sem, r_var.at(k, 0))
                    act.activation(lnv, ve, ACT.Ln).then_inc(act_step, 1)
                    chain_act(j)
                    r_rsq.by(act.activation(y0, lnv, ACT.Exp, scale=-0.5))
                if stage == "high":
                    act.wait_ge(g_tr.sem, g_tr.at(u, 0))
                    g_xh.by(act.activation(xT[0][:, p, :], bank[:, 7, :], ACT.Copy,
                                           scale=norm_w if kind == "mamba" else 1.0))
                if stage == "exp" and kind == "moe":
                    act.wait_ge(e_sub.sem, e_sub.at(k, 0))
                    e_exp.by(act.activation(gexp, glog, ACT.Exp))

            steps = [0]

            def chain_act(j):
                steps[0] += 1
                act.wait_ge(act_step, steps[0])

            def ffn(j, u, k):
                for i in range(STEPS + 1):
                    if i < STEPS:
                        act.wait_ge(f_s1.sem, f_s1.at(k, i))
                        if i >= 4:
                            act.wait_ge(f_s2.sem, f_s2.at(k, i - 4))
                        f_hi.by(act.activation(f_h[0][:, i % 4, :], bank[:, i % 3, :], ACT.Relu))
                    if i in ACT_STAGES:
                        prologue(j, u + 1, ACT_STAGES[i])
                    if i in (11, 19):
                        t = (11, 19).index(i)
                        act.wait_ge(f_s2.sem, f_s2.at(k, M1 * t + M1 - 1))
                        f_evh.by(act.activation((f_q, f_k)[t][0][:], bank[:, 3 + t, :], ACT.Copy))
                    if i in (21, 23):
                        probs(j, k, (i - 21) // 2)
                    if i == 23:
                        copy_pT(j, k, 0)
                act.wait_ge(f_s2.sem, f_s2.at(k, STEPS - 1))
                f_evh.by(act.activation(f_vT[:], bank[:, 3, :], ACT.Copy))
                copy_pT(j, k, 1)
                probs(j, k, 2)
                copy_pT(j, k, 2)
                probs(j, k, 3)
                copy_pT(j, k, 3)

            def probs(j, k, qt):
                act.wait_ge(f_max.sem, f_max.at(k, qt))
                if qt >= 2:
                    act.wait_ge(f_ptr.sem, f_ptr.at(k, qt - 2))
                f_prob.by(act.activation(f_p[:, qt % 2, :], bank[:, 5, :], ACT.Exp, bias=f_s[:, 1, qt:qt + 1],
                                         scale=LEAF_SCALE, accum_out=f_s[:, 2, qt:qt + 1]))

            def copy_pT(j, k, qt):
                act.wait_ge(f_ptr.sem, f_ptr.at(k, qt))
                f_pok.by(act.activation(f_pT[:, :, qt * P:(qt + 1) * P],
                                        bank[:, 6, :].rearrange("p (t q) -> p t q", t=NT), ACT.Copy))

            def moe(j, u, k):
                for i in range(MSTEPS + 1):
                    if i < MSTEPS:
                        act.wait_ge(m_a.sem, m_a.at(k, i))
                        if i >= 2:
                            act.wait_ge(m_ts.sem, m_ts.at(k, i - 2))
                        m_silu.by(act.activation(m_sl[:, i % 2, :], bank[:, i % 2, :], ACT.Silu))
                    if i >= 1:
                        act.wait_ge(m_hs.sem, m_hs.at(k, i - 1))
                        if i - 1 >= 3:
                            act.wait_ge(m_s2.sem, m_s2.at(k, i - 4))
                        m_hi.by(act.activation(m_hh[0][:, (i - 1) % 3, :], m_h[:, (i - 1) % 3, :], ACT.Copy))
                    if i in ACT_STAGES:
                        prologue(j, u + 1, ACT_STAGES[i])
                act.wait_ge(m_s2.sem, m_s2.at(k, MSTEPS - 1))
                m_y.by(act.activation(m_yT[:], bank[:, 6, :], ACT.Copy))

            def mha(j, u, k):
                for side in range(2):
                    full = a_rot[side][0]
                    for c in range(3):
                        if c == 0:
                            act.wait_ge(a_rotd.sem, a_rotd.at(k, side))
                        else:
                            act.wait_ge(a_res.sem, a_res.at(k, 2 * side + c - 1))
                        a_prt.by(act.activation(a_part[side][c], full, ACT.Copy))
                for stage in ACT_STAGES.values():
                    prologue(j, u + 1, stage)
                act.wait_ge(a_mtr.sem, a_mtr.at(k, 0))
                a_mok.by(act.activation(a_mT[:], bank[0:48, 4, 0:T // 2].bitcast(BF16), ACT.Copy))
                act.wait_ge(a_wr.sem, a_wr.at(k, 5))
                for s_ in range(NS2):
                    g, kt = s_ // (2 * NT), s_ // 2 % NT
                    w = T - kt * P
                    act.wait_ge(a_s2.sem, a_s2.at(k, s_))
                    if s_ >= 4:
                        act.wait_ge(a_pv.sem, a_pv.at(k, (s_ - 4) // 2))
                    b = 2 * (s_ % 2)
                    a_e2.by(act.activation(a_p[:, s_ % 4, :, 0:w], bank[:, b:b + 2, 0:w], ACT.Exp))
                    if s_ % 8 == 3 and g >= 1:
                        heads_out(j, k, g - 1)
                heads_out(j, k, 3)
                act.wait_ge(a_out.sem, a_out.at(k, 3))
                a_y.by(act.activation(a_yT, bank[:, 5, :], ACT.Identity, bias=out_b))

            def heads_out(j, k, g):
                act.wait_ge(a_pv.sem, a_pv.at(k, NT * g + NT - 1))
                if g >= 1:
                    act.wait_ge(a_norm.sem, a_norm.at(k, g - 1))
                a_osb.by(act.activation(a_o[:], bank[:, 6, :], ACT.Copy))

            def mamba(j, u, k):
                for m in range(2):
                    act.wait_ge(n_in.sem, n_in.at(k, m))
                    n_xps.by(act.activation(n_xp[:, m, 3:3 + T], bank[:, m, :], ACT.Copy))
                for m in range(2):
                    act.wait_ge(n_in.sem, n_in.at(k, 2 + m))
                    n_sil.by(act.activation(n_sz[:, m, :], bank[:, 2 + m, :], ACT.Silu))
                for m in range(2):
                    act.wait_ge(n_cvs.sem, n_cvs.at(k, m))
                    n_sil.by(act.activation(n_xc[:, m, :], n_cv[:, m, :], ACT.Silu))
                act.wait_ge(n_xdb.sem, n_xdb.at(k, 0))
                n_dtc.by(act.activation(n_dtr[:], bank[0:64, 4, :], ACT.Copy))
                act.wait_ge(n_xdb.sem, n_xdb.at(k, 1))
                n_bc1.by(act.activation(n_bc[:], bank[0:96, 5, :], ACT.Copy))
                for m in range(2):
                    act.wait_ge(n_dtp.sem, n_dtp.at(k, m))
                    n_abss.by(act.activation(n_abs[:, m, :], bank[:, m, :], ACT.Abs, bias=b_dt[:, m:m + 1]))
                act.wait_ge(n_abss.sem, n_abss.at(k, 1))
                n_us.by(act.activation(n_u[:], n_abs[:], ACT.Exp, scale=-1.0))
                act.wait_ge(n_us.sem, n_us.at(k, 0))
                n_lns.by(act.activation(n_ln[:], n_u[:], ACT.Ln, bias=1.0))
                act.wait_ge(n_dts.sem, n_dts.at(k, 0))
                for n in range(NSTATE):
                    for m in range(NHALF):
                        if n >= 1:
                            act.wait_ge(n_scan.sem, n_scan.at(k, 2 * n + m - 2))
                        n_das.by(act.activation(n_da[:, m, :], n_dt[:, m, :], ACT.Exp, scale=amat[:, m, n:n + 1]))
                    act.wait_ge(n_cr.sem, n_cr.at(k, n))
                    if n >= 2:
                        act.wait_ge(n_hcs.sem, n_hcs.at(k, 2 * n - 3))
                    n_csc.by(act.activation(n_cs[:, n % 2, :], bank[:, n % 2, :], ACT.Copy))
                    if n in ACT_STAGES:
                        prologue(j, u + 1, ACT_STAGES[n])
                act.wait_ge(n_o.sem, n_o.at(k, 0))
                act.wait_ge(n_hcs.sem, n_hcs.at(k, 2 * NSTATE - 1))
                n_oc.by(act.activation(n_yT, bank[:, 6, :], ACT.Copy))

            with act.Fori(0, PAIRS) as j:
                steps[0] = 0
                for stage in ACT_STAGES.values():
                    prologue(j, 0, stage)
                for u, (kind, p) in enumerate(UNITS):
                    {"ffn": ffn, "moe": moe, "mha": mha, "mamba": mamba}[kind](j, u, kth[u])
                    unit_end(act, j, u)

        @block.vector
        def _(dve):
            V = nc.vector
            dve.wait_ge(loaded, 16 * NLOAD)
            for n, (dst, src) in enumerate(((fw1, stage_w[0]), (fw2, stage_w[1]), (aw, stage_w[2]), (win, stage_w[3]),
                                            (rw, stage_w[4]), (mw, stage_w[5]))):
                dve.wait_ge(split_done, n + 1)
                V.tensor_tensor(dst[1][:], src[:], dst[0][:].bitcast(F32), ALU.subtract).then_inc(dve_set, 1)
            dve.wait_ge(loaded, 16 * (NLOAD + 1))
            count = [6]

            def set_step(ins):
                count[0] += 1
                ins.then_inc(dve_set, 1)
                dve.wait_ge(dve_set, count[0])

            V.tensor_copy(biasw[32:64, :], stage_b[32:64, :])
            set_step(V.tensor_copy(biasw[64:128, :], stage_b[64:128, :]))
            set_step(V.tensor_tensor(rest_b[64:128, :], stage_b[64:128, :], biasw[64:128, :], ALU.subtract))
            set_step(V.tensor_copy(biasw[64:128, :], rest_b[64:128, :]))
            set_step(V.tensor_tensor(rest_b[96:128, :], rest_b[96:128, :], biasw[96:128, :], ALU.subtract))
            set_step(V.tensor_copy(biasw[96:128, :], rest_b[96:128, :]))
            V.memset(ve, 1.0).then_inc(setup_done, 1)
            dve.wait_ge(setup_done, 3)

            steps = [0]

            def step(j, ins):
                steps[0] += 1
                ins.then_inc(dve_step, 1)
                dve.wait_ge(dve_step, steps[0])

            def newton(j):
                step(j, V.tensor_tensor(y2, y0, y0, ALU.mult))
                step(j, V.tensor_tensor(y2, y2, ve, ALU.mult))
                step(j, V.tensor_scalar(y2, y2, -0.5, 1.5, ALU.mult, ALU.add))
                step(j, V.tensor_tensor(rstd, y2, y0, ALU.mult))

            def stats(j, src):
                for t in range(NT):
                    step(j, V.bn_stats(st[:, t, :], src[:, t, :]))

            def prologue(j, u, stage):
                if u == NU:
                    return
                kind, p = UNITS[u]
                k = kth[u]
                if stage == "stats":
                    if u < 2:
                        dve.wait_ge(x_in, 32)
                    stats(j, X[:, p])
                    for t in range(NT):
                        ins = V.bn_aggr(mv[:, t, :], st[:, t, :])
                        if t < NT - 1:
                            step(j, ins)
                    g_var.by(ins)
                if stage == "rows":
                    dve.wait_ge(g_var.sem, g_var.at(u, 0))
                    step(j, V.tensor_scalar(ve, mv[:, :, 1], EPS, None, ALU.add))
                    dve.wait_ge(g_rsq.sem, g_rsq.at(u, 0))
                    newton(j)
                    for t in range(NT):
                        ins = V.tensor_scalar(xn[:, p, t, :], X[:, p, t, :], mv[:, t, 0:1], rstd[:, t:t + 1],
                                              ALU.subtract, ALU.mult)
                        if t < NT - 1 or kind == "mamba":
                            step(j, ins)
                    if kind == "mamba":
                        stats(j, xn[:, p])
                        for t in range(NT):
                            step(j, V.bn_aggr(mv[:, t, :], st[:, t, :]))
                        step(j, V.tensor_tensor(y2, mv[:, :, 0], mv[:, :, 0], ALU.mult))
                        step(j, V.tensor_tensor(y2, y2, mv[:, :, 1], ALU.add))
                        r_var.by(V.tensor_scalar(ve, y2, EPS, None, ALU.add))
                    else:
                        g_xn.by(ins)
                if stage == "rms" and kind == "mamba":
                    dve.wait_ge(r_rsq.sem, r_rsq.at(k, 0))
                    dve.wait_ge(r_var.sem, r_var.at(k, 0))
                    newton(j)
                    for t in range(NT):
                        ins = V.tensor_scalar(xm[p][:, t, :], xn[:, p, t, :], rstd[:, t:t + 1], None, ALU.mult)
                        if t < NT - 1:
                            step(j, ins)
                    g_xn.by(ins)
                if stage == "low":
                    dve.wait_ge(g_xh.sem, g_xh.at(u, 0))
                    g_xl.by(V.scalar_tensor_tensor(xT[1][:, p, :], bank[:, 7, :], norm_w if kind == "mamba" else 1.0,
                                                   xT[0][:, p, :].bitcast(F32), ALU.mult, ALU.subtract))
                if kind == "ffn":
                    if stage == "first":
                        dve.wait_ge(t_sc.sem, t_sc.at(k, 0))
                        t_bit.by(V.tensor_scalar(dbit[:], bank[0:96, 7, :], node_b[0:96], 0.0, ALU.add, ALU.is_ge))
                    if stage in ("second", "third", "fourth"):
                        t = ("second", "third", "fourth").index(stage)
                        dve.wait_ge(t_cnt.sem, t_cnt.at(k, t))
                        t_sel.by(V.tensor_scalar(R[:, p, t, :], bank[:, 7, :], leaf_thr, None, ALU.is_ge))
                if kind == "moe":
                    if stage == "first":
                        dve.wait_ge(e_log.sem, e_log.at(k, 0))
                        raw = bank[:, 7, 0:NT * EXPERTS].rearrange("p (t e) -> p t e", t=NT)
                        step(j, V.tensor_reduce(gmax, raw, AX_X, ALU.max))
                        e_sub.by(V.tensor_tensor(glog, raw, per_token(gmax), ALU.subtract))
                    if stage == "second":
                        dve.wait_ge(e_exp.sem, e_exp.at(k, 0))
                        route(j, cmp[p])
                    if stage == "third":
                        dve.wait_ge(e_tr.sem, e_tr.at(k, 0))
                        e_row.by(V.tensor_copy(R[0:96, p, 0, :], bank[0:96, 7, 0:T // 2].bitcast(BF16)))

            def per_token(v):
                return v.unsqueeze(2).to_broadcast([P, NT, EXPERTS])

            def route(j, cmp):
                step(j, V.tensor_reduce(gsum, gexp, AX_X, ALU.add))
                step(j, V.reciprocal(grec, gsum))
                step(j, V.tensor_tensor(gsc, gexp, per_token(grec), ALU.mult))
                step(j, V.tensor_tensor(gbi, gsc, gate_b[:].unsqueeze(1).to_broadcast([P, NT, EXPERTS]), ALU.add))
                full = [P, NT, EXPERTS, EXPERTS]
                other = gbi.unsqueeze(2).to_broadcast(full)
                own = gbi.unsqueeze(3).to_broadcast(full)
                step(j, V.tensor_tensor(cmp[:, 0], other, own, ALU.is_gt))
                step(j, V.tensor_tensor(cmp[:, 1], other, own, ALU.is_equal))
                step(j, V.tensor_tensor(cmp[:, 1], cmp[:, 1], tri[:].unsqueeze(1).to_broadcast(full), ALU.mult))
                step(j, V.tensor_tensor(cmp[:, 0], cmp[:, 0], cmp[:, 1], ALU.add))
                step(j, V.tensor_reduce(grank, cmp[:, 0], AX_X, ALU.add))
                step(j, V.scalar_tensor_tensor(gcmb, grank, 1.5, gsc, ALU.is_lt, ALU.mult))
                step(j, V.tensor_copy(cparts[:, :, 0:8], gcmb))
                step(j, V.tensor_tensor(gr1, gcmb, cparts[:, :, 0:8], ALU.subtract))
                step(j, V.tensor_copy(cparts[:, :, 32:40], gr1))
                step(j, V.tensor_tensor(gr2, gr1, cparts[:, :, 32:40], ALU.subtract))
                e_prt.by(V.tensor_copy(cparts[:, :, 64:72], gr2))

            def add_rows(j, p, src, scale=1.0):
                V.scalar_tensor_tensor(flat(X[:, p]), src, scale, flat(X[:, p]), ALU.mult, ALU.add)

            def ffn(j, u, k, p):
                for i in range(STEPS):
                    dve.wait_ge(f_hi.sem, f_hi.at(k, i))
                    f_lo.by(V.scalar_tensor_tensor(f_h[1][:, i % 4, :], bank[:, i % 3, :], 0.0,
                                                   f_h[0][:, i % 4, :].bitcast(F32), ALU.max, ALU.subtract))
                    if i in DVE_STAGES:
                        prologue(j, u + 1, DVE_STAGES[i])
                    if i in (11, 19):
                        t = (11, 19).index(i)
                        dve.wait_ge(f_evh.sem, f_evh.at(k, t))
                        f_evl.by(V.tensor_tensor((f_q, f_k)[t][1][:], bank[:, 3 + t, :], (f_q, f_k)[t][0][:].bitcast(F32),
                                                 ALU.subtract))
                    if i in (20, 22):
                        score_max(j, k, (i - 20) // 2)
                dve.wait_ge(f_vtr.sem, f_vtr.at(k, 0))
                f_vok.by(V.tensor_copy(f_v[:], bank[:, 3, :].rearrange("p (t d) -> p t d", t=NT)))
                score_max(j, k, 2)
                score_max(j, k, 3)
                dve.wait_ge(f_prob.sem, f_prob.at(k, 3))
                step(j, V.reciprocal(f_s[:, 3, :], f_s[:, 2, :]))
                step(j, V.tensor_scalar(f_s[:, 4, :], f_s[:, 3, :], 0.5, None, ALU.mult))
                dve.wait_ge(f_pv.sem, f_pv.at(k, NT - 1))
                for qt in range(NT):
                    V.scalar_tensor_tensor(X[:, p, qt, :], bank[:, 4, qt * P:(qt + 1) * P], f_s[:, 4, qt:qt + 1],
                                           X[:, p, qt, :], ALU.mult, ALU.add)

            def score_max(j, k, qt):
                dve.wait_ge(f_sco.sem, f_sco.at(k, qt))
                step(j, V.tensor_reduce(f_s[:, 0, qt:qt + 1], bank[:, 5, :], AX_X, ALU.max))
                f_max.by(V.tensor_scalar(f_s[:, 1, qt:qt + 1], f_s[:, 0, qt:qt + 1], -LEAF_SCALE, None, ALU.mult))

            def moe(j, u, k, p):
                for i in range(MSTEPS):
                    e = i // 2
                    dve.wait_ge(m_b.sem, m_b.at(k, i))
                    dve.wait_ge(m_silu.sem, m_silu.at(k, i))
                    if i >= 3:
                        dve.wait_ge(m_lo.sem, m_lo.at(k, i - 3))
                    if e < EXPERTS:
                        m_ts.by(V.tensor_tensor(m_t[:, i % 2, :], m_sl[:, i % 2, :], bank[:, 2 + i % 2, :], ALU.mult))
                        dve.wait_ge(m_ts.sem, m_ts.at(k, i))
                        dve.wait_ge(m_cr.sem, m_cr.at(k, e))
                        m_hs.by(V.tensor_tensor(m_h[:, i % 3, :], m_t[:, i % 2, :], bank[:, 4 + e % 2, :], ALU.mult))
                    else:
                        m_hs.by(V.tensor_tensor(m_h[:, i % 3, :], m_sl[:, i % 2, :], bank[:, 2 + i % 2, :], ALU.mult))
                    if i in DVE_STAGES:
                        prologue(j, u + 1, DVE_STAGES[i])
                dve.wait_ge(m_ytr.sem, m_ytr.at(k, 0))
                add_rows(j, p, bank[:, 0, :], 0.5)

            def mha(j, u, k, p):
                dve.wait_ge(a_cst.sem, a_cst.at(k, 4))
                for side in range(2):
                    s_ = HEAD_SCALE if side == 0 else 1.0
                    for c in range(2):
                        dve.wait_ge(a_proj.sem, a_proj.at(k, 2 * side + c))
                        step(j, V.scalar_tensor_tensor(a_rot[side][c], bank[:, 2 * side + c, :], s_, rope[:, c, :],
                                                       ALU.mult, ALU.mult))
                    a_rotd.by(V.tensor_tensor(a_rot[side][0], a_rot[side][0], a_rot[side][1], ALU.add))
                dve.wait_ge(a_proj.sem, a_proj.at(k, 4))
                a_vok.by(V.tensor_copy(a_v[:, :, :, 0:DH], bank[:, 4, :].rearrange("p (t h d) -> p t h d", t=NT, d=DH)))
                for s_, (qt, h0, nh) in enumerate(SLOT1):
                    dve.wait_ge(a_s1.sem, a_s1.at(k, s_))
                    w = (qt + 1) * P
                    b = 2 * (s_ % 2)
                    if qt < 2:
                        src = bank[:, b:b + 2, :].rearrange("p b (h w) -> p (b h) w", w=w)
                    else:
                        src = bank[:, b:b + 2, 0:w]
                    a_m1.by(V.tensor_reduce(a_mx[:, qt, h0:h0 + nh], src, AX_X, ALU.max, negate=True))
                    if s_ in DVE_STAGES:
                        prologue(j, u + 1, DVE_STAGES[s_])
                dve.wait_ge(a_m1.sem, a_m1.at(k, len(SLOT1) - 1))
                step(j, V.tensor_copy(a_mp[:, :, 0, :], a_mx[:]))
                step(j, V.tensor_tensor(a_mr[:], a_mx[:], a_mp[:, :, 0, :], ALU.subtract))
                step(j, V.tensor_copy(a_mp[:, :, 1, :], a_mr[:]))
                step(j, V.tensor_tensor(a_mx[:], a_mr[:], a_mp[:, :, 1, :], ALU.subtract))
                a_mpt.by(V.tensor_copy(a_mp[:, :, 2, :], a_mx[:]))
                for g in range(4):
                    dve.wait_ge(a_rep.sem, a_rep.at(k, g))
                    step(j, V.reciprocal(a_rec, bank[:, 4, :]))
                    if g >= 1:
                        dve.wait_ge(a_out.sem, a_out.at(k, g - 1))
                    a_norm.by(V.tensor_tensor(a_on, a_o[:], a_rec, ALU.mult))
                dve.wait_ge(a_ytr.sem, a_ytr.at(k, 0))
                add_rows(j, p, bank[:, 4, :])

            def mamba(j, u, k, p):
                V.tensor_tensor(X[:, p], X[:, p], xn[:, p], ALU.add)
                dve.wait_ge(n_fill.sem, n_fill.at(k, 0))
                for m in range(2):
                    dve.wait_ge(n_xps.sem, n_xps.at(k, m))
                    step(j, V.tensor_scalar(n_cv[:, m, :], n_xp[:, m, 0:T], conv_w[:, m, 0:1], conv_b[:, m:m + 1],
                                            ALU.mult, ALU.add))
                    for c in range(1, 4):
                        ins = V.scalar_tensor_tensor(n_cv[:, m, :], n_xp[:, m, c:c + T], conv_w[:, m, c:c + 1],
                                                     n_cv[:, m, :], ALU.mult, ALU.add)
                        if c < 3:
                            step(j, ins)
                    n_cvs.by(ins)
                dve.wait_ge(n_bc1.sem, n_bc1.at(k, 0))
                step(j, V.tensor_tensor(n_r[:], bank[0:96, 5, :], n_bc[:], ALU.subtract))
                V.tensor_copy(n_bc[32:64], n_r[32:64])
                step(j, V.tensor_copy(n_bc[64:96], n_r[64:96]))
                step(j, V.tensor_tensor(n_r[64:96], n_r[64:96], n_bc[64:96], ALU.subtract))
                n_bcp.by(V.tensor_copy(n_bc[64:96], n_r[64:96]))
                for m in range(2):
                    dve.wait_ge(n_abss.sem, n_abss.at(k, m))
                    ins = V.tensor_scalar(n_pos[:, m, :], bank[:, m, :], b_dt[:, m:m + 1], 0.0, ALU.add, ALU.max)
                n_poss.by(ins)
                dve.wait_ge(n_us.sem, n_us.at(k, 0))
                dve.wait_ge(n_sil.sem, n_sil.at(k, 3))
                step(j, V.tensor_scalar(n_cor[:], n_u[:], 1.0, -1.0, ALU.add, ALU.add))
                step(j, V.tensor_tensor(n_cor[:], n_u[:], n_cor[:], ALU.subtract))
                dve.wait_ge(n_lns.sem, n_lns.at(k, 0))
                step(j, V.tensor_tensor(n_cor[:], n_cor[:], n_ln[:], ALU.add))
                dve.wait_ge(n_lows.sem, n_lows.at(k, 0))
                step(j, V.tensor_tensor(n_cor[:], n_cor[:], n_low[:], ALU.max))
                step(j, V.tensor_tensor(n_cor[:], n_cor[:], n_u[:], ALU.min))
                dve.wait_ge(n_poss.sem, n_poss.at(k, 0))
                n_dts.by(V.tensor_tensor(n_dt[:], n_cor[:], n_pos[:], ALU.add))
                dve.wait_ge(n_dts.sem, n_dts.at(k, 0))
                dve.wait_ge(n_sil.sem, n_sil.at(k, 3))
                n_dtxs.by(V.tensor_tensor(n_dtx[:], n_dt[:], n_xc[:], ALU.mult))
                dve.wait_ge(n_dtxs.sem, n_dtxs.at(k, 0))
                for n in range(NSTATE):
                    dve.wait_ge(n_br.sem, n_br.at(k, n))
                    for m in range(NHALF):
                        i = 2 * n + m
                        if n >= 1:
                            dve.wait_ge(n_scan.sem, n_scan.at(k, i - 2))
                        n_dbs.by(V.tensor_tensor(n_db[:, m, :], n_dtx[:, m, :], bank[:, 4 + n % 2, :], ALU.mult))
                    for m in range(NHALF):
                        i = 2 * n + m
                        dve.wait_ge(n_dbs.sem, n_dbs.at(k, i))
                        dve.wait_ge(n_das.sem, n_das.at(k, i))
                        if n >= 1:
                            dve.wait_ge(n_hcs.sem, n_hcs.at(k, i - 2))
                        n_scan.by(V.tensor_tensor_scan(n_h[:, m, :], n_da[:, m, :], n_db[:, m, :], 0.0,
                                                       ALU.mult, ALU.add))
                    if n in DVE_STAGES:
                        prologue(j, u + 1, DVE_STAGES[n])
                dve.wait_ge(n_ya.sem, n_ya.at(k, 2 * NSTATE - 1))
                dve.wait_ge(n_scan.sem, n_scan.at(k, 2 * NSTATE - 1))
                for m in range(2):
                    step(j, V.scalar_tensor_tensor(n_db[:, m, :], n_xc[:, m, :], d_skip[:, m:m + 1], bank[:, 2 + m, :],
                                                   ALU.mult, ALU.add))
                n_y.by(V.tensor_tensor(n_db[:], n_db[:], n_sz[:], ALU.mult))
                dve.wait_ge(n_otr.sem, n_otr.at(k, 0))
                add_rows(j, p, bank[:, 4, :])

            with dve.Fori(0, PAIRS) as j:
                steps[0] = 0
                for stage in DVE_STAGES.values():
                    prologue(j, 0, stage)
                for u, (kind, p) in enumerate(UNITS):
                    {"ffn": ffn, "moe": moe, "mha": mha, "mamba": mamba}[kind](j, u, kth[u], p)
                    unit_end(dve, j, u)

        @block.tensor
        def _(pe):
            mm = nc.tensor.matmul
            pe.wait_ge(setup_done, 3)

            def product(dst, w, x, start=True, stop=True):
                mm(dst, w[0], x[0], start=start, stop=False)
                mm(dst, w[0], x[1], start=False, stop=False)
                return mm(dst, w[1], x[0], start=False, stop=stop)

            def xs(p):
                return [xT[0][:, p, :], xT[1][:, p, :]]

            def rows(dst, src, idn):
                for t in range(NT):
                    ins = nc.tensor.transpose(dst(t), src(t), idn)
                return ins

            def back(b, src):
                return rows(lambda t: bank[:, b, t * P:(t + 1) * P], lambda t: src[:, t * P:(t + 1) * P], ident[:])

            def prologue(j, u, stage):
                if u == NU:
                    return
                kind, p = UNITS[u]
                k = kth[u]
                if stage == "turn":
                    pe.wait_ge(g_xn.sem, g_xn.at(u, 0))
                    src = xm[p] if kind == "mamba" else xn[:, p]
                    g_tr.by(rows(lambda t: bank[:, 7, t * P:(t + 1) * P], lambda t: src[:, t, :], ident[:]))
                if kind == "ffn":
                    if stage == "first":
                        pe.wait_ge(g_xl.sem, g_xl.at(u, 0))
                        t_sc.by(product(bank[0:96, 7, :], [rw[0][:, 0:96], rw[1][:, 0:96]], xs(p)))
                    if stage == "second":
                        pe.wait_ge(t_bit.sem, t_bit.at(k, 0))
                        t_cnt.by(mm(bank[:, 7, :], tree[:, 0, :], dbit[:], start=True, stop=True))
                    if stage in ("third", "fourth"):
                        t = ("third", "fourth").index(stage) + 1
                        pe.wait_ge(t_sel.sem, t_sel.at(k, t - 1))
                        t_cnt.by(mm(bank[:, 7, :], tree[:, t, :], dbit[:], start=True, stop=True))
                if kind == "moe":
                    if stage == "first":
                        pe.wait_ge(g_xl.sem, g_xl.at(u, 0))
                        for t in range(NT):
                            x = [xT[c][:, p, t * P:(t + 1) * P] for c in range(2)]
                            ins = product(bank[:, 7, t * EXPERTS:(t + 1) * EXPERTS], x,
                                          [rw[0][:, 96:104], rw[1][:, 96:104]])
                        e_log.by(ins)
                    if stage == "third":
                        pe.wait_ge(e_prt.sem, e_prt.at(k, 0))
                        tr = bank[0:96, 7, 0:T // 2].bitcast(BF16)
                        e_tr.by(rows(lambda t: tr[:, t * P:(t + 1) * P], lambda t: cparts[:, t, :], identb))

            def ready(j, u):
                kind, p = UNITS[u]
                pe.wait_ge(g_xl.sem, g_xl.at(u, 0))

            def ffn(j, u, k, p):
                x = xs(p)
                ready(j, u)
                pe.wait_ge(t_sel.sem, t_sel.at(k, TREES - 1))
                for i in range(STEPS + 2):
                    if i < STEPS:
                        t, m = divmod(i, M1)
                        b = bank[:, i % 3, :]
                        if i >= 3:
                            pe.wait_ge(f_lo.sem, f_lo.at(k, i - 3))
                        product(b, [fw1[c][:, t, m * P:(m + 1) * P] for c in range(2)], x, stop=False)
                        f_s1.by(mm(b, b1w[:, t, m * P:(m + 1) * P], R[:, p, t, :], start=False, stop=True))
                    if i >= 2:
                        i2 = i - 2
                        t, m = divmod(i2, M1)
                        acc = bank[:, 3 + t % 2, :]
                        pe.wait_ge(f_lo.sem, f_lo.at(k, i2))
                        if i2 == 2 * M1:
                            pe.wait_ge(f_evl.sem, f_evl.at(k, 0))
                        if m == 0:
                            mm(acc, b2w[:, t, :], R[:, p, t, :], start=True, stop=False)
                        f_s2.by(product(acc, [fw2[c][:, t, m, :] for c in range(2)],
                                        [f_h[c][:, i2 % 4, :] for c in range(2)], start=False, stop=m == M1 - 1))
                    if i in PE_STAGES:
                        prologue(j, u + 1, PE_STAGES[i])
                    if i in (21, 23):
                        score(j, k, (i - 21) // 2)
                    if i == 24:
                        turn(j, k, 0)
                pe.wait_ge(f_evh.sem, f_evh.at(k, 2))
                f_vtr.by(back(3, f_vT))
                score(j, k, 2)
                turn(j, k, 1)
                turn(j, k, 2)
                score(j, k, 3)
                pe.wait_ge(f_vok.sem, f_vok.at(k, 0))
                weigh(j, k, 0)
                weigh(j, k, 1)
                weigh(j, k, 2)
                turn(j, k, 3)
                weigh(j, k, 3)

            def score(j, k, qt):
                if qt == 0:
                    pe.wait_ge(f_evl.sem, f_evl.at(k, 1))
                else:
                    pe.wait_ge(f_prob.sem, f_prob.at(k, qt - 1))
                f_sco.by(product(bank[:, 5, :], [f_q[c][:, qt * P:(qt + 1) * P] for c in range(2)],
                                 [f_k[c][:] for c in range(2)]))

            def turn(j, k, qt):
                pe.wait_ge(f_prob.sem, f_prob.at(k, qt))
                if qt:
                    pe.wait_ge(f_pok.sem, f_pok.at(k, qt - 1))
                f_ptr.by(rows(lambda t: bank[:, 6, t * P:(t + 1) * P],
                              lambda t: f_p[:, qt % 2, t * P:(t + 1) * P], ident[:]))

            def weigh(j, k, qt):
                pe.wait_ge(f_pok.sem, f_pok.at(k, qt))
                for kt in range(NT):
                    ins = mm(bank[:, 4, qt * P:(qt + 1) * P], f_pT[:, kt, qt * P:(qt + 1) * P], f_v[:, kt, :],
                             start=kt == 0, stop=kt == NT - 1)
                f_pv.by(ins)

            def moe(j, u, k, p):
                x = xs(p)
                ready(j, u)
                pe.wait_ge(e_row.sem, e_row.at(k, 0))
                for i in range(MSTEPS + 3):
                    if i < MSTEPS:
                        e, m = divmod(i, 2)
                        if i >= 2:
                            pe.wait_ge(m_ts.sem, m_ts.at(k, i - 2))
                        m_a.by(product(bank[:, i % 2, :], [mw[c][:, e, m, :] for c in range(2)], x))
                        m_b.by(product(bank[:, 2 + i % 2, :], [mw[c][:, e, 2 + m, :] for c in range(2)], x))
                        if m == 0 and e < EXPERTS:
                            if e >= 2:
                                pe.wait_ge(m_hs.sem, m_hs.at(k, i - 3))
                            m_cr.by(mm(bank[:, 4 + e % 2, :], pick[:, e:e + 1].to_broadcast([96, P]), R[0:96, p, 0, :],
                                       start=True, stop=True))
                    if i >= 3:
                        i2 = i - 3
                        e, m = divmod(i2, 2)
                        pe.wait_ge(m_lo.sem, m_lo.at(k, i2))
                        m_s2.by(product(bank[:, 6, :], [mw[c][:, e, 4 + m, :] for c in range(2)],
                                        [m_hh[c][:, i2 % 3, :] for c in range(2)], start=i2 == 0, stop=i2 == MSTEPS - 1))
                    if i in PE_STAGES:
                        prologue(j, u + 1, PE_STAGES[i])
                pe.wait_ge(m_y.sem, m_y.at(k, 0))
                pe.wait_ge(m_ts.sem, m_ts.at(k, 2 * EXPERTS - 1))
                pe.wait_ge(m_hs.sem, m_hs.at(k, MSTEPS - 1))
                m_ytr.by(back(0, m_yT))

            def mha(j, u, k, p):
                x = xs(p)
                ready(j, u)
                for n in range(4):
                    a_proj.by(product(bank[:, n, :], [aw[c][:, n, :] for c in range(2)], x))
                for t in range(NT):
                    ins = product(bank[:, 4, t * P:(t + 1) * P], [xT[c][:, p, t * P:(t + 1) * P] for c in range(2)],
                                  [aw[c][:, 4, :] for c in range(2)])
                a_proj.by(ins)
                pe.wait_ge(a_ld.sem, a_ld.at(k, 4 * SLOTS - 1))
                pe.wait_ge(a_cst.sem, a_cst.at(k, 4))
                pe.wait_ge(a_fill.sem, a_fill.at(k, 2))
                pe.wait_ge(a_rotd.sem, a_rotd.at(k, 1))
                for s_, (qt, h0, nh) in enumerate(SLOT1):
                    if s_ >= 2:
                        pe.wait_ge(a_m1.sem, a_m1.at(k, s_ - 2))
                    w = (qt + 1) * P
                    for n in range(nh):
                        h = h0 + n
                        if qt < 2:
                            per = T // w
                            b, c0 = 2 * (s_ % 2) + n // per, n % per * w
                        else:
                            b, c0 = 2 * (s_ % 2) + n, 0
                        mm(bank[:, b, c0:c0 + w], a_q[:, h // 2, qt * P:(qt + 1) * P], a_k[:, h, 0:w],
                           start=True, stop=False)
                        ins = mm(bank[:, b, c0 + qt * P:c0 + w], identb, mask_qk, start=False, stop=True)
                    a_s1.by(ins)
                    if s_ in PE_STAGES:
                        prologue(j, u + 1, PE_STAGES[s_])
                pe.wait_ge(a_mpt.sem, a_mpt.at(k, 0))
                pe.wait_ge(a_vok.sem, a_vok.at(k, 0))
                tr = bank[0:48, 4, 0:T // 2].bitcast(BF16)
                a_mtr.by(rows(lambda t: tr[:, t * P:(t + 1) * P], lambda t: flat(a_mp[:, t]), identb))
                pe.wait_ge(a_m1.sem, a_m1.at(k, len(SLOT1) - 1))
                pe.wait_ge(a_mld.sem, a_mld.at(k, 1))
                for s_ in range(NS2 + 3):
                    if s_ < NS2:
                        g, kt, half = s_ // (2 * NT), s_ // 2 % NT, s_ % 2
                        w = T - kt * P
                        if s_ >= 2:
                            pe.wait_ge(a_e2.sem, a_e2.at(k, s_ - 2))
                        for n in range(2):
                            h = 4 * g + 2 * half + n
                            b = 2 * (s_ % 2) + n
                            mm(bank[:, b, 0:w], a_k[:, h, kt * P:(kt + 1) * P], a_q[:, h // 2, kt * P:T],
                               start=True, stop=False)
                            ins = mm(bank[:, b, 0:P], identb, mask_kq, start=False, stop=True)
                        a_s2.by(ins)
                    if s_ >= 3 and s_ % 2 == 1:
                        q_ = (s_ - 3) // 2
                        g, kt = divmod(q_, NT)
                        pe.wait_ge(a_e2.sem, a_e2.at(k, 2 * q_ + 1))
                        if kt == 0 and g >= 1:
                            pe.wait_ge(a_osb.sem, a_osb.at(k, g - 1))
                        for c in range(4):
                            ring = (2 * q_ + c // 2) % 4
                            ins = mm(bank[32 * c:32 * c + 32, 6, kt * P:T], a_v[:, kt, 4 * g + c, :],
                                     a_p[:, ring, c % 2, 0:T - kt * P], start=kt == 0, stop=kt == NT - 1)
                        a_pv.by(ins)
                        if kt == 2 and g >= 1:
                            head_rows(j, k, g - 1)
                head_rows(j, k, 3)
                pe.wait_ge(a_y.sem, a_y.at(k, 0))
                a_ytr.by(back(4, a_yT))

            def head_rows(j, k, g):
                pe.wait_ge(a_osb.sem, a_osb.at(k, g))
                if g == 0:
                    pe.wait_ge(a_mok.sem, a_mok.at(k, 0))
                else:
                    pe.wait_ge(a_norm.sem, a_norm.at(k, g - 1))
                a_rep.by(mm(bank[:, 4, :], spread[:], a_o[:], start=True, stop=True))
                pe.wait_ge(a_norm.sem, a_norm.at(k, g))
                a_out.by(mm(bank[:, 5, :], owT[:, g, :], a_on, start=g == 0, stop=g == 3))

            def mamba(j, u, k, p):
                x = xs(p)
                ready(j, u)
                for n in range(4):
                    n_in.by(product(bank[:, n, :], [win[c][:, n, :] for c in range(2)], x))
                pe.wait_ge(n_sil.sem, n_sil.at(k, 3))
                for n, (b, c0, c1) in enumerate(((4, 0, 64), (5, 64, 160))):
                    for m in range(2):
                        ins = mm(bank[0:c1 - c0, b, :], wx[:, m, c0:c1], n_xc[:, m, :], start=m == 0, stop=m == 1)
                    n_xdb.by(ins)
                pe.wait_ge(n_dtc.sem, n_dtc.at(k, 0))
                for m in range(2):
                    n_dtp.by(mm(bank[:, m, :], wdt[:, m, :], n_dtr[:], start=True, stop=True))
                pe.wait_ge(n_bcp.sem, n_bcp.at(k, 0))
                pe.wait_ge(n_poss.sem, n_poss.at(k, 0))
                pe.wait_ge(n_abss.sem, n_abss.at(k, 1))
                for n in range(NSTATE + 2):
                    if n < NSTATE:
                        if n >= 2:
                            pe.wait_ge(n_dbs.sem, n_dbs.at(k, 2 * n - 3))
                        n_br.by(mm(bank[:, 4 + n % 2, :], pick[:, n:n + 1].to_broadcast([96, P]), n_bc[:],
                                   start=True, stop=True))
                        if n >= 2:
                            pe.wait_ge(n_csc.sem, n_csc.at(k, n - 2))
                        n_cr.by(mm(bank[:, n % 2, :], pick[:, 16 + n:17 + n].to_broadcast([96, P]), n_bc[:],
                                   start=True, stop=True))
                    if n >= 2:
                        for m in range(2):
                            pe.wait_ge(n_hcs.sem, n_hcs.at(k, 2 * n - 4 + m))
                            n_ya.by(mm(bank[:, 2 + m, :], ident[:], n_hc[:, m, :], start=n == 2, stop=n == NSTATE + 1))
                    if n in PE_STAGES:
                        prologue(j, u + 1, PE_STAGES[n])
                pe.wait_ge(n_y.sem, n_y.at(k, 0))
                for m in range(2):
                    ins = mm(bank[:, 6, :], wout[:, m, :], n_db[:, m, :], start=m == 0, stop=m == 1)
                n_o.by(ins)
                pe.wait_ge(n_oc.sem, n_oc.at(k, 0))
                n_otr.by(back(4, n_yT))

            with pe.Fori(0, PAIRS) as j:
                for stage in PE_STAGES.values():
                    prologue(j, 0, stage)
                for u, (kind, p) in enumerate(UNITS):
                    {"ffn": ffn, "moe": moe, "mha": mha, "mamba": mamba}[kind](j, u, kth[u], p)
                    unit_end(pe, j, u)

        for signal in signals:
            signal.whole()


def constants():
    f, half = np.float32, P // 2
    pos = np.arange(T, dtype=f)
    freqs = (f(1.0) / f(10000.0) ** (np.arange(half, dtype=f) / f(half))).astype(f)
    angle = pos[:, None] * freqs[None, :]
    sin, cos = np.sin(angle).astype(f).T, np.cos(angle).astype(f).T
    rope = np.stack([np.concatenate([cos, cos]), np.concatenate([-sin, sin])], 1)
    eye = np.eye(P, dtype=f)
    later = np.arange(P)[None, :] > np.arange(P)[:, None]
    mask_qk = np.where(later, f(-1e9), f(0))
    mask_kq = np.where(later.T, f(-1e9), f(0))
    path = np.zeros((LEAVES, LEAVES), f)
    depth = LEAVES.bit_length() - 1
    path[LEAVES - 1] = -depth
    for leaf in range(LEAVES):
        node = leaf + LEAVES - 1
        while node:
            up = (node - 1) // 2
            path[up, leaf] = 1 if node == 2 * up + 2 else -1
            path[LEAVES - 1, leaf] += node == 2 * up + 1
            node = up
    tree = np.zeros((96, TREES, P), f)
    thr = np.full(P, -0.5, f)
    thr[0:32] = 0.5
    for t in range(TREES):
        tree[32 * t:32 * t + LEAVES, t, 0:LEAVES] = -path
        for c in range(1, 4):
            tree[32 * t:32 * t + LEAVES, t, 32 * c:32 * c + LEAVES] = path
    big = np.zeros((32, TREES * (M1 * P + P)), f)
    for t in range(TREES):
        for leaf in range(LEAVES):
            big[leaf, t * M1 * P + leaf * LEAF_W:t * M1 * P + (leaf + 1) * LEAF_W] = -2.0 ** 100
    pick = np.zeros((96, 32), f)
    for c in range(3):
        pick[32 * c:32 * c + 32] = np.eye(32, dtype=f)
    spread = np.zeros((P, P), f)
    for c in range(4):
        spread[32 * c + DH, 32 * c:32 * c + 32] = 1
    tri = np.broadcast_to(np.tril(np.ones((EXPERTS, EXPERTS), f), -1), (P, EXPERTS, EXPERTS))
    bf = np.dtype("bfloat16")

    def parts(v):
        got = []
        for _ in range(3):
            got.append(v.astype(bf).astype(f))
            v = v - got[-1]
        return got
    slopes = np.array([2.0 ** (-8.0 * (i + 1) / HEADS) for i in range(HEADS)], f)
    q_rows, k_rows = np.zeros((2, 16, HEADS, T), f)
    k_rows[0:3] = 1
    even = pos - pos % 2
    for n, part in enumerate(parts(slopes)):
        for c, v in enumerate((even, pos - even)):
            q_rows[3 + 2 * n + c] = part[:, None]
            k_rows[3 + 2 * n + c] = v[None, :]
    for n, part in enumerate(parts(-slopes[:, None] * pos[None, :])):
        q_rows[9 + n] = part
        k_rows[9 + n] = 1

    def by_parity(rows):
        return rows.reshape(16, HEADS // 2, 2, T).transpose(0, 2, 1, 3).astype(bf)
    return {"rope": rope, "ident": eye, "spread": spread, "tri": tri,
            "cbf": np.stack([eye, mask_qk, mask_kq], 1).astype(bf), "tree": tree.astype(bf), "leaf_mask": big.astype(bf),
            "pick": pick.astype(bf), "q_rows": by_parity(q_rows), "k_rows": by_parity(k_rows)}, thr


def layouts(a):
    const, thr = constants()
    f = np.float32

    def zeros(*shape):
        return np.zeros(shape, f)
    d = dict(const)
    d["x"] = a["L0_attn_x"].reshape(BATCHES, NT, P, P)
    fw1, fw2, bias = zeros(P, TREES, M1 * P), zeros(P, TREES, M1, P), zeros(P, TREES * (M1 * P + P))
    rw, col = zeros(P, 96 + EXPERTS), zeros(P, 20)
    for t, n in enumerate("qkv"):
        fw1[:, t] = a[f"L0_ffn_{n}_w1"].transpose(1, 0, 2).reshape(P, -1)
        fw2[:, t] = a[f"L0_ffn_{n}_w2"].reshape(M1, P, P).transpose(1, 0, 2)
        rw[:, 32 * t:32 * t + LEAVES - 1] = a[f"L0_ffn_{n}_node_w"].T
        col[32 * t:32 * t + LEAVES - 1, 1] = a[f"L0_ffn_{n}_node_b"]
        for c in range(1, 4):
            for leaf in range(LEAVES):
                at = t * M1 * P + leaf * LEAF_W
                bias[32 * c + leaf, at:at + LEAF_W] = a[f"L0_ffn_{n}_b1"][leaf]
            at = TREES * M1 * P + t * P
            bias[32 * c:32 * c + LEAVES, at:at + P] = a[f"L0_ffn_{n}_b2"]
    rw[:, 96:] = a["L1_ffn_gate_w"].T
    mw = zeros(P, MLPS, 6, P)
    for e in range(MLPS):
        w1, w2, w3 = (a[f"L1_ffn_w{n}"][e] if e < EXPERTS else a[f"L1_ffn_sw{n}"] for n in (1, 2, 3))
        mw[:, e, 0:2] = w1.T.reshape(P, 2, P)
        mw[:, e, 2:4] = w3.T.reshape(P, 2, P)
        mw[:, e, 4:6] = w2.T.reshape(2, P, P).transpose(1, 0, 2)
    wq, wk, wv = (a[f"L0_attn_w{n}"].T for n in "qkv")
    d["aw"] = np.stack([wq, np.roll(wq, P // 2, 1), wk, np.roll(wk, P // 2, 1), wv], 1)
    ow = zeros(4, 32, 4, P)
    ow[:, 0:DH] = a["L0_attn_out_w"].T.reshape(4, 4, DH, P).transpose(1, 2, 0, 3)
    d["owT"] = ow.reshape(P, 4, P)
    d["win"] = a["L1_attn_W_in"].reshape(P, 4, P)
    wx = a["L1_attn_W_x"].reshape(NHALF, P, 96).transpose(1, 0, 2)
    d["wx"] = np.concatenate([wx[:, :, 0:64]] + [wx[:, :, 64:96]] * 3, 2)
    d["wdt"] = a["L1_attn_W_dt"].reshape(64, NHALF, P)
    d["wout"] = a["L1_attn_W_out"].reshape(NHALF, P, P).transpose(1, 0, 2)
    d["a_log"] = a["L1_attn_A_log"].reshape(NHALF, P, NSTATE).transpose(1, 0, 2)
    col[:, 0], col[:, 2], col[:, 3], col[:, 4] = thr, a["L1_attn_norm_w"], EPS, a["L0_attn_out_b"]
    col[:, 5:13] = a["L1_attn_conv_w"].reshape(NHALF, P, 4).transpose(1, 0, 2).reshape(P, 8)
    for at, name in ((13, "conv_b"), (15, "b_dt"), (17, "D")):
        col[:, at:at + 2] = a[f"L1_attn_{name}"].reshape(NHALF, P).T
    d["gate_b"] = np.broadcast_to(a["L1_ffn_gate_bias"], (P, EXPERTS))
    d.update(fw1=fw1, fw2=fw2, bias=bias, rw=rw, col=col, mw=mw)
    return d


def kernel(**inputs):
    import numpy as _np
    import concourse.bacc as _bacc
    from concourse import mybir as _mybir
    from concourse.bass_utils import run_bass_kernel_spmd as _run

    nc = _bacc.Bacc("TRN2", target_bir_lowering=False, num_devices=1)
    arrays, args = {}, {}
    for name, a in layouts({n: _np.asarray(v) for n, v in inputs.items()}).items():
        a = _np.ascontiguousarray(a)
        arrays[f"in_{name}_dram"] = a
        args[name] = nc.dram_tensor(f"in_{name}_dram", a.shape, _mybir.dt.from_np(a.dtype), kind="ExternalInput").ap()
    out = nc.dram_tensor("out_dram", (BATCHES, NT, P, P), F32, kind="ExternalOutput").ap()
    program(nc, args, out)
    r = _run(nc, [arrays], core_ids=[0])
    return r.results[0]["out_dram"].reshape(BATCHES, T, P)
```

```python
from contextlib import ExitStack

import numpy as np
import concourse.bass as bass
from concourse import mybir

F32 = mybir.dt.float32
F32R = mybir.dt.float32r
BF16 = mybir.dt.bfloat16
ALU = mybir.AluOpType
ACT = mybir.ActivationFunctionType
AX_X = mybir.AxisListType.X

P = 128
T = 512
NT = T // P
BATCHES = 4
PAIRS = BATCHES // 2
LEAVES, LEAF_W, TREES = 16, 64, 3
M1 = LEAVES * LEAF_W // P
STEPS = TREES * M1
EXPERTS, MLPS = 8, 9
MSTEPS = MLPS * 2
HEADS, DH, SLOTS = 16, 8, 6
NSTATE, NHALF = 16, 2
EPS = 1e-5
LEAF_SCALE = float(np.float32(1.0) / np.sqrt(P).astype(np.float32))
HEAD_SCALE = float(1.0 / np.sqrt(np.float32(DH)))

LAYERS = ["ffn", "mha", "ffn", "moe", "mamba", "moe"]
UNITS = [(kind, batch) for kind in LAYERS for batch in range(2)]
COUNT = {kind: sum(1 for u in UNITS if u[0] == kind) for kind in LAYERS}
COUNT["unit"] = len(UNITS)
PART_RUNS = [(0, 3, 0), (3, 2, 1), (5, 1, 2)]
EARLY, MAX2 = 7, 9
DVE_STAGES = {1: "stats", 3: "rows", 5: "rms", 8: "low", 10: "first", 12: "second", 13: "scores", 14: "third",
              15: "combine", 16: "fourth", 17: "row"}
ACT_STAGES = {7: "high"}
POOL_STAGES = {1: "guess", 3: "rms", 10: "exp", 11: "exp2"}
PE_STAGES = {6: "turn", 9: "first", 11: "second", 13: "third", 15: "fourth", 16: "weights"}

MAX_ROW = SLOTS * DH


class Signal:

    def __init__(self, sem, kind, per, step=1):
        self.sem, self.kind, self.per, self.step = sem, kind, per, step
        self.made = 0

    def by(self, instruction):
        self.made += 1
        instruction.then_inc(self.sem, self.step)

    def at(self, k, i):
        assert 0 <= i < self.per and 0 <= k < COUNT[self.kind]
        return (k * self.per + i + 1) * self.step

    def whole(self):
        assert self.made == self.per * COUNT[self.kind], (self.made, self.per, self.kind)


def program(nc, A, out):
    with ExitStack() as ctx:
        def sb(name, shape, dt=F32, stack=ctx):
            return stack.enter_context(nc.sbuf_tensor(name, shape, dt))

        def sem(name):
            return ctx.enter_context(nc.semaphore(name))

        bank = ctx.enter_context(nc.psum_tensor("bank", [P, 8, T], F32))

        fw1 = [sb(f"fw1_{s}", [P, TREES, M1 * P], F32R) for s in "hl"]
        fw2 = [sb(f"fw2_{s}", [P, TREES, M1, P], F32R) for s in "hl"]
        mw = [sb(f"mw_{s}", [P, MLPS, 6, P], F32R) for s in "hl"]
        aw = [sb(f"aw_{s}", [P, 5, P], F32R) for s in "hl"]
        win = [sb(f"win_{s}", [P, 4, P], F32R) for s in "hl"]
        rw = [sb(f"rw_{s}", [P, 96 + EXPERTS], F32R) for s in "hl"]
        biasw = sb("biasw", [P, TREES * (M1 * P + P)], BF16)
        b1w = biasw[:, 0:TREES * M1 * P].rearrange("p (t n) -> p t n", t=TREES)
        b2w = biasw[:, TREES * M1 * P:].rearrange("p (t n) -> p t n", t=TREES)
        owT = sb("owT", [P, P])
        out_b = sb("out_b", [P, P])
        half = sb("half", [P, NT, EXPERTS])
        euler = sb("euler", [P, NT, EXPERTS])
        wx = sb("wx", [P, NHALF, 160])
        wdt = sb("wdt", [64, NHALF, P])
        wout = sb("wout", [P, NHALF, P])
        col = sb("col", [P, 20])
        leaf_thr, node_b, norm_w = (col[:, i:i + 1] for i in range(3))
        conv_w = col[:, 5:13].rearrange("p (m c) -> p m c", m=NHALF)
        conv_b, b_dt, d_skip = col[:, 13:15], col[:, 15:17], col[:, 17:19]
        amat = sb("amat", [P, NHALF, NSTATE])
        gate_b = sb("gate_b", [P, EXPERTS])
        tri = sb("tri", [P, EXPERTS, EXPERTS])
        ident = sb("ident", [P, P])
        cbf = sb("cbf", [P, 3, P], BF16)
        identb, mask_qk, mask_kq = cbf[:, 0, :], cbf[:, 1, :], cbf[:, 2, :]
        tree = sb("tree", [96, TREES, P], BF16)
        pick = sb("pick", [96, 32], BF16)

        X = sb("X", [P, 2, NT, P])
        xn = sb("xn", [P, 2, NT, P])
        xT = [sb(f"xT_{s}", [P, 2, T], F32R) for s in "hl"]
        R = sb("R", [P, 2, TREES, T], BF16)
        xm = [R[:, p, 0:2, :].rearrange("p a t -> p (a t)").bitcast(F32).rearrange("p (t d) -> p t d", t=NT)
              for p in range(2)]
        cmp = [R[:, p, 1:3, :].rearrange("p a t -> p (a t)").bitcast(F32)
               .rearrange("p (c t a b) -> p c t a b", c=2, t=NT, a=EXPERTS) for p in range(2)]
        dbit = sb("dbit", [96, T], BF16)
        st = sb("st", [P, NT, 6])
        mv = sb("mv", [P, NT, 2])
        small = sb("small", [P, 8, NT])
        lnv, y0, ve, y2, rstd, gmax, gsum, grec = (small[:, i, :] for i in range(8))
        gbuf = sb("gbuf", [P, 8, NT, EXPERTS])
        glog, gexp, gsc, gbi, grank, gcmb, gr1, gr2 = (gbuf[:, i] for i in range(8))
        cparts = sb("cparts", [P, NT, 96], BF16)

        s = ExitStack()
        stage_fw1 = sb("stage_fw1", [P, TREES, M1 * P], F32, s)
        stage_fw2 = sb("stage_fw2", [P, TREES, M1, P], F32, s)
        stage_b = sb("stage_b", [P, TREES * (M1 * P + P)], F32, s)
        rest_b = sb("rest_b", [P, TREES * (M1 * P + P)], F32, s)
        stage_m8 = sb("stage_m8", [P, 6 * P], F32, s)
        s.close()
        stage_ma, stage_mb = stage_fw1[:].rearrange("p t n -> p (t n)"), stage_fw2[:].rearrange("p t m d -> p (t m d)")
        spare = R[:].rearrange("p a b t -> p (a b t)").bitcast(F32)
        stage_aw, stage_win, stage_rw = spare[:, 0:640], spare[:, 640:1152], spare[:, 1152:1152 + 96 + EXPERTS]
        mwf = [mw[c][:].rearrange("p e n d -> p (e n d)") for c in range(2)]
        HALF_MW = EXPERTS * 3 * P
        splits = [("fw1_in", [fw1[c][:].rearrange("p t n -> p (t n)") for c in range(2)],
                   stage_fw1[:].rearrange("p t n -> p (t n)")),
                  ("fw2_in", [fw2[c][:].rearrange("p t m d -> p (t m d)") for c in range(2)],
                   stage_fw2[:].rearrange("p t m d -> p (t m d)")),
                  ("small_in", [aw[c][:].rearrange("p n d -> p (n d)") for c in range(2)], stage_aw),
                  ("small_in", [win[c][:].rearrange("p n d -> p (n d)") for c in range(2)], stage_win),
                  ("small_in", [rw[c][:] for c in range(2)], stage_rw),
                  ("small_in", [mwf[c][:, 2 * HALF_MW:] for c in range(2)], stage_m8[:]),
                  ("mwa_in", [mwf[c][:, 0:HALF_MW] for c in range(2)], stage_ma),
                  ("mwb_in", [mwf[c][:, HALF_MW:2 * HALF_MW] for c in range(2)], stage_mb)]

        s = ExitStack()
        f_h = [sb(f"f_h{c}", [P, 4, T], F32R, s) for c in "hl"]
        f_q = [sb(f"f_q{c}", [P, T], F32R, s) for c in "hl"]
        f_k = [sb(f"f_k{c}", [P, T], F32R, s) for c in "hl"]
        f_vT = sb("f_vT", [P, T], F32, s)
        f_v = sb("f_v", [P, NT, P], F32, s)
        f_p = sb("f_p", [P, 2, T], F32, s)
        f_pT = sb("f_pT", [P, NT, T], F32, s)
        f_s = sb("f_s", [P, 5, NT], F32, s)
        s.close()

        s = ExitStack()
        m_sl = sb("m_sl", [P, 2, T], F32, s)
        m_t = sb("m_t", [P, 2, T], F32, s)
        m_h = sb("m_h", [P, 3, T], F32, s)
        m_hh = [sb(f"m_hh{c}", [P, 3, T], F32R, s) for c in "hl"]
        m_yT = sb("m_yT", [P, T], F32, s)
        s.close()

        s = ExitStack()
        a_q = sb("a_q", [P, HEADS // 2, T], BF16, s)
        a_k = sb("a_k", [P, HEADS, T], BF16, s)
        a_v = sb("a_v", [P, NT, HEADS, 32], F32, s)
        a_p = sb("a_p", [P, 4, 2, T], F32, s)
        rope = sb("rope", [P, 2, T], F32, s)
        a_mx = sb("a_mx", [P, 2, NT, 8], F32, s)
        a_mr = sb("a_mr", [P, NT, 8], F32, s)
        a_mp = sb("a_mp", [P, 2, NT, 3, 8], BF16, s)
        a_mT = sb("a_mT", [24, 2, T], BF16, s)
        a_rec = sb("a_rec", [P, NT, 4], F32, s)
        s.close()
        a_o, a_rows = rope[:, 0, :], rope[:, 1, :].rearrange("p (t f) -> p t f", t=NT)
        a_rot = [[a_p[:, side, 0, :], a_p[:, side, 1, :]] for side in range(2)]
        a_parts = [a_p[:, 2 + side].rearrange("p a t -> p (a t)").bitcast(BF16)[:, 0:3 * T]
                   .rearrange("p (c t) -> p c t", c=3) for side in range(2)]

        s = ExitStack()
        n_xp = sb("n_xp", [P, NHALF, T + 4], F32, s)
        n_xc = sb("n_xc", [P, NHALF, T], F32, s)
        n_sz = sb("n_sz", [P, NHALF, T], F32, s)
        n_dtr = sb("n_dtr", [64, T], F32, s)
        n_dt = sb("n_dt", [P, NHALF, T], F32, s)
        n_dtx = sb("n_dtx", [P, NHALF, T], F32, s)
        n_da = sb("n_da", [P, NHALF, T], F32, s)
        n_db = sb("n_db", [P, NHALF, T], F32, s)
        n_h = sb("n_h", [P, NHALF, T], F32, s)
        n_hc = sb("n_hc", [P, NHALF, T], F32, s)
        n_cs = sb("n_cs", [P, 2, T], F32, s)
        n_bc = sb("n_bc", [96, T], BF16, s)
        n_r = sb("n_r", [96, T], F32, s)
        s.close()
        n_cv = n_cor = n_hc
        n_abs, n_u, n_ln, n_low, n_pos = n_db, n_h, n_da, n_cs, n_dtx

        parts_dram = nc.dram_tensor("parts_dram", [2, 2, 3, P // 2, T], BF16, kind="Internal").ap()
        max_dram = nc.dram_tensor("max_dram", [2, 24, T], BF16, kind="Internal").ap()

        signals = []

        def sig(name, kind, per, step=1):
            signals.append(Signal(sem(name), kind, per, step))
            return signals[-1]

        arrived = {name: sem(name) for name in ("fw1_in", "bias_in", "fw2_in", "small_in", "mwa_in", "mwb_in")}
        split_done = sem("split_done")
        setup_done = sem("setup_done")
        pair_done = sem("pair_done")
        low_done = sem("low_done")
        bias_act = sem("bias_act")
        bias_dve = sem("bias_dve")
        amat_done = sem("amat_done")
        unit_done = sem("unit_done")
        x_in = sem("x_in")
        x_out = sem("x_out")
        dve_step = sem("dve_step")

        g_var = sig("g_var", "unit", 1)
        g_rsq = sig("g_rsq", "unit", 1)
        r_var = sig("r_var", "mamba", 1)
        r_rsq = sig("r_rsq", "mamba", 1)
        g_xn = sig("g_xn", "unit", 1)
        g_tr = sig("g_tr", "unit", 1)
        g_xh = sig("g_xh", "unit", 1)
        g_xl = sig("g_xl", "unit", 1)
        t_sc = sig("t_sc", "ffn", 1)
        t_bit = sig("t_bit", "ffn", 1)
        t_cnt = sig("t_cnt", "ffn", TREES)
        t_sel = sig("t_sel", "ffn", TREES)
        e_log = sig("e_log", "moe", 1)
        e_sub = sig("e_sub", "moe", 1)
        e_exp = sig("e_exp", "moe", 2)
        e_prt = sig("e_prt", "moe", 1)
        e_tr = sig("e_tr", "moe", 1)
        e_row = sig("e_row", "moe", 1)
        f_s1 = sig("f_s1", "ffn", STEPS)
        f_hi = sig("f_hi", "ffn", STEPS)
        f_lo = sig("f_lo", "ffn", STEPS)
        f_s2 = sig("f_s2", "ffn", STEPS)
        f_evh = sig("f_evh", "ffn", TREES)
        f_evl = sig("f_evl", "ffn", 2)
        f_vtr = sig("f_vtr", "ffn", 1)
        f_vok = sig("f_vok", "ffn", 1)
        f_sco = sig("f_sco", "ffn", NT)
        f_max = sig("f_max", "ffn", NT)
        f_prob = sig("f_prob", "ffn", NT)
        f_ptr = sig("f_ptr", "ffn", NT)
        f_pok = sig("f_pok", "ffn", NT)
        f_pv = sig("f_pv", "ffn", NT)
        m_a = sig("m_a", "moe", MSTEPS)
        m_b = sig("m_b", "moe", MSTEPS)
        m_cr = sig("m_cr", "moe", EXPERTS)
        m_silu = sig("m_silu", "moe", MSTEPS)
        m_ts = sig("m_ts", "moe", 2 * EXPERTS)
        m_hs = sig("m_hs", "moe", MSTEPS)
        m_hi = sig("m_hi", "moe", MSTEPS)
        m_lo = sig("m_lo", "moe", MSTEPS)
        m_s2 = sig("m_s2", "moe", MSTEPS)
        m_y = sig("m_y", "moe", 1)
        m_ytr = sig("m_ytr", "moe", 1)
        SLOT1 = [(qt, h, n) for qt, n in ((0, 4), (1, 2), (2, 1), (3, 1)) for h in range(0, 8, n)]
        NS1, NS2 = len(SLOT1), 4 * NT * 2
        a_proj = sig("a_proj", "mha", 5)
        a_rotd = sig("a_rotd", "mha", 2)
        a_prt = sig("a_prt", "mha", 6)
        a_res = sig("a_res", "mha", 4)
        a_fill = sig("a_fill", "mha", 3)
        a_vok = sig("a_vok", "mha", 1)
        a_wr = [sig(f"a_wr_{s}", "mha", 2, 16) for s in "qk"]
        a_ld = [sig(f"a_ld_{s}", "mha", 6, 16) for s in "qk"]
        a_rld = sig("a_rld", "mha", 1, 16)
        a_cst = sig("a_cst", "mha", 4, 16)
        a_s1 = sig("a_s1", "mha", 2 * NS1)
        a_m1 = sig("a_m1", "mha", 2 * NS1)
        a_mpt = sig("a_mpt", "mha", 2)
        a_mtr = sig("a_mtr", "mha", 2)
        a_mok = sig("a_mok", "mha", 2)
        a_mwr = sig("a_mwr", "mha", 2, 16)
        a_mld = sig("a_mld", "mha", 4, 16)
        a_s2 = sig("a_s2", "mha", NS2)
        a_e2 = sig("a_e2", "mha", NS2)
        a_pv = sig("a_pv", "mha", 4 * NT)
        a_osb = sig("a_osb", "mha", 4)
        a_otr = sig("a_otr", "mha", 4)
        a_norm = sig("a_norm", "mha", 4)
        a_ctr = sig("a_ctr", "mha", 1)
        a_cok = sig("a_cok", "mha", 1)
        a_out = sig("a_out", "mha", 1)
        n_in = sig("n_in", "mamba", 4)
        n_fill = sig("n_fill", "mamba", 1)
        n_xps = sig("n_xps", "mamba", 2)
        n_cvs = sig("n_cvs", "mamba", 2)
        n_sil = sig("n_sil", "mamba", 4)
        n_xdb = sig("n_xdb", "mamba", 2)
        n_dtc = sig("n_dtc", "mamba", 1)
        n_bc1 = sig("n_bc1", "mamba", 1)
        n_bcp = sig("n_bcp", "mamba", 1)
        n_dtp = sig("n_dtp", "mamba", 2)
        n_abss = sig("n_abss", "mamba", 2)
        n_us = sig("n_us", "mamba", 1)
        n_lns = sig("n_lns", "mamba", 1)
        n_a1 = sig("n_a1", "mamba", 1)
        n_lows = sig("n_lows", "mamba", 1)
        n_poss = sig("n_poss", "mamba", 1)
        n_dts = sig("n_dts", "mamba", 1)
        n_dtxs = sig("n_dtxs", "mamba", 1)
        n_br = sig("n_br", "mamba", NSTATE)
        n_cr = sig("n_cr", "mamba", NSTATE)
        n_das = sig("n_das", "mamba", 2 * NSTATE)
        n_csc = sig("n_csc", "mamba", NSTATE)
        n_dbs = sig("n_dbs", "mamba", 2 * NSTATE)
        n_scan = sig("n_scan", "mamba", 2 * NSTATE)
        n_hcs = sig("n_hcs", "mamba", 2 * NSTATE)
        n_ya = sig("n_ya", "mamba", 2 * NSTATE)
        n_y = sig("n_y", "mamba", 1)
        n_o = sig("n_o", "mamba", 1)

        kth = [sum(1 for v in UNITS[:u] if v[0] == UNITS[u][0]) for u in range(len(UNITS))]
        NU = len(UNITS)

        def unit_end(eng, j, u):
            eng.drain().then_inc(unit_done, 1)
            if u < NU - 1:
                eng.wait_ge(unit_done, 4 * (u + 1))
            else:
                eng.wait_ge(pair_done, j + 1)

        def stack_parts(eng, k, side):
            for odd in range(2):
                a_wr[side].by(eng.dma_start(parts_dram[side, odd].rearrange("c r t -> r c t"),
                                            a_parts[side][64 * odd:64 * odd + 64]))
            eng.wait_ge(a_wr[side].sem, a_wr[side].at(k, 1))
            for odd in range(2):
                src = parts_dram[side, odd].rearrange("c (d h) t -> c d h t", d=DH)
                for slot, n, part in PART_RUNS:
                    r = 64 * odd + DH * slot
                    if side == 0:
                        rows = src[part].rearrange("d h t -> (d h t)").unsqueeze(0).to_broadcast([n, DH * (HEADS // 2) * T])
                        dst = a_q[r:r + n * DH].rearrange("r h t -> r (h t)")
                    else:
                        rows, dst = src[0:n].rearrange("c d h t -> (c d) h t"), a_k[r:r + n * DH, odd::2]
                    a_ld[side].by(eng.dma_start(dst, rows))

        def flat(ap):
            return ap.rearrange("p a b -> p (a b)")

        numbers = [x.num for x in (unit_done, x_in, x_out, dve_step)] + [x.sem.num for x in signals]
        assert numbers == list(range(unit_done.num, unit_done.num + len(numbers)))
        block = ctx.enter_context(nc.Block())

        NSMALL = 17

        @block.sync
        def _(sp):
            def load(dst, name, signal, part=slice(None)):
                sp.dma_start(dst, A[name][:, part] if name == "mw" else A[name]).then_inc(arrived[signal], 16)

            load(splits[0][2], "fw1", "fw1_in")
            load(stage_b[:], "bias", "bias_in")
            load(splits[1][2], "fw2", "fw2_in")
            small = [(stage_aw, "aw"), (stage_win, "win"), (stage_rw, "rw")] + \
                    [(t[:], name) for t, name in ((owT, "owT"), (wx, "wx"), (wdt, "wdt"), (wout, "wout"), (col, "col"),
                                                  (amat, "a_log"), (gate_b, "gate_b"), (tri, "tri"), (ident, "ident"),
                                                  (out_b, "out_b"), (cbf, "cbf"), (tree, "tree"), (pick, "pick"))]
            assert len(small) + 1 == NSMALL
            for dst, name in small:
                load(dst, name, "small_in")
            load(stage_m8[:], "mw", "small_in", slice(2 * HALF_MW, None))
            sp.wait_ge(low_done, 1)
            load(stage_ma, "mw", "mwa_in", slice(0, HALF_MW))
            sp.wait_ge(low_done, 2)
            load(stage_mb, "mw", "mwb_in", slice(HALF_MW, 2 * HALF_MW))
            with sp.Fori(0, PAIRS) as j:
                for p in range(2):
                    sp.dma_start(X[:, p], A["x"][bass.ds(j * 2 + p, 1)].rearrange("o t p d -> p (o t) d")) \
                        .then_inc(x_in, 16)
                for u, (kind, p) in enumerate(UNITS):
                    k = kth[u]
                    if kind == "mha":
                        sp.wait_ge(unit_done, 4 * u)
                        a_rld.by(sp.dma_start(rope[:], A["rope"]))
                        for odd in range(2):
                            r = 64 * odd + MAX_ROW
                            a_cst.by(sp.dma_start(a_q[r:r + 16], A["q_rows"][:, odd]))
                            a_cst.by(sp.dma_start(a_k[r:r + 16, odd::2], A["k_rows"][:, odd]))
                        sp.wait_ge(a_prt.sem, a_prt.at(k, 2))
                        stack_parts(sp, k, 0)
                        for part in range(2):
                            sp.wait_ge(a_mok.sem, a_mok.at(k, part))
                            a_mwr.by(sp.dma_start(max_dram[part], a_mT[:, part]))
                            sp.wait_ge(a_mwr.sem, a_mwr.at(k, part))
                            for odd in range(2):
                                r = 64 * odd + MAX_ROW
                                a_mld.by(sp.dma_start(a_q[r:r + 3, 4 * part:4 * part + 4],
                                                      max_dram[part].rearrange("(c h o) t -> o c h t", c=3, o=2)[odd]))
                sp.wait_ge(unit_done, 4 * NU)
                for p in range(2):
                    sp.dma_start(out[bass.ds(j * 2 + p, 1)].rearrange("o t p d -> p (o t) d"), X[:, p]).then_inc(x_out, 16)
                sp.wait_ge(x_out, 32)
                sp.sem_clear(range(numbers[0], numbers[-1] + 1))
                sp.sem_inc(pair_done, 1)

        @block.gpsimd
        def _(pool):
            pool.memset(half[:], -0.5)
            pool.memset(euler[:], float(np.exp(np.float32(1.0))))
            pool.memset(cparts[:], 0.0).then_inc(setup_done, 1)
            pool.wait_ge(setup_done, 3)

            def prologue(u, stage):
                if u == NU:
                    return
                kind, p = UNITS[u]
                k = kth[u]
                if stage == "guess":
                    pool.wait_ge(g_var.sem, g_var.at(u, 0))
                    g_rsq.by(nc.gpsimd.tensor_tensor(y0, ve, half[:, :, 0], ALU.pow))
                if stage == "rms" and kind == "mamba":
                    pool.wait_ge(r_var.sem, r_var.at(k, 0))
                    r_rsq.by(nc.gpsimd.tensor_tensor(y0, ve, half[:, :, 0], ALU.pow))
                if stage in ("exp", "exp2") and kind == "moe":
                    pool.wait_ge(e_sub.sem, e_sub.at(k, 0))
                    t = 0 if stage == "exp" else 2
                    e_exp.by(nc.gpsimd.tensor_tensor(gexp[:, t:t + 2], euler[:, t:t + 2], glog[:, t:t + 2], ALU.pow))

            with pool.Fori(0, PAIRS) as j:
                prologue(0, "guess")
                prologue(0, "exp")
                for u, (kind, p) in enumerate(UNITS):
                    k = kth[u]
                    if kind == "ffn":
                        for stage in POOL_STAGES.values():
                            prologue(u + 1, stage)
                    if kind == "moe":
                        for i in range(MSTEPS):
                            pool.wait_ge(m_hi.sem, m_hi.at(k, i))
                            m_lo.by(nc.gpsimd.tensor_tensor(m_hh[1][:, i % 3, :], m_h[:, i % 3, :],
                                                            m_hh[0][:, i % 3, :].bitcast(F32), ALU.subtract))
                            if i in POOL_STAGES:
                                prologue(u + 1, POOL_STAGES[i])
                    if kind == "mha":
                        a_fill.by(nc.gpsimd.memset(a_v[:, :, :, DH:32], 1.0))
                        for odd in (1, 0):
                            pool.wait_ge(a_fill.sem, a_fill.at(k, 1 - odd))
                            other = a_k[64 * (1 - odd):64 * (1 - odd) + 64, odd::2]
                            a_fill.by(nc.gpsimd.memset(other.bitcast(F32), 0.0))
                        pool.wait_ge(a_fill.sem, a_fill.at(k, 2))
                        for stage in POOL_STAGES.values():
                            prologue(u + 1, stage)
                    if kind == "mamba":
                        n_fill.by(nc.gpsimd.memset(n_xp[:, :, 0:3], 0.0))
                        pool.wait_ge(n_us.sem, n_us.at(k, 0))
                        n_a1.by(nc.gpsimd.tensor_scalar(n_low[:], n_u[:], -0.5, 1.0, ALU.mult, ALU.add))
                        pool.wait_ge(n_a1.sem, n_a1.at(k, 0))
                        n_lows.by(nc.gpsimd.tensor_tensor(n_low[:], n_low[:], n_u[:], ALU.mult))
                        for n in range(2 * NSTATE):
                            m = n % 2
                            pool.wait_ge(n_scan.sem, n_scan.at(k, n))
                            pool.wait_ge(n_csc.sem, n_csc.at(k, n // 2))
                            if n >= 2:
                                pool.wait_ge(n_ya.sem, n_ya.at(k, n - 2))
                            n_hcs.by(nc.gpsimd.tensor_tensor(n_hc[:, m, :], n_h[:, m, :], n_cs[:, n // 2 % 2, :],
                                                             ALU.mult))
                            if m == 1 and n // 2 in POOL_STAGES:
                                prologue(u + 1, POOL_STAGES[n // 2])
                    unit_end(pool, j, u)

        @block.scalar
        def _(act):
            def arrival(signal):
                act.wait_ge(arrived[signal], 16 * (NSMALL if signal == "small_in" else 1))

            def bias_part(first, src):
                bias_rows = biasw[first:P]
                nc.scalar.activation(bias_rows, src[first:P], ACT.Copy).then_inc(bias_act, 1)

            for n, (signal, dst, src) in enumerate(splits):
                arrival(signal)
                nc.scalar.activation(dst[0], src, ACT.Copy).then_inc(split_done, 1)
                if n == 0:
                    arrival("bias_in")
                    bias_part(0, stage_b)
                if n == 1:
                    act.wait_ge(bias_dve, 1)
                    bias_part(64, rest_b)
                if n == 5:
                    act.wait_ge(bias_dve, 2)
                    bias_part(96, rest_b)
                    nc.scalar.activation(amat[:], amat[:], ACT.Exp).then_inc(amat_done, 1)
                    act.wait_ge(amat_done, 1)
                    nc.scalar.mul(amat[:], amat[:], -1.0).then_inc(amat_done, 1)
            act.wait_ge(split_done, len(splits))
            act.wait_ge(amat_done, 2)
            act.wait_ge(bias_act, 3)
            act.drain().then_inc(setup_done, 1)
            act.wait_ge(setup_done, 3)

            def prologue(j, u, stage):
                if u == NU:
                    return
                kind, p = UNITS[u]
                k = kth[u]
                if stage == "high":
                    act.wait_ge(g_tr.sem, g_tr.at(u, 0))
                    g_xh.by(act.activation(xT[0][:, p, :], bank[:, 7, :], ACT.Copy,
                                           scale=norm_w if kind == "mamba" else 1.0))
            def ffn(j, u, k):
                for i in range(STEPS + 1):
                    if i < STEPS:
                        act.wait_ge(f_s1.sem, f_s1.at(k, i))
                        if i >= 4:
                            act.wait_ge(f_s2.sem, f_s2.at(k, i - 4))
                        f_hi.by(act.activation(f_h[0][:, i % 4, :], bank[:, i % 3, :], ACT.Relu))
                    if i in ACT_STAGES:
                        prologue(j, u + 1, ACT_STAGES[i])
                    if i in (11, 19):
                        t = (11, 19).index(i)
                        act.wait_ge(f_s2.sem, f_s2.at(k, M1 * t + M1 - 1))
                        f_evh.by(act.activation((f_q, f_k)[t][0][:], bank[:, 3 + t, :], ACT.Copy))
                    if i in (21, 23):
                        probs(j, k, (i - 21) // 2)
                    if i == 23:
                        copy_pT(j, k, 0)
                act.wait_ge(f_s2.sem, f_s2.at(k, STEPS - 1))
                f_evh.by(act.activation(f_vT[:], bank[:, 3, :], ACT.Copy))
                copy_pT(j, k, 1)
                probs(j, k, 2)
                copy_pT(j, k, 2)
                probs(j, k, 3)
                copy_pT(j, k, 3)

            def probs(j, k, qt):
                act.wait_ge(f_max.sem, f_max.at(k, qt))
                if qt >= 2:
                    act.wait_ge(f_ptr.sem, f_ptr.at(k, qt - 2))
                f_prob.by(act.activation(f_p[:, qt % 2, :], bank[:, 5, :], ACT.Exp, bias=f_s[:, 1, qt:qt + 1],
                                         scale=LEAF_SCALE, accum_out=f_s[:, 2, qt:qt + 1]))

            def copy_pT(j, k, qt):
                act.wait_ge(f_ptr.sem, f_ptr.at(k, qt))
                f_pok.by(act.activation(f_pT[:, :, qt * P:(qt + 1) * P],
                                        bank[:, 6, :].rearrange("p (t q) -> p t q", t=NT), ACT.Copy))

            def moe(j, u, k):
                for i in range(MSTEPS + 1):
                    if i < MSTEPS:
                        act.wait_ge(m_a.sem, m_a.at(k, i))
                        if i >= 2:
                            act.wait_ge(m_ts.sem, m_ts.at(k, i - 2))
                        m_silu.by(act.activation(m_sl[:, i % 2, :], bank[:, i % 2, :], ACT.Silu))
                    if i >= 1:
                        act.wait_ge(m_hs.sem, m_hs.at(k, i - 1))
                        if i - 1 >= 3:
                            act.wait_ge(m_s2.sem, m_s2.at(k, i - 4))
                        m_hi.by(act.activation(m_hh[0][:, (i - 1) % 3, :], m_h[:, (i - 1) % 3, :], ACT.Copy))
                    if i in ACT_STAGES:
                        prologue(j, u + 1, ACT_STAGES[i])
                act.wait_ge(m_s2.sem, m_s2.at(k, MSTEPS - 1))
                m_y.by(act.activation(m_yT[:], bank[:, 6, :], ACT.Copy))

            def mha(j, u, k):
                for side in range(2):
                    for c in range(3):
                        if c == 0:
                            act.wait_ge(a_rotd.sem, a_rotd.at(k, side))
                        else:
                            act.wait_ge(a_res.sem, a_res.at(k, 2 * side + c - 1))
                        a_prt.by(act.activation(a_parts[side][:, c, :], a_rot[side][0], ACT.Copy))
                act.wait_ge(a_prt.sem, a_prt.at(k, 5))
                stack_parts(nc.scalar, k, 1)
                for stage in ACT_STAGES.values():
                    prologue(j, u + 1, stage)
                max_rows(k, 0)
                for side in range(2):
                    act.wait_ge(a_wr[side].sem, a_wr[side].at(k, 1))
                for s_ in range(NS2):
                    g, kt = s_ // (2 * NT), s_ // 2 % NT
                    w = T - kt * P
                    act.wait_ge(a_s2.sem, a_s2.at(k, s_))
                    if s_ >= 4:
                        act.wait_ge(a_pv.sem, a_pv.at(k, (s_ - 4) // 2))
                    b = 2 * (s_ % 2)
                    a_e2.by(act.activation(a_p[:, s_ % 4, :, 0:w], bank[:, b:b + 2, 0:w], ACT.Exp))
                    if s_ % 8 == 3 and g >= 1:
                        heads_out(k, g - 1)
                    if s_ == MAX2:
                        max_rows(k, 1)
                heads_out(k, 3)
                act.wait_ge(a_ctr.sem, a_ctr.at(k, 0))
                a_cok.by(act.activation(a_o, bank[:, 4, :], ACT.Copy))

            def max_rows(k, part):
                act.wait_ge(a_mtr.sem, a_mtr.at(k, part))
                a_mok.by(act.activation(a_mT[:, part], bank[0:24, 7, 0:T // 2].bitcast(BF16), ACT.Copy))

            def heads_out(k, g):
                act.wait_ge(a_pv.sem, a_pv.at(k, NT * g + NT - 1))
                if g >= 1:
                    act.wait_ge(a_otr.sem, a_otr.at(k, g - 1))
                a_osb.by(act.activation(a_o, bank[:, 6, :], ACT.Copy))

            def mamba(j, u, k):
                for m in range(2):
                    act.wait_ge(n_in.sem, n_in.at(k, m))
                    n_xps.by(act.activation(n_xp[:, m, 3:3 + T], bank[:, m, :], ACT.Copy))
                for m in range(2):
                    act.wait_ge(n_in.sem, n_in.at(k, 2 + m))
                    n_sil.by(act.activation(n_sz[:, m, :], bank[:, 2 + m, :], ACT.Silu))
                for m in range(2):
                    act.wait_ge(n_cvs.sem, n_cvs.at(k, m))
                    n_sil.by(act.activation(n_xc[:, m, :], n_cv[:, m, :], ACT.Silu))
                act.activation(lnv, half[:, 0, 0:NT], ACT.Exp)
                act.wait_ge(n_xdb.sem, n_xdb.at(k, 0))
                n_dtc.by(act.activation(n_dtr[:], bank[0:64, 4, :], ACT.Copy))
                act.wait_ge(n_xdb.sem, n_xdb.at(k, 1))
                n_bc1.by(act.activation(n_bc[:], bank[0:96, 5, :], ACT.Copy))
                for m in range(2):
                    act.wait_ge(n_dtp.sem, n_dtp.at(k, m))
                    n_abss.by(act.activation(n_abs[:, m, :], bank[:, m, :], ACT.Abs, bias=b_dt[:, m:m + 1]))
                act.wait_ge(n_abss.sem, n_abss.at(k, 1))
                n_us.by(act.activation(n_u[:], n_abs[:], ACT.Exp, scale=-1.0))
                act.wait_ge(n_us.sem, n_us.at(k, 0))
                n_lns.by(act.activation(n_ln[:], n_u[:], ACT.Ln, bias=1.0))
                act.wait_ge(n_dts.sem, n_dts.at(k, 0))
                for n in range(NSTATE):
                    for m in range(NHALF):
                        if n >= 1:
                            act.wait_ge(n_scan.sem, n_scan.at(k, 2 * n + m - 2))
                        n_das.by(act.activation(n_da[:, m, :], n_dt[:, m, :], ACT.Exp, scale=amat[:, m, n:n + 1]))
                    act.wait_ge(n_cr.sem, n_cr.at(k, n))
                    if n >= 2:
                        act.wait_ge(n_hcs.sem, n_hcs.at(k, 2 * n - 3))
                    n_csc.by(act.activation(n_cs[:, n % 2, :], bank[:, n % 2, :], ACT.Copy))
                    if n in ACT_STAGES:
                        prologue(j, u + 1, ACT_STAGES[n])

            with act.Fori(0, PAIRS) as j:
                for stage in ACT_STAGES.values():
                    prologue(j, 0, stage)
                for u, (kind, p) in enumerate(UNITS):
                    {"ffn": ffn, "moe": moe, "mha": mha, "mamba": mamba}[kind](j, u, kth[u])
                    unit_end(act, j, u)

        @block.vector
        def _(dve):
            V = nc.vector
            for n, (_, dst, src) in enumerate(splits):
                dve.wait_ge(split_done, n + 1)
                V.tensor_tensor(dst[1], src, dst[0].bitcast(F32), ALU.subtract).then_inc(low_done, 1)
                if n == 0:
                    dve.wait_ge(bias_act, 1)
                    V.tensor_tensor(rest_b[64:128, :], stage_b[64:128, :], biasw[64:128, :], ALU.subtract) \
                        .then_inc(bias_dve, 1)
                if n == 1:
                    dve.wait_ge(bias_act, 2)
                    V.tensor_tensor(rest_b[96:128, :], rest_b[96:128, :], biasw[96:128, :], ALU.subtract) \
                        .then_inc(bias_dve, 1)
            dve.wait_ge(low_done, len(splits))
            dve.wait_ge(bias_dve, 2)
            V.memset(ve, 1.0).then_inc(setup_done, 1)
            dve.wait_ge(setup_done, 3)

            steps = [0]

            def step(j, ins):
                steps[0] += 1
                ins.then_inc(dve_step, 1)
                dve.wait_ge(dve_step, steps[0])

            def newton(j):
                step(j, V.tensor_tensor(y2, y0, y0, ALU.mult))
                step(j, V.tensor_tensor(y2, y2, ve, ALU.mult))
                step(j, V.tensor_scalar(y2, y2, -0.5, 1.5, ALU.mult, ALU.add))
                step(j, V.tensor_tensor(rstd, y2, y0, ALU.mult))

            def stats(j, src):
                for t in range(NT):
                    ins = V.bn_stats(st[:, t, :], src[:, t, :])
                step(j, ins)
                for t in range(NT):
                    ins = V.bn_aggr(mv[:, t, :], st[:, t, :])
                step(j, ins)

            def prologue(j, u, stage):
                if u == NU:
                    return
                kind, p = UNITS[u]
                k = kth[u]
                if stage == "stats":
                    if u < 2:
                        dve.wait_ge(x_in, 32)
                    stats(j, X[:, p])
                    g_var.by(V.tensor_scalar(ve, mv[:, :, 1], EPS, None, ALU.add))
                if stage == "rows":
                    dve.wait_ge(g_var.sem, g_var.at(u, 0))
                    dve.wait_ge(g_rsq.sem, g_rsq.at(u, 0))
                    newton(j)
                    for t in range(NT):
                        ins = V.tensor_scalar(xn[:, p, t, :], X[:, p, t, :], mv[:, t, 0:1], rstd[:, t:t + 1],
                                              ALU.subtract, ALU.mult)
                    if kind == "mamba":
                        step(j, ins)
                        stats(j, xn[:, p])
                        step(j, V.tensor_tensor(y2, mv[:, :, 0], mv[:, :, 0], ALU.mult))
                        step(j, V.tensor_tensor(y2, y2, mv[:, :, 1], ALU.add))
                        r_var.by(V.tensor_scalar(ve, y2, EPS, None, ALU.add))
                    else:
                        g_xn.by(ins)
                if stage == "rms" and kind == "mamba":
                    dve.wait_ge(r_rsq.sem, r_rsq.at(k, 0))
                    dve.wait_ge(r_var.sem, r_var.at(k, 0))
                    newton(j)
                    for t in range(NT):
                        ins = V.tensor_scalar(xm[p][:, t, :], xn[:, p, t, :], rstd[:, t:t + 1], None, ALU.mult)
                    g_xn.by(ins)
                if stage == "low":
                    dve.wait_ge(g_xh.sem, g_xh.at(u, 0))
                    g_xl.by(V.scalar_tensor_tensor(xT[1][:, p, :], bank[:, 7, :], norm_w if kind == "mamba" else 1.0,
                                                   xT[0][:, p, :].bitcast(F32), ALU.mult, ALU.subtract))
                if kind == "ffn":
                    if stage == "first":
                        dve.wait_ge(t_sc.sem, t_sc.at(k, 0))
                        t_bit.by(V.tensor_scalar(dbit[:], bank[0:96, 7, :], node_b[0:96], 0.0, ALU.add, ALU.is_ge))
                    if stage in ("second", "third", "fourth"):
                        t = ("second", "third", "fourth").index(stage)
                        dve.wait_ge(t_cnt.sem, t_cnt.at(k, t))
                        t_sel.by(V.tensor_scalar(R[:, p, t, :], bank[:, 7, :], leaf_thr, None, ALU.is_ge))
                if kind == "moe":
                    if stage == "first":
                        dve.wait_ge(e_log.sem, e_log.at(k, 0))
                        raw = bank[:, 7, 0:NT * EXPERTS].rearrange("p (t e) -> p t e", t=NT)
                        step(j, V.tensor_reduce(gmax, raw, AX_X, ALU.max))
                        e_sub.by(V.tensor_tensor(glog, raw, per_token(gmax), ALU.subtract))
                    if stage == "scores":
                        dve.wait_ge(e_exp.sem, e_exp.at(k, 1))
                        scores(j)
                    if stage == "third":
                        ranks(j, cmp[p])
                    if stage == "combine":
                        combine(j)
                    if stage == "row":
                        dve.wait_ge(e_tr.sem, e_tr.at(k, 0))
                        e_row.by(V.tensor_copy(R[0:96, p, 0, :], bank[0:96, 7, 0:T // 2].bitcast(BF16)))

            def per_token(v):
                return v.unsqueeze(2).to_broadcast([P, NT, EXPERTS])

            def scores(j):
                step(j, V.tensor_reduce(gsum, gexp, AX_X, ALU.add))
                step(j, V.reciprocal(grec, gsum))
                step(j, V.tensor_tensor(gsc, gexp, per_token(grec), ALU.mult))
                step(j, V.tensor_tensor(gbi, gsc, gate_b[:].unsqueeze(1).to_broadcast([P, NT, EXPERTS]), ALU.add))

            def ranks(j, cmp):
                full = [P, NT, EXPERTS, EXPERTS]
                other = gbi.unsqueeze(2).to_broadcast(full)
                own = gbi.unsqueeze(3).to_broadcast(full)
                V.tensor_tensor(cmp[:, 0], other, own, ALU.is_gt)
                step(j, V.tensor_tensor(cmp[:, 1], other, own, ALU.is_equal))
                step(j, V.tensor_tensor(cmp[:, 1], cmp[:, 1], tri[:].unsqueeze(1).to_broadcast(full), ALU.mult))
                step(j, V.tensor_tensor(cmp[:, 0], cmp[:, 0], cmp[:, 1], ALU.add))
                step(j, V.tensor_reduce(grank, cmp[:, 0], AX_X, ALU.add))

            def combine(j):
                step(j, V.scalar_tensor_tensor(gcmb, grank, 1.5, gsc, ALU.is_lt, ALU.mult))
                step(j, V.tensor_copy(cparts[:, :, 0:8], gcmb))
                step(j, V.tensor_tensor(gr1, gcmb, cparts[:, :, 0:8], ALU.subtract))
                step(j, V.tensor_copy(cparts[:, :, 32:40], gr1))
                step(j, V.tensor_tensor(gr2, gr1, cparts[:, :, 32:40], ALU.subtract))
                e_prt.by(V.tensor_copy(cparts[:, :, 64:72], gr2))

            def add_rows(j, p, src, scale=1.0):
                V.scalar_tensor_tensor(flat(X[:, p]), src, scale, flat(X[:, p]), ALU.mult, ALU.add)

            def ffn(j, u, k, p):
                for i in range(STEPS):
                    dve.wait_ge(f_hi.sem, f_hi.at(k, i))
                    f_lo.by(V.scalar_tensor_tensor(f_h[1][:, i % 4, :], bank[:, i % 3, :], 0.0,
                                                   f_h[0][:, i % 4, :].bitcast(F32), ALU.max, ALU.subtract))
                    if i in DVE_STAGES:
                        prologue(j, u + 1, DVE_STAGES[i])
                    if i in (11, 19):
                        t = (11, 19).index(i)
                        dve.wait_ge(f_evh.sem, f_evh.at(k, t))
                        f_evl.by(V.tensor_tensor((f_q, f_k)[t][1][:], bank[:, 3 + t, :], (f_q, f_k)[t][0][:].bitcast(F32),
                                                 ALU.subtract))
                    if i in (20, 22):
                        score_max(j, k, (i - 20) // 2)
                dve.wait_ge(f_vtr.sem, f_vtr.at(k, 0))
                f_vok.by(V.tensor_copy(f_v[:], bank[:, 3, :].rearrange("p (t d) -> p t d", t=NT)))
                score_max(j, k, 2)
                score_max(j, k, 3)
                dve.wait_ge(f_prob.sem, f_prob.at(k, 3))
                step(j, V.reciprocal(f_s[:, 3, :], f_s[:, 2, :]))
                step(j, V.tensor_scalar(f_s[:, 4, :], f_s[:, 3, :], 0.5, None, ALU.mult))
                dve.wait_ge(f_pv.sem, f_pv.at(k, NT - 1))
                for qt in range(NT):
                    V.scalar_tensor_tensor(X[:, p, qt, :], bank[:, 4, qt * P:(qt + 1) * P], f_s[:, 4, qt:qt + 1],
                                           X[:, p, qt, :], ALU.mult, ALU.add)

            def score_max(j, k, qt):
                dve.wait_ge(f_sco.sem, f_sco.at(k, qt))
                step(j, V.tensor_reduce(f_s[:, 0, qt:qt + 1], bank[:, 5, :], AX_X, ALU.max))
                f_max.by(V.tensor_scalar(f_s[:, 1, qt:qt + 1], f_s[:, 0, qt:qt + 1], -LEAF_SCALE, None, ALU.mult))

            def moe(j, u, k, p):
                for i in range(MSTEPS):
                    e = i // 2
                    dve.wait_ge(m_b.sem, m_b.at(k, i))
                    dve.wait_ge(m_silu.sem, m_silu.at(k, i))
                    if i >= 3:
                        dve.wait_ge(m_lo.sem, m_lo.at(k, i - 3))
                    if e < EXPERTS:
                        m_ts.by(V.tensor_tensor(m_t[:, i % 2, :], m_sl[:, i % 2, :], bank[:, 2 + i % 2, :], ALU.mult))
                        dve.wait_ge(m_ts.sem, m_ts.at(k, i))
                        dve.wait_ge(m_cr.sem, m_cr.at(k, e))
                        m_hs.by(V.tensor_tensor(m_h[:, i % 3, :], m_t[:, i % 2, :], bank[:, 4 + e % 2, :], ALU.mult))
                    else:
                        m_hs.by(V.tensor_tensor(m_h[:, i % 3, :], m_sl[:, i % 2, :], bank[:, 2 + i % 2, :], ALU.mult))
                    if i in DVE_STAGES:
                        prologue(j, u + 1, DVE_STAGES[i])
                dve.wait_ge(m_ytr.sem, m_ytr.at(k, 0))
                add_rows(j, p, bank[:, 0, :], 0.5)

            def mha(j, u, k, p):
                V.tensor_tensor(X[:, p], X[:, p], out_b[:].unsqueeze(1).to_broadcast([P, NT, P]), ALU.add)
                dve.wait_ge(a_rld.sem, a_rld.at(k, 0))
                for side in range(2):
                    s_ = HEAD_SCALE if side == 0 else 1.0
                    for c in range(2):
                        dve.wait_ge(a_proj.sem, a_proj.at(k, 2 * side + c))
                        ins = V.scalar_tensor_tensor(a_rot[side][c], bank[:, 2 * side + c, :], s_, rope[:, c, :],
                                                     ALU.mult, ALU.mult)
                    step(j, ins)
                    a_rotd.by(V.tensor_tensor(a_rot[side][0], a_rot[side][0], a_rot[side][1], ALU.add))
                    residual(k, side, 0)
                    if side == 1:
                        dve.wait_ge(a_proj.sem, a_proj.at(k, 4))
                        a_vok.by(V.tensor_copy(a_v[:, :, :, 0:DH],
                                               bank[:, 4, :].rearrange("p (t h d) -> p t h d", t=NT, d=DH)))
                    residual(k, side, 1)
                for stage in DVE_STAGES.values():
                    prologue(j, u + 1, stage)
                maxima(k, range(NS1))
                max_parts(j, k, 0)
                maxima(k, range(NS1, 2 * NS1))
                max_parts(j, k, 1)
                for g in range(4):
                    dve.wait_ge(a_otr.sem, a_otr.at(k, g))
                    src = bank[:, 7, :].rearrange("p (t c w) -> p t c w", t=NT, c=4)
                    step(j, V.reciprocal(a_rec[:], src[:, :, :, DH]))
                    a_norm.by(V.tensor_tensor(a_rows[:, :, 32 * g:32 * g + 32].rearrange("p t (c d) -> p t c d", d=DH),
                                              src[:, :, :, 0:DH], a_rec[:].unsqueeze(3).to_broadcast([P, NT, 4, DH]),
                                              ALU.mult))
                dve.wait_ge(a_out.sem, a_out.at(k, 0))
                add_rows(j, p, bank[:, 5, :])

            def residual(k, side, c):
                dve.wait_ge(a_prt.sem, a_prt.at(k, 3 * side + c))
                a_res.by(V.tensor_tensor(a_rot[side][0], a_rot[side][0], a_parts[side][:, c, :], ALU.subtract))

            def maxima(k, which):
                for s_ in which:
                    part, (qt, h0, nh) = s_ // NS1, SLOT1[s_ % NS1]
                    w = (qt + 1) * P
                    dve.wait_ge(a_s1.sem, a_s1.at(k, s_))
                    src = bank[:, 4 + s_ % 2, 0:nh * w].rearrange("p (h w) -> p h w", w=w)
                    a_m1.by(V.tensor_reduce(a_mx[:, part, qt, h0:h0 + nh], src, AX_X, ALU.max, negate=True))

            def max_parts(j, k, part):
                dve.wait_ge(a_m1.sem, a_m1.at(k, part * NS1 + NS1 - 1))
                step(j, V.tensor_copy(a_mp[:, part, :, 0, :], a_mx[:, part]))
                step(j, V.tensor_tensor(a_mr[:], a_mx[:, part], a_mp[:, part, :, 0, :], ALU.subtract))
                step(j, V.tensor_copy(a_mp[:, part, :, 1, :], a_mr[:]))
                step(j, V.tensor_tensor(a_mx[:, part], a_mr[:], a_mp[:, part, :, 1, :], ALU.subtract))
                a_mpt.by(V.tensor_copy(a_mp[:, part, :, 2, :], a_mx[:, part]))

            def mamba(j, u, k, p):
                V.tensor_tensor(X[:, p], X[:, p], xn[:, p], ALU.add)
                dve.wait_ge(n_fill.sem, n_fill.at(k, 0))
                for m in range(2):
                    dve.wait_ge(n_xps.sem, n_xps.at(k, m))
                    step(j, V.tensor_scalar(n_cv[:, m, :], n_xp[:, m, 0:T], conv_w[:, m, 0:1], conv_b[:, m:m + 1],
                                            ALU.mult, ALU.add))
                    for c in range(1, 4):
                        ins = V.scalar_tensor_tensor(n_cv[:, m, :], n_xp[:, m, c:c + T], conv_w[:, m, c:c + 1],
                                                     n_cv[:, m, :], ALU.mult, ALU.add)
                        if c < 3:
                            step(j, ins)
                    n_cvs.by(ins)
                dve.wait_ge(n_bc1.sem, n_bc1.at(k, 0))
                step(j, V.tensor_tensor(n_r[:], bank[0:96, 5, :], n_bc[:], ALU.subtract))
                V.tensor_copy(n_bc[32:64], n_r[32:64])
                step(j, V.tensor_copy(n_bc[64:96], n_r[64:96]))
                step(j, V.tensor_tensor(n_r[64:96], n_r[64:96], n_bc[64:96], ALU.subtract))
                n_bcp.by(V.tensor_copy(n_bc[64:96], n_r[64:96]))
                for m in range(2):
                    dve.wait_ge(n_abss.sem, n_abss.at(k, m))
                    ins = V.tensor_scalar(n_pos[:, m, :], bank[:, m, :], b_dt[:, m:m + 1], 0.0, ALU.add, ALU.max)
                n_poss.by(ins)
                dve.wait_ge(n_us.sem, n_us.at(k, 0))
                dve.wait_ge(n_sil.sem, n_sil.at(k, 3))
                step(j, V.tensor_scalar(n_cor[:], n_u[:], 1.0, -1.0, ALU.add, ALU.add))
                step(j, V.tensor_tensor(n_cor[:], n_u[:], n_cor[:], ALU.subtract))
                dve.wait_ge(n_lns.sem, n_lns.at(k, 0))
                step(j, V.tensor_tensor(n_cor[:], n_cor[:], n_ln[:], ALU.add))
                dve.wait_ge(n_lows.sem, n_lows.at(k, 0))
                step(j, V.tensor_tensor(n_cor[:], n_cor[:], n_low[:], ALU.max))
                step(j, V.tensor_tensor(n_cor[:], n_cor[:], n_u[:], ALU.min))
                dve.wait_ge(n_poss.sem, n_poss.at(k, 0))
                n_dts.by(V.tensor_tensor(n_dt[:], n_cor[:], n_pos[:], ALU.add))
                dve.wait_ge(n_dts.sem, n_dts.at(k, 0))
                dve.wait_ge(n_sil.sem, n_sil.at(k, 3))
                n_dtxs.by(V.tensor_tensor(n_dtx[:], n_dt[:], n_xc[:], ALU.mult))
                dve.wait_ge(n_dtxs.sem, n_dtxs.at(k, 0))
                for n in range(NSTATE):
                    dve.wait_ge(n_br.sem, n_br.at(k, n))
                    for m in range(NHALF):
                        i = 2 * n + m
                        if n >= 1:
                            dve.wait_ge(n_scan.sem, n_scan.at(k, i - 2))
                        n_dbs.by(V.tensor_tensor(n_db[:, m, :], n_dtx[:, m, :], bank[:, 4 + n % 2, :], ALU.mult))
                    for m in range(NHALF):
                        i = 2 * n + m
                        dve.wait_ge(n_dbs.sem, n_dbs.at(k, i))
                        dve.wait_ge(n_das.sem, n_das.at(k, i))
                        if n >= 1:
                            dve.wait_ge(n_hcs.sem, n_hcs.at(k, i - 2))
                        n_scan.by(V.tensor_tensor_scan(n_h[:, m, :], n_da[:, m, :], n_db[:, m, :], 0.0,
                                                       ALU.mult, ALU.add))
                    if n in DVE_STAGES:
                        prologue(j, u + 1, DVE_STAGES[n])
                for at in range(NSTATE, NSTATE + 2):
                    prologue(j, u + 1, DVE_STAGES[at])
                dve.wait_ge(n_ya.sem, n_ya.at(k, 2 * NSTATE - 1))
                dve.wait_ge(n_scan.sem, n_scan.at(k, 2 * NSTATE - 1))
                for m in range(2):
                    step(j, V.scalar_tensor_tensor(n_db[:, m, :], n_xc[:, m, :], d_skip[:, m:m + 1], bank[:, 2 + m, :],
                                                   ALU.mult, ALU.add))
                n_y.by(V.tensor_tensor(n_db[:], n_db[:], n_sz[:], ALU.mult))
                dve.wait_ge(n_o.sem, n_o.at(k, 0))
                add_rows(j, p, bank[:, 6, :])

            with dve.Fori(0, PAIRS) as j:
                steps[0] = 0
                for stage in DVE_STAGES.values():
                    prologue(j, 0, stage)
                for u, (kind, p) in enumerate(UNITS):
                    {"ffn": ffn, "moe": moe, "mha": mha, "mamba": mamba}[kind](j, u, kth[u], p)
                    unit_end(dve, j, u)

        @block.tensor
        def _(pe):
            mm = nc.tensor.matmul
            pe.wait_ge(setup_done, 3)

            def product(dst, w, x, start=True, stop=True):
                mm(dst, w[0], x[0], start=start, stop=False)
                mm(dst, w[0], x[1], start=False, stop=False)
                return mm(dst, w[1], x[0], start=False, stop=stop)

            def xs(p):
                return [xT[0][:, p, :], xT[1][:, p, :]]

            def rows(dst, src, idn):
                for t in range(NT):
                    ins = nc.tensor.transpose(dst(t), src(t), idn)
                return ins

            def back(b, src):
                return rows(lambda t: bank[:, b, t * P:(t + 1) * P], lambda t: src[:, t * P:(t + 1) * P], ident[:])

            def prologue(j, u, stage):
                if u == NU:
                    return
                kind, p = UNITS[u]
                k = kth[u]
                if stage == "turn":
                    pe.wait_ge(g_xn.sem, g_xn.at(u, 0))
                    src = xm[p] if kind == "mamba" else xn[:, p]
                    g_tr.by(rows(lambda t: bank[:, 7, t * P:(t + 1) * P], lambda t: src[:, t, :], ident[:]))
                if kind == "ffn":
                    if stage == "first":
                        pe.wait_ge(g_xl.sem, g_xl.at(u, 0))
                        t_sc.by(product(bank[0:96, 7, :], [rw[0][:, 0:96], rw[1][:, 0:96]], xs(p)))
                    if stage == "second":
                        pe.wait_ge(t_bit.sem, t_bit.at(k, 0))
                        t_cnt.by(mm(bank[:, 7, :], tree[:, 0, :], dbit[:], start=True, stop=True))
                    if stage in ("third", "fourth"):
                        t = ("third", "fourth").index(stage) + 1
                        pe.wait_ge(t_sel.sem, t_sel.at(k, t - 1))
                        t_cnt.by(mm(bank[:, 7, :], tree[:, t, :], dbit[:], start=True, stop=True))
                if kind == "moe":
                    if stage == "first":
                        pe.wait_ge(g_xl.sem, g_xl.at(u, 0))
                        for t in range(NT):
                            x = [xT[c][:, p, t * P:(t + 1) * P] for c in range(2)]
                            ins = product(bank[:, 7, t * EXPERTS:(t + 1) * EXPERTS], x,
                                          [rw[0][:, 96:104], rw[1][:, 96:104]])
                        e_log.by(ins)
                    if stage == "weights":
                        pe.wait_ge(e_prt.sem, e_prt.at(k, 0))
                        tr = bank[0:96, 7, 0:T // 2].bitcast(BF16)
                        e_tr.by(rows(lambda t: tr[:, t * P:(t + 1) * P], lambda t: cparts[:, t, :], identb))

            def ready(j, u):
                kind, p = UNITS[u]
                pe.wait_ge(g_xl.sem, g_xl.at(u, 0))

            def ffn(j, u, k, p):
                x = xs(p)
                ready(j, u)
                pe.wait_ge(t_sel.sem, t_sel.at(k, TREES - 1))
                for i in range(STEPS + 2):
                    if i < STEPS:
                        t, m = divmod(i, M1)
                        b = bank[:, i % 3, :]
                        if i >= 3:
                            pe.wait_ge(f_lo.sem, f_lo.at(k, i - 3))
                        product(b, [fw1[c][:, t, m * P:(m + 1) * P] for c in range(2)], x, stop=False)
                        f_s1.by(mm(b, b1w[:, t, m * P:(m + 1) * P], R[:, p, t, :], start=False, stop=True))
                    if i >= 2:
                        i2 = i - 2
                        t, m = divmod(i2, M1)
                        acc = bank[:, 3 + t % 2, :]
                        pe.wait_ge(f_lo.sem, f_lo.at(k, i2))
                        if i2 == 2 * M1:
                            pe.wait_ge(f_evl.sem, f_evl.at(k, 0))
                        if m == 0:
                            mm(acc, b2w[:, t, :], R[:, p, t, :], start=True, stop=False)
                        f_s2.by(product(acc, [fw2[c][:, t, m, :] for c in range(2)],
                                        [f_h[c][:, i2 % 4, :] for c in range(2)], start=False, stop=m == M1 - 1))
                    if i in PE_STAGES:
                        prologue(j, u + 1, PE_STAGES[i])
                    if i in (21, 23):
                        score(j, k, (i - 21) // 2)
                    if i == 24:
                        turn(j, k, 0)
                pe.wait_ge(f_evh.sem, f_evh.at(k, 2))
                f_vtr.by(back(3, f_vT))
                score(j, k, 2)
                turn(j, k, 1)
                turn(j, k, 2)
                score(j, k, 3)
                pe.wait_ge(f_vok.sem, f_vok.at(k, 0))
                weigh(j, k, 0)
                weigh(j, k, 1)
                weigh(j, k, 2)
                turn(j, k, 3)
                weigh(j, k, 3)

            def score(j, k, qt):
                if qt == 0:
                    pe.wait_ge(f_evl.sem, f_evl.at(k, 1))
                else:
                    pe.wait_ge(f_prob.sem, f_prob.at(k, qt - 1))
                f_sco.by(product(bank[:, 5, :], [f_q[c][:, qt * P:(qt + 1) * P] for c in range(2)],
                                 [f_k[c][:] for c in range(2)]))

            def turn(j, k, qt):
                pe.wait_ge(f_prob.sem, f_prob.at(k, qt))
                if qt:
                    pe.wait_ge(f_pok.sem, f_pok.at(k, qt - 1))
                f_ptr.by(rows(lambda t: bank[:, 6, t * P:(t + 1) * P],
                              lambda t: f_p[:, qt % 2, t * P:(t + 1) * P], ident[:]))

            def weigh(j, k, qt):
                pe.wait_ge(f_pok.sem, f_pok.at(k, qt))
                for kt in range(NT):
                    ins = mm(bank[:, 4, qt * P:(qt + 1) * P], f_pT[:, kt, qt * P:(qt + 1) * P], f_v[:, kt, :],
                             start=kt == 0, stop=kt == NT - 1)
                f_pv.by(ins)

            def moe(j, u, k, p):
                x = xs(p)
                ready(j, u)
                pe.wait_ge(e_row.sem, e_row.at(k, 0))
                for i in range(MSTEPS + 3):
                    if i < MSTEPS:
                        e, m = divmod(i, 2)
                        if i >= 2:
                            pe.wait_ge(m_ts.sem, m_ts.at(k, i - 2))
                        m_a.by(product(bank[:, i % 2, :], [mw[c][:, e, m, :] for c in range(2)], x))
                        m_b.by(product(bank[:, 2 + i % 2, :], [mw[c][:, e, 2 + m, :] for c in range(2)], x))
                        if m == 0 and e < EXPERTS:
                            if e >= 2:
                                pe.wait_ge(m_hs.sem, m_hs.at(k, i - 3))
                            m_cr.by(mm(bank[:, 4 + e % 2, :], pick[:, e:e + 1].to_broadcast([96, P]), R[0:96, p, 0, :],
                                       start=True, stop=True))
                    if i >= 3:
                        i2 = i - 3
                        e, m = divmod(i2, 2)
                        pe.wait_ge(m_lo.sem, m_lo.at(k, i2))
                        m_s2.by(product(bank[:, 6, :], [mw[c][:, e, 4 + m, :] for c in range(2)],
                                        [m_hh[c][:, i2 % 3, :] for c in range(2)], start=i2 == 0, stop=i2 == MSTEPS - 1))
                    if i in PE_STAGES:
                        prologue(j, u + 1, PE_STAGES[i])
                pe.wait_ge(m_y.sem, m_y.at(k, 0))
                pe.wait_ge(m_ts.sem, m_ts.at(k, 2 * EXPERTS - 1))
                pe.wait_ge(m_hs.sem, m_hs.at(k, MSTEPS - 1))
                m_ytr.by(back(0, m_yT))

            def mha(j, u, k, p):
                x = xs(p)
                ready(j, u)
                for n in range(4):
                    a_proj.by(product(bank[:, n, :], [aw[c][:, n, :] for c in range(2)], x))
                for t in range(NT):
                    ins = product(bank[:, 4, t * P:(t + 1) * P], [xT[c][:, p, t * P:(t + 1) * P] for c in range(2)],
                                  [aw[c][:, 4, :] for c in range(2)])
                a_proj.by(ins)
                for stage in PE_STAGES.values():
                    prologue(j, u + 1, stage)
                for side in range(2):
                    pe.wait_ge(a_ld[side].sem, a_ld[side].at(k, 5))
                pe.wait_ge(a_cst.sem, a_cst.at(k, 3))
                pe.wait_ge(a_fill.sem, a_fill.at(k, 2))
                pe.wait_ge(a_vok.sem, a_vok.at(k, 0))
                for s_ in range(NS1):
                    score_slot(k, s_)
                turn_max(k, 0)
                done = NS1
                while done < NS1 + EARLY:
                    score_slot(k, done)
                    done += 1
                for s_ in range(NS2 + 3):
                    if s_ < NS2:
                        g, kt, pair = s_ // (2 * NT), s_ // 2 % NT, s_ % 2
                        w = T - kt * P
                        if s_ % (NS2 // 2) == 0:
                            pe.wait_ge(a_mld.sem, a_mld.at(k, 1 + 2 * (s_ // (NS2 // 2))))
                        if s_ >= 2:
                            pe.wait_ge(a_e2.sem, a_e2.at(k, s_ - 2))
                        for n in range(2):
                            h = 4 * g + 2 * pair + n
                            b = 2 * (s_ % 2) + n
                            mm(bank[:, b, 0:w], a_k[:, h, kt * P:(kt + 1) * P], a_q[:, h // 2, kt * P:T],
                               start=True, stop=False)
                            ins = mm(bank[:, b, 0:P], identb, mask_kq, start=False, stop=True)
                        a_s2.by(ins)
                    while done < min(2 * NS1, NS1 + EARLY + 3 * (s_ + 1) // 2):
                        score_slot(k, done)
                        done += 1
                    if s_ == MAX2:
                        turn_max(k, 1)
                    if s_ >= 3 and s_ % 2 == 1:
                        q_ = (s_ - 3) // 2
                        g, kt = divmod(q_, NT)
                        pe.wait_ge(a_e2.sem, a_e2.at(k, 2 * q_ + 1))
                        if kt == 0 and g >= 1:
                            pe.wait_ge(a_osb.sem, a_osb.at(k, g - 1))
                        for c in range(4):
                            ring = (2 * q_ + c // 2) % 4
                            ins = mm(bank[32 * c:32 * c + 32, 6, kt * P:T], a_v[:, kt, 4 * g + c, :],
                                     a_p[:, ring, c % 2, 0:T - kt * P], start=kt == 0, stop=kt == NT - 1)
                        a_pv.by(ins)
                        if kt == 1 and g >= 1:
                            head_rows(k, g - 1)
                head_rows(k, 3)
                pe.wait_ge(a_norm.sem, a_norm.at(k, 3))
                pe.wait_ge(a_m1.sem, a_m1.at(k, 2 * NS1 - 1))
                a_ctr.by(rows(lambda t: bank[:, 4, t * P:(t + 1) * P], lambda t: a_rows[:, t, :], ident[:]))
                pe.wait_ge(a_cok.sem, a_cok.at(k, 0))
                for t in range(NT):
                    ins = mm(bank[:, 5, t * P:(t + 1) * P], a_o[:, t * P:(t + 1) * P], owT[:], start=True, stop=True)
                a_out.by(ins)

            def score_slot(k, s_):
                part, (qt, h0, nh) = s_ // NS1, SLOT1[s_ % NS1]
                w = (qt + 1) * P
                b = 4 + s_ % 2
                if s_ >= 2:
                    pe.wait_ge(a_m1.sem, a_m1.at(k, s_ - 2))
                for n in range(nh):
                    h = 8 * part + h0 + n
                    mm(bank[:, b, n * w:(n + 1) * w], a_q[:, h // 2, qt * P:(qt + 1) * P], a_k[:, h, 0:w],
                       start=True, stop=False)
                    ins = mm(bank[:, b, n * w + qt * P:(n + 1) * w], identb, mask_qk, start=False, stop=True)
                a_s1.by(ins)

            def turn_max(k, part):
                pe.wait_ge(a_mpt.sem, a_mpt.at(k, part))
                tr = bank[0:24, 7, 0:T // 2].bitcast(BF16)
                a_mtr.by(rows(lambda t: tr[:, t * P:(t + 1) * P], lambda t: flat(a_mp[:, part, t]), identb))

            def head_rows(k, g):
                pe.wait_ge(a_osb.sem, a_osb.at(k, g))
                if g == 0:
                    pe.wait_ge(a_mok.sem, a_mok.at(k, 1))
                else:
                    pe.wait_ge(a_norm.sem, a_norm.at(k, g - 1))
                a_otr.by(back(7, a_o))

            def mamba(j, u, k, p):
                x = xs(p)
                ready(j, u)
                for n in range(4):
                    n_in.by(product(bank[:, n, :], [win[c][:, n, :] for c in range(2)], x))
                for m in range(2):
                    pe.wait_ge(n_sil.sem, n_sil.at(k, 2 + m))
                    for b, c0, c1 in ((4, 0, 64), (5, 64, 160)):
                        ins = mm(bank[0:c1 - c0, b, :], wx[:, m, c0:c1], n_xc[:, m, :], start=m == 0, stop=m == 1)
                        if m == 1:
                            n_xdb.by(ins)
                pe.wait_ge(n_dtc.sem, n_dtc.at(k, 0))
                for m in range(2):
                    n_dtp.by(mm(bank[:, m, :], wdt[:, m, :], n_dtr[:], start=True, stop=True))
                pe.wait_ge(n_bcp.sem, n_bcp.at(k, 0))
                pe.wait_ge(n_poss.sem, n_poss.at(k, 0))
                pe.wait_ge(n_abss.sem, n_abss.at(k, 1))
                for n in range(NSTATE + 2):
                    if n < NSTATE:
                        if n >= 2:
                            pe.wait_ge(n_dbs.sem, n_dbs.at(k, 2 * n - 3))
                        n_br.by(mm(bank[:, 4 + n % 2, :], pick[:, n:n + 1].to_broadcast([96, P]), n_bc[:],
                                   start=True, stop=True))
                        if n >= 2:
                            pe.wait_ge(n_csc.sem, n_csc.at(k, n - 2))
                        n_cr.by(mm(bank[:, n % 2, :], pick[:, 16 + n:17 + n].to_broadcast([96, P]), n_bc[:],
                                   start=True, stop=True))
                    if n >= 2:
                        for m in range(2):
                            pe.wait_ge(n_hcs.sem, n_hcs.at(k, 2 * n - 4 + m))
                            n_ya.by(mm(bank[:, 2 + m, :], ident[:], n_hc[:, m, :], start=n == 2, stop=n == NSTATE + 1))
                    if n in PE_STAGES:
                        prologue(j, u + 1, PE_STAGES[n])
                pe.wait_ge(n_y.sem, n_y.at(k, 0))
                for t in range(NT):
                    for m in range(2):
                        ins = mm(bank[:, 6, t * P:(t + 1) * P], n_db[:, m, t * P:(t + 1) * P], wout[:, m, :],
                                 start=m == 0, stop=m == 1)
                n_o.by(ins)

            with pe.Fori(0, PAIRS) as j:
                for stage in PE_STAGES.values():
                    prologue(j, 0, stage)
                for u, (kind, p) in enumerate(UNITS):
                    {"ffn": ffn, "moe": moe, "mha": mha, "mamba": mamba}[kind](j, u, kth[u], p)
                    unit_end(pe, j, u)

        for signal in signals:
            signal.whole()


def constants():
    f, half = np.float32, P // 2
    pos = np.arange(T, dtype=f)
    freqs = (f(1.0) / f(10000.0) ** (np.arange(half, dtype=f) / f(half))).astype(f)
    angle = pos[:, None] * freqs[None, :]
    sin, cos = np.sin(angle).astype(f).T, np.cos(angle).astype(f).T
    rope = np.stack([np.concatenate([cos, cos]), np.concatenate([-sin, sin])], 1)
    eye = np.eye(P, dtype=f)
    later = np.arange(P)[None, :] > np.arange(P)[:, None]
    mask_qk = np.where(later, f(-1e9), f(0))
    mask_kq = np.where(later.T, f(-1e9), f(0))
    path = np.zeros((LEAVES, LEAVES), f)
    depth = LEAVES.bit_length() - 1
    path[LEAVES - 1] = -depth
    for leaf in range(LEAVES):
        node = leaf + LEAVES - 1
        while node:
            up = (node - 1) // 2
            path[up, leaf] = 1 if node == 2 * up + 2 else -1
            path[LEAVES - 1, leaf] += node == 2 * up + 1
            node = up
    tree = np.zeros((96, TREES, P), f)
    thr = np.full(P, -0.5, f)
    thr[0:32] = 0.5
    for t in range(TREES):
        tree[32 * t:32 * t + LEAVES, t, 0:LEAVES] = -path
        for c in range(1, 4):
            tree[32 * t:32 * t + LEAVES, t, 32 * c:32 * c + LEAVES] = path
    big = np.zeros((P, TREES * (M1 * P + P)), f)
    for t in range(TREES):
        for leaf in range(LEAVES):
            big[leaf, t * M1 * P + leaf * LEAF_W:t * M1 * P + (leaf + 1) * LEAF_W] = -2.0 ** 100
    pick = np.zeros((96, 32), f)
    for c in range(3):
        pick[32 * c:32 * c + 32] = np.eye(32, dtype=f)
    tri = np.broadcast_to(np.tril(np.ones((EXPERTS, EXPERTS), f), -1), (P, EXPERTS, EXPERTS))
    bf = np.dtype("bfloat16")

    def parts(v):
        got = []
        for _ in range(3):
            got.append(v.astype(bf).astype(f))
            v = v - got[-1]
        return got
    slopes = np.array([2.0 ** (-8.0 * (i + 1) / HEADS) for i in range(HEADS)], f)
    q_rows, k_rows = np.zeros((2, 16, HEADS, T), f)
    k_rows[0:3] = 1
    even = pos - pos % 2
    for n, part in enumerate(parts(slopes)):
        for c, v in enumerate((even, pos - even)):
            q_rows[3 + 2 * n + c] = part[:, None]
            k_rows[3 + 2 * n + c] = v[None, :]
    for n, part in enumerate(parts(-slopes[:, None] * pos[None, :])):
        q_rows[9 + n] = part
        k_rows[9 + n] = 1

    def by_parity(rows):
        return rows.reshape(16, HEADS // 2, 2, T).transpose(0, 2, 1, 3).astype(bf)
    return {"rope": rope, "ident": eye, "tri": tri,
            "cbf": np.stack([eye, mask_qk, mask_kq], 1).astype(bf), "tree": tree.astype(bf), "bias": big,
            "pick": pick.astype(bf), "q_rows": by_parity(q_rows), "k_rows": by_parity(k_rows)}, thr


def layouts(a):
    const, thr = constants()
    by_dim = np.arange(P).reshape(HEADS // 2, 2, DH).transpose(1, 2, 0).reshape(-1)
    f = np.float32

    def zeros(*shape):
        return np.zeros(shape, f)
    d = dict(const)
    d["rope"] = const["rope"][by_dim]
    d["x"] = a["L0_attn_x"].reshape(BATCHES, NT, P, P)
    fw1, fw2, bias = zeros(P, TREES, M1 * P), zeros(P, TREES, M1, P), const["bias"]
    rw, col = zeros(P, 96 + EXPERTS), zeros(P, 20)
    for t, n in enumerate("qkv"):
        fw1[:, t] = a[f"L0_ffn_{n}_w1"].transpose(1, 0, 2).reshape(P, -1)
        fw2[:, t] = a[f"L0_ffn_{n}_w2"].reshape(M1, P, P).transpose(1, 0, 2)
        rw[:, 32 * t:32 * t + LEAVES - 1] = a[f"L0_ffn_{n}_node_w"].T
        col[32 * t:32 * t + LEAVES - 1, 1] = a[f"L0_ffn_{n}_node_b"]
        for c in range(1, 4):
            for leaf in range(LEAVES):
                at = t * M1 * P + leaf * LEAF_W
                bias[32 * c + leaf, at:at + LEAF_W] = a[f"L0_ffn_{n}_b1"][leaf]
            at = TREES * M1 * P + t * P
            bias[32 * c:32 * c + LEAVES, at:at + P] = a[f"L0_ffn_{n}_b2"]
    rw[:, 96:] = a["L1_ffn_gate_w"].T
    mw = zeros(P, MLPS, 6, P)
    for e in range(MLPS):
        w1, w2, w3 = (a[f"L1_ffn_w{n}"][e] if e < EXPERTS else a[f"L1_ffn_sw{n}"] for n in (1, 2, 3))
        mw[:, e, 0:2] = w1.T.reshape(P, 2, P)
        mw[:, e, 2:4] = w3.T.reshape(P, 2, P)
        mw[:, e, 4:6] = w2.T.reshape(2, P, P).transpose(1, 0, 2)
    wq, wk, wv = (a[f"L0_attn_w{n}"].T for n in "qkv")
    d["aw"] = np.stack([wq[:, by_dim], np.roll(wq, P // 2, 1)[:, by_dim], wk[:, by_dim],
                        np.roll(wk, P // 2, 1)[:, by_dim], wv], 1)
    d["owT"] = a["L0_attn_out_w"].T
    d["out_b"] = np.broadcast_to(a["L0_attn_out_b"], (P, P))
    d["win"] = a["L1_attn_W_in"].reshape(P, 4, P)
    wx = a["L1_attn_W_x"].reshape(NHALF, P, 96).transpose(1, 0, 2)
    d["wx"] = np.concatenate([wx[:, :, 0:64]] + [wx[:, :, 64:96]] * 3, 2)
    d["wdt"] = a["L1_attn_W_dt"].reshape(64, NHALF, P)
    d["wout"] = a["L1_attn_W_out"].reshape(NHALF, P, P).transpose(1, 0, 2)
    d["a_log"] = a["L1_attn_A_log"].reshape(NHALF, P, NSTATE).transpose(1, 0, 2)
    col[:, 0], col[:, 2] = thr, a["L1_attn_norm_w"]
    col[:, 5:13] = a["L1_attn_conv_w"].reshape(NHALF, P, 4).transpose(1, 0, 2).reshape(P, 8)
    for at, name in ((13, "conv_b"), (15, "b_dt"), (17, "D")):
        col[:, at:at + 2] = a[f"L1_attn_{name}"].reshape(NHALF, P).T
    d["gate_b"] = np.broadcast_to(a["L1_ffn_gate_bias"], (P, EXPERTS))
    d.update(fw1=fw1.reshape(P, -1), fw2=fw2.reshape(P, -1), bias=bias, rw=rw, col=col, mw=mw.reshape(P, -1))
    d["aw"], d["win"] = d["aw"].reshape(P, -1), d["win"].reshape(P, -1)
    return d


def kernel(**inputs):
    import numpy as _np
    import concourse.bacc as _bacc
    from concourse import mybir as _mybir
    from concourse.bass_utils import run_bass_kernel_spmd as _run

    nc = _bacc.Bacc("TRN2", target_bir_lowering=False, num_devices=1)
    arrays, args = {}, {}
    for name, a in layouts({n: _np.asarray(v) for n, v in inputs.items()}).items():
        a = _np.ascontiguousarray(a)
        arrays[f"in_{name}_dram"] = a
        args[name] = nc.dram_tensor(f"in_{name}_dram", a.shape, _mybir.dt.from_np(a.dtype), kind="ExternalInput").ap()
    out = nc.dram_tensor("out_dram", (BATCHES, NT, P, P), F32, kind="ExternalOutput").ap()
    program(nc, args, out)
    r = _run(nc, [arrays], core_ids=[0])
    return r.results[0]["out_dram"].reshape(BATCHES, T, P)
```

```python
from contextlib import ExitStack

import numpy as np
import concourse.bass as bass
from concourse import mybir

F32 = mybir.dt.float32
F32R = mybir.dt.float32r
BF16 = mybir.dt.bfloat16
ALU = mybir.AluOpType
ACT = mybir.ActivationFunctionType
AX_X = mybir.AxisListType.X

P = 128
T = 512
NT = T // P
BATCHES = 4
PAIRS = BATCHES // 2
LEAVES, LEAF_W, TREES = 16, 64, 3
M1 = LEAVES * LEAF_W // P
STEPS = TREES * M1
EXPERTS, MLPS = 8, 9
MSTEPS = MLPS * 2
HEADS, DH, SLOTS = 16, 8, 6
NSTATE, NHALF = 16, 2
EPS = 1e-5
LEAF_SCALE = float(np.float32(1.0) / np.sqrt(P).astype(np.float32))
HEAD_SCALE = float(1.0 / np.sqrt(np.float32(DH)))

LAYERS = ["ffn", "mha", "ffn", "moe", "mamba", "moe"]
UNITS = [(kind, batch) for kind in LAYERS for batch in range(2)]
COUNT = {kind: sum(1 for u in UNITS if u[0] == kind) for kind in LAYERS}
COUNT["unit"], COUNT["pair"] = len(UNITS), 1
PART_RUNS = [(0, 3, 0), (3, 2, 1), (5, 1, 2)]
QUADS = HEADS // 4
SLOTS_4 = [(0, 0, 4)] + [(qt, h, n) for qt, n in ((1, 2), (2, 1), (3, 1)) for h in range(0, 4, n)]
NS1 = len(SLOTS_4)
STEPS_4 = 2 * NT
NS2 = QUADS * STEPS_4


def heads_plan():
    early, rate = NS1 + 11, 1.5
    jobs = [("slot", n) for n in range(QUADS * NS1)]
    for quad in range(QUADS):
        jobs.insert((quad + 1) * NS1 + quad + 2, ("turn", quad))
    plan = {-1: jobs[:early]}
    for step in range(NS2):
        at = [int(early + rate * (step + n)) for n in range(2)]
        plan[step] = jobs[at[0]:at[1]]
        if step % STEPS_4 == 5 and step > STEPS_4:
            plan[step].append(("rows", step // STEPS_4 - 1))
    plan[NS2] = [("rows", QUADS - 1)]
    return plan


HEADS_PLAN = heads_plan()
RING_OF_4 = len(HEADS_PLAN[-1]) - 8
HEADS_JOBS = [job for step in sorted(HEADS_PLAN) for job in HEADS_PLAN[step]]
DVE_STAGES = {0: "stats", 2: "rows", 4: "rms", 6: "low", 8: "first", 10: "second", 12: "third",
              14: "fourth", 15: "ranks", 16: "combine", 17: "row"}
POOL_STAGES = {0: "guess", 3: "rms", 8: "exp 0", 9: "exp 1", 10: "exp 2", 11: "exp 3"}
ACT_STAGES = {5: "high", 8: "exp 0"}
PE_STAGES = {4: "turn", 7: "first", 9: "second", 11: "third", 13: "fourth", 18: "weights"}
HEAD_DVE_STAGES = {0: "stats", 2: "rows", 6: "low", 7: "first", 9: "second", 10: "third", 11: "fourth", 12: "k first",
                   14: "k second", 15: "k rest", 16: "k last"}
HEAD_ACT_STAGES = {5: "high", 10: "q 0", 11: "q 1", 12: "q 2", 15: "k 0", 16: "k 1", 17: "k 2"}
HEAD_PE_STAGES = {4: "turn", 7: "first", 9: "second", 12: "k first", 14: "k second"}
FFN_LAG = 7
SPLIT_AT = (0, list(range(8, 24, 2))[:EXPERTS])
MOE_LAG = 2
ATTEND_AT = {0: [("values", 0)], 1: [("score", 2), ("turn", 1)], 3: [("turn", 2), ("score", 3)],
             5: [("weigh", 0), ("weigh", 1), ("weigh", 2), ("turn", 3)], 7: [("weigh", 3)]}
EXPS = [f"exp {t}" for t in range(NT)]
HEAD_PARTS = [f"{side} {c}" for side in "qk" for c in range(3)]
HEAD_ROTATIONS = ["first", "second", "k first", "k second"]
HEAD_RESIDUALS = ["third", "fourth", "k rest", "k last"]
HEAD_LAG = 11


def stage_at(table, i, kind):
    late = ("turn", "high", "low")
    if kind == "mha" and table is not POOL_STAGES:
        for own, ahead in ((DVE_STAGES, HEAD_DVE_STAGES), (ACT_STAGES, HEAD_ACT_STAGES), (PE_STAGES, HEAD_PE_STAGES)):
            if table is own:
                return ahead.get(i)
    if kind == "mamba":
        kept = late + ("stats", "rows", "rms", "guess")
        table = {n + 2 * (name in late): name for n, name in table.items() if name in kept}
    return table.get(i)


MAX_ROW = SLOTS * DH


class Signal:

    def __init__(self, sem, kind, per, step=1):
        self.sem, self.kind, self.per, self.step = sem, kind, per, step
        self.made = 0

    def by(self, instruction):
        self.made += 1
        instruction.then_inc(self.sem, self.step)

    def at(self, k, i):
        assert 0 <= k * self.per + i and i < self.per and k < COUNT[self.kind]
        return (k * self.per + i + 1) * self.step

    def whole(self):
        assert self.made == self.per * COUNT[self.kind], (self.made, self.per, self.kind)


def program(nc, A, out):
    with ExitStack() as ctx:
        def sb(name, shape, dt=F32, stack=ctx):
            return stack.enter_context(nc.sbuf_tensor(name, shape, dt))

        def sem(name):
            return ctx.enter_context(nc.semaphore(name))

        bank = ctx.enter_context(nc.psum_tensor("bank", [P, 8, T], F32))

        fw1 = [sb(f"fw1_{s}", [P, TREES, M1 * P], F32R) for s in "hl"]
        fw2 = [sb(f"fw2_{s}", [P, TREES, M1, P], F32R) for s in "hl"]
        mw = [sb(f"mw_{s}", [P, MLPS, 6, P], F32R) for s in "hl"]
        aw = [sb(f"aw_{s}", [P, 5, P], F32R) for s in "hl"]
        win = [sb(f"win_{s}", [P, 4, P], F32R) for s in "hl"]
        rw = [sb(f"rw_{s}", [P, 96 + EXPERTS], F32R) for s in "hl"]
        biasw = sb("biasw", [P, TREES * (M1 * P + P)], BF16)
        b1w = biasw[:, 0:TREES * M1 * P].rearrange("p (t n) -> p t n", t=TREES)
        b2w = biasw[:, TREES * M1 * P:].rearrange("p (t n) -> p t n", t=TREES)
        owT = sb("owT", [P, P])
        out_b = sb("out_b", [P, P])
        half = sb("half", [P, NT, EXPERTS])
        euler = sb("euler", [P, NT, EXPERTS])
        wx = sb("wx", [P, NHALF, 96])
        wdt = sb("wdt", [64, NHALF, P])
        wout = sb("wout", [P, NHALF, P])
        taps = sb("taps", [P, 4, P])
        col = sb("col", [P, 20])
        leaf_thr, node_b, norm_w = (col[:, i:i + 1] for i in range(3))
        conv_w = col[:, 5:13].rearrange("p (m c) -> p m c", m=NHALF)
        conv_b, b_dt, d_skip = col[:, 13:15], col[:, 15:17], col[:, 17:19]
        amat = sb("amat", [P, NHALF, NSTATE])
        gate_b = sb("gate_b", [P, EXPERTS])
        tri = sb("tri", [P, EXPERTS, EXPERTS])
        ident = sb("ident", [P, P])
        cbf = sb("cbf", [P, 3, P], BF16)
        identb, mask_qk, mask_kq = cbf[:, 0, :], cbf[:, 1, :], cbf[:, 2, :]
        tree = sb("tree", [96, TREES, P], BF16)
        pick = sb("pick", [96, 32], BF16)

        X = sb("X", [P, 2, NT, P])
        xn = sb("xn", [P, 2, NT, P])
        xT = [sb(f"xT_{s}", [P, 2, T], F32R) for s in "hl"]
        R = sb("R", [P, 2, TREES, T], BF16)
        xm = [R[:, p, 0:2, :].rearrange("p a t -> p (a t)").bitcast(F32).rearrange("p (t d) -> p t d", t=NT)
              for p in range(2)]
        cmp = [R[:, p, 1:3, :].rearrange("p a t -> p (a t)").bitcast(F32)
               .rearrange("p (c t a b) -> p c t a b", c=2, t=NT, a=EXPERTS) for p in range(2)]
        dbit = sb("dbit", [96, T], BF16)
        st = sb("st", [P, NT, 6])
        mv = sb("mv", [P, NT, 2])
        small = sb("small", [P, 8, NT])
        preload, y0, ve, y2, rstd, gmax, gsum, grec = (small[:, i, :] for i in range(8))
        gbuf = sb("gbuf", [P, 8, NT, EXPERTS])
        glog, gexp, gsc, gbi, grank, gcmb, gr1, gr2 = (gbuf[:, i] for i in range(8))
        cparts = sb("cparts", [P, NT, 96], BF16)

        s = ExitStack()
        stage_fw1 = sb("stage_fw1", [P, TREES, M1 * P], F32, s)
        stage_fw2 = sb("stage_fw2", [P, TREES, M1, P], F32, s)
        stage_b = sb("stage_b", [P, TREES * (M1 * P + P)], F32, s)
        rest_b = sb("rest_b", [P, TREES * (M1 * P + P)], F32, s)
        stage_m8 = sb("stage_m8", [P, 6 * P], F32, s)
        s.close()
        spare = R[:].rearrange("p a b t -> p (a b t)").bitcast(F32)
        stage_aw, stage_win, stage_rw = spare[:, 0:640], spare[:, 640:1152], spare[:, 1152:1152 + 96 + EXPERTS]
        mwf = [mw[c][:].rearrange("p e n d -> p (e n d)") for c in range(2)]
        ROUTED = EXPERTS * 6 * P
        splits = [("fw1_in", [fw1[c][:].rearrange("p t n -> p (t n)") for c in range(2)],
                   stage_fw1[:].rearrange("p t n -> p (t n)")),
                  ("fw2_in", [fw2[c][:].rearrange("p t m d -> p (t m d)") for c in range(2)],
                   stage_fw2[:].rearrange("p t m d -> p (t m d)")),
                  ("small_in", [aw[c][:].rearrange("p n d -> p (n d)") for c in range(2)], stage_aw),
                  ("small_in", [win[c][:].rearrange("p n d -> p (n d)") for c in range(2)], stage_win),
                  ("small_in", [rw[c][:] for c in range(2)], stage_rw),
                  ("small_in", [mwf[c][:, ROUTED:] for c in range(2)], stage_m8[:])]

        s = ExitStack()
        f_h = [sb(f"f_h{c}", [P, 4, T], F32R, s) for c in "hl"]
        f_q = [sb(f"f_q{c}", [P, T], F32R, s) for c in "hl"]
        f_k = [sb(f"f_k{c}", [P, T], F32R, s) for c in "hl"]
        f_vT = sb("f_vT", [P, T], F32, s)
        f_v = sb("f_v", [P, NT, P], F32, s)
        f_p = sb("f_p", [P, 2, T], F32, s)
        f_pT = sb("f_pT", [P, NT, T], F32, s)
        f_s = sb("f_s", [P, 5, NT], F32, s)
        w_stage = sb("w_stage", [P, 2, 6 * P], F32, s)
        s.close()

        s = ExitStack()
        m_sl = sb("m_sl", [P, 2, T], F32, s)
        m_t = sb("m_t", [P, 2, T], F32, s)
        m_h = sb("m_h", [P, 3, T], F32, s)
        m_hh = [sb(f"m_hh{c}", [P, 3, T], F32R, s) for c in "hl"]
        m_yT = sb("m_yT", [P, T], F32, s)
        s.close()

        s = ExitStack()
        a_q = sb("a_q", [P, HEADS // 2, T], BF16, s)
        a_k = sb("a_k", [P, HEADS, T], BF16, s)
        a_v = sb("a_v", [P, NT, HEADS, 32], F32, s)
        a_p = sb("a_p", [P, 4, 2, T], F32, s)
        rope = sb("rope", [P, 2, T], F32, s)
        a_o = sb("a_o", [P, T], F32, s)
        a_mx = sb("a_mx", [P, QUADS, NT, 4], F32, s)
        a_mr = sb("a_mr", [P, NT, 4], F32, s)
        a_mp = sb("a_mp", [P, QUADS, NT, 3, 4], BF16, s)
        a_rec = sb("a_rec", [P, NT, 4], F32, s)
        s.close()
        a_parts = R[:, 0]
        a_rows = R[:, 1, 0:2].rearrange("p a t -> p (a t)").bitcast(F32).rearrange("p (t f) -> p t f", t=NT)
        a_mT = R[0:12, 1, 2]

        def a_rot(p):
            return [xn[:, b].rearrange("p t d -> p (t d)") for b in (p, 1 - p)]

        s = ExitStack()
        n_xp = sb("n_xp", [P, NHALF, T + 4], F32, s)
        n_xc = sb("n_xc", [P, NHALF, T], F32, s)
        n_sz = sb("n_sz", [P, NHALF, T], F32, s)
        n_dtr = sb("n_dtr", [64, T], F32, s)
        n_dt = sb("n_dt", [P, NHALF, T], F32, s)
        n_dtx = sb("n_dtx", [P, NHALF, T], F32, s)
        n_da = sb("n_da", [P, NHALF, T], F32, s)
        n_db = sb("n_db", [P, NHALF, T], F32, s)
        n_h = sb("n_h", [P, NHALF, T], F32, s)
        n_hc = sb("n_hc", [P, NHALF, T], F32, s)
        n_cs = sb("n_cs", [P, 2, T], F32, s)
        n_bc = sb("n_bc", [96, T], BF16, s)
        n_r = sb("n_r", [96, T], F32, s)
        n_mid = sb("n_mid", [96, T], BF16, s)
        s.close()
        n_cv = n_cor = n_hc
        n_abs, n_u, n_ln, n_low, n_pos = n_db, n_h, n_da, n_cs, n_dtx

        stack_dram = nc.dram_tensor("stack_dram", [2, 2, P // 2, HEADS // 2, T], BF16, kind="Internal").ap()
        max_dram = nc.dram_tensor("max_dram", [QUADS, 12, T], BF16, kind="Internal").ap()

        signals = []

        def sig(name, kind, per, step=1):
            signals.append(Signal(sem(name), kind, per, step))
            return signals[-1]

        arrived = {name: sem(name) for name in ("fw1_in", "bias_in", "fw2_in", "small_in")}
        taps_done = sem("taps_done")
        rows_in = sem("rows_in")
        split_done = sem("split_done")
        setup_done = sem("setup_done")
        x_first = sem("x_first")
        x_last = sem("x_last")
        pair_done = sem("pair_done")
        low_done = sem("low_done")
        bias_act = sem("bias_act")
        bias_dve = sem("bias_dve")
        amat_done = sem("amat_done")
        unit_done = sem("unit_done")
        x_in = sem("x_in")
        x_out = sem("x_out")
        x_next = sem("x_next")
        dve_step = sem("dve_step")

        g_var = sig("g_var", "unit", 1)
        g_rsq = sig("g_rsq", "unit", 1)
        r_var = sig("r_var", "mamba", 1)
        r_rsq = sig("r_rsq", "mamba", 1)
        g_xn = sig("g_xn", "unit", 1)
        g_tr = sig("g_tr", "unit", 1)
        g_xh = sig("g_xh", "unit", 1)
        g_xl = sig("g_xl", "unit", 1)
        t_sc = sig("t_sc", "ffn", 1)
        t_bit = sig("t_bit", "ffn", 1)
        t_cnt = sig("t_cnt", "ffn", TREES)
        t_sel = sig("t_sel", "ffn", TREES)
        e_log = sig("e_log", "moe", 1)
        e_sub = sig("e_sub", "moe", 1)
        e_exp = sig("e_exp", "moe", NT)
        e_prt = sig("e_prt", "moe", 1)
        e_tr = sig("e_tr", "moe", 1)
        e_row = sig("e_row", "moe", 1)
        f_s1 = sig("f_s1", "ffn", STEPS)
        f_hi = sig("f_hi", "ffn", STEPS)
        f_lo = sig("f_lo", "ffn", STEPS)
        f_s2 = sig("f_s2", "ffn", STEPS)
        f_evh = sig("f_evh", "ffn", TREES)
        f_evl = sig("f_evl", "ffn", 2)
        f_vtr = sig("f_vtr", "ffn", 1)
        f_vok = sig("f_vok", "ffn", 1)
        f_sco = sig("f_sco", "ffn", NT)
        f_max = sig("f_max", "ffn", NT)
        f_prob = sig("f_prob", "ffn", NT)
        f_ptr = sig("f_ptr", "ffn", NT)
        f_pok = sig("f_pok", "ffn", NT)
        f_pv = sig("f_pv", "ffn", NT)
        w_in = [sig(f"w_in_{n}", "pair", EXPERTS // 2, 16) for n in range(2)]
        w_hi = sig("w_hi", "pair", EXPERTS)
        w_lo = sig("w_lo", "pair", EXPERTS)
        m_a = sig("m_a", "moe", MSTEPS)
        m_b = sig("m_b", "moe", MSTEPS)
        m_cr = sig("m_cr", "moe", EXPERTS)
        m_silu = sig("m_silu", "moe", MSTEPS)
        m_ts = sig("m_ts", "moe", 2 * EXPERTS)
        m_hs = sig("m_hs", "moe", MSTEPS)
        m_hi = sig("m_hi", "moe", MSTEPS)
        m_lo = sig("m_lo", "moe", MSTEPS)
        m_s2 = sig("m_s2", "moe", MSTEPS)
        m_y = sig("m_y", "moe", 1)
        m_ytr = sig("m_ytr", "moe", 1)
        m_res = sig("m_res", "moe", 1)
        a_proj = sig("a_proj", "mha", 4)
        a_took = sig("a_took", "mha", 4)
        a_vpr = sig("a_vpr", "mha", 1)
        a_rotd = sig("a_rotd", "mha", 2)
        a_prt = sig("a_prt", "mha", 6)
        a_res = sig("a_res", "mha", 4)
        a_fill = sig("a_fill", "pair", 3)
        a_vok = sig("a_vok", "mha", 1)
        a_wr = sig("a_wr", "mha", 12, 16)
        a_ldq = [sig(f"a_ldq_{n}", "mha", 1, 16) for n in range(2)]
        a_ldk = [sig(f"a_ldk_{n}", "mha", 2, 16) for n in range(2)]
        a_rld = sig("a_rld", "pair", 1, 16)
        a_s1 = sig("a_s1", "mha", QUADS * NS1)
        a_m1 = sig("a_m1", "mha", QUADS * NS1)
        a_mpt = sig("a_mpt", "mha", QUADS)
        a_mtr = sig("a_mtr", "mha", QUADS)
        a_mok = sig("a_mok", "mha", QUADS)
        a_mwr = sig("a_mwr", "mha", QUADS, 16)
        a_mld = [sig(f"a_mld_{n}", "mha", 2, 16) for n in range(QUADS)]
        a_s2 = sig("a_s2", "mha", NS2)
        a_e2 = sig("a_e2", "mha", NS2)
        a_pv = sig("a_pv", "mha", 4 * NT)
        a_osb = sig("a_osb", "mha", 4)
        a_otr = sig("a_otr", "mha", 4)
        a_norm = sig("a_norm", "mha", 4)
        a_ctr = sig("a_ctr", "mha", 1)
        a_cok = sig("a_cok", "mha", 1)
        a_out = sig("a_out", "mha", 1)
        n_in = sig("n_in", "mamba", 4)
        n_fill = sig("n_fill", "mamba", 1)
        n_xps = sig("n_xps", "mamba", 2)
        n_cvs = sig("n_cvs", "mamba", 1)
        n_cvp = sig("n_cvp", "mamba", 1)
        n_sil = sig("n_sil", "mamba", 4)
        n_xdb = sig("n_xdb", "mamba", 1)
        n_dtc = sig("n_dtc", "mamba", 1)
        n_bc1 = sig("n_bc1", "mamba", 1)
        n_bcp = sig("n_bcp", "mamba", 1)
        n_mids = sig("n_mids", "mamba", 1)
        n_bcm = sig("n_bcm", "mamba", 1)
        n_dtp = sig("n_dtp", "mamba", 2)
        n_abss = sig("n_abss", "mamba", 2)
        n_us = sig("n_us", "mamba", 1)
        n_lns = sig("n_lns", "mamba", 1)
        n_a1 = sig("n_a1", "mamba", 1)
        n_lows = sig("n_lows", "mamba", 1)
        n_poss = sig("n_poss", "mamba", 2)
        n_dts = sig("n_dts", "mamba", 1)
        n_dtxs = sig("n_dtxs", "mamba", 1)
        n_br = sig("n_br", "mamba", NSTATE)
        n_cr = sig("n_cr", "mamba", NSTATE)
        n_das = sig("n_das", "mamba", 2 * NSTATE)
        n_csc = sig("n_csc", "mamba", NSTATE)
        n_dbs = sig("n_dbs", "mamba", 2 * NSTATE)
        n_scan = sig("n_scan", "mamba", 2 * NSTATE)
        n_hcs = sig("n_hcs", "mamba", 2 * NSTATE)
        n_ya = sig("n_ya", "mamba", 2 * NSTATE)
        n_y = sig("n_y", "mamba", 2)
        n_o = sig("n_o", "mamba", 1)

        kth = [sum(1 for v in UNITS[:u] if v[0] == UNITS[u][0]) for u in range(len(UNITS))]
        NU = len(UNITS)

        def runs_on(u):
            return UNITS[u] in (("ffn", 0), ("moe", 0))

        def done_before(u):
            return 4 * sum(not runs_on(v) for v in range(u))

        def unit_end(eng, j, u):
            if runs_on(u):
                return
            eng.drain().then_inc(unit_done, 1)
            if u < NU - 1:
                eng.wait_ge(unit_done, done_before(u + 1))
            else:
                eng.wait_ge(pair_done, j + 1)

        def job_bank(i):
            return (4, 5, 2, 3)[i % 4] if i < RING_OF_4 else 4 + i % 2

        def flat(ap):
            return ap.rearrange("p a b -> p (a b)")

        numbers = [x.num for x in (unit_done, x_in, x_out, x_next, dve_step)] + [x.sem.num for x in signals]
        assert numbers == list(range(unit_done.num, unit_done.num + len(numbers)))
        block = ctx.enter_context(nc.Block())

        NSMALL = 17

        @block.sync
        def _(sp):
            def load(dst, name, signal, part=slice(None)):
                sp.dma_start(dst, A[name][:, part] if name == "mw" else A[name]).then_inc(arrived[signal], 16)

            load(splits[0][2], "fw1", "fw1_in")
            load(stage_b[:], "bias", "bias_in")
            load(splits[1][2], "fw2", "fw2_in")
            small = [(stage_aw, "aw"), (stage_win, "win"), (stage_rw, "rw")] + \
                    [(t[:], name) for t, name in ((owT, "owT"), (wx, "wx"), (wdt, "wdt"), (wout, "wout"), (col, "col"),
                                                  (amat, "a_log"), (gate_b, "gate_b"), (tri, "tri"), (ident, "ident"),
                                                  (out_b, "out_b"), (cbf, "cbf"), (tree, "tree"), (pick, "pick"))]
            assert len(small) + 1 == NSMALL
            for dst, name in small:
                load(dst, name, "small_in")
            load(stage_m8[:], "mw", "small_in", slice(ROUTED, None))
            sp.dma_start(X[:, 0], A["x"][0].rearrange("t p d -> p t d")).then_inc(x_first, 16)
            for side, name in enumerate(("q_rows", "k_rows")):
                for odd in range(2):
                    sp.dma_start(stack_dram[side, odd, MAX_ROW:], A[name][:, odd]).then_inc(rows_in, 16)
            sp.wait_ge(rows_in, 64)
            with sp.Fori(0, PAIRS) as j:
                sp.dma_start(X[:, 1], A["x"][bass.ds(j * 2 + 1, 1)].rearrange("o t p d -> p (o t) d")).then_inc(x_in, 16)
                sp.wait_ge(setup_done, 3)
                for e in range(EXPERTS):
                    if e >= 2:
                        sp.wait_ge(w_lo.sem, w_lo.at(0, e - 2))
                    w_in[e % 2].by(sp.dma_start(w_stage[:, e % 2], A["mw"][:, e * 6 * P:(e + 1) * 6 * P]))
                for u, (kind, p) in enumerate(UNITS):
                    k = kth[u]
                    if kind == "mha":
                        if k % 2 == 0:
                            sp.wait_ge(unit_done, done_before(u))
                        else:
                            sp.wait_ge(a_s2.sem, a_s2.at(k - 1, NS2 - 1))
                        sp.wait_ge(a_wr.sem, a_wr.at(k, 11))
                        for n in range(2):
                            pairs = slice(4 * n, 4 * n + 4)
                            a_ldq[n].by(sp.dma_start(a_q[:, pairs], stack_dram[0].rearrange("o r h t -> (o r) h t")[:, pairs]))
                            for odd in range(2):
                                a_ldk[n].by(sp.dma_start(a_k[64 * odd:64 * odd + 64, 8 * n + odd:8 * n + 8:2],
                                                         stack_dram[1, odd][:, pairs]))
                        for quad in range(QUADS):
                            sp.wait_ge(a_mok.sem, a_mok.at(k, quad))
                            a_mwr.by(sp.dma_start(max_dram[quad], a_mT))
                            sp.wait_ge(a_mwr.sem, a_mwr.at(k, quad))
                            for odd in range(2):
                                r = 64 * odd + MAX_ROW
                                a_mld[quad].by(sp.dma_start(a_q[r:r + 3, 2 * quad:2 * quad + 2],
                                                      max_dram[quad].rearrange("(c h o) t -> o c h t", c=3, o=2)[odd]))
                    if u + 1 < NU and UNITS[u + 1][0] == "mha":
                        k = kth[u + 1]
                        if k == 0:
                            sp.wait_ge(setup_done, 3)
                            a_rld.by(sp.dma_start(rope[:], A["rope"]))
                        for side in range(2):
                            sp.wait_ge(a_prt.sem, a_prt.at(k, 3 * side + 2))
                            for slot, n, part in PART_RUNS:
                                for odd in range(2):
                                    src = a_parts[64 * odd:64 * odd + 64]
                                    src = src[:, part:part + 1].to_broadcast([64, n, T]) if side == 0 else src[:, 0:n]
                                    dst = stack_dram[side, odd, DH * slot:DH * (slot + n)]
                                    a_wr.by(sp.dma_start(dst.rearrange("(c d) h t -> (d h) c t", c=n), src))
                    if u == NU - 1:
                        sp.wait_ge(m_res.sem, m_res.at(k - 1, 0))
                        sp.dma_start(out[bass.ds(j * 2, 1)].rearrange("o t p d -> p (o t) d"), X[:, 0]).then_inc(x_out, 16)
                        sp.wait_ge(x_out, 16)
                        sp.dma_start(X[:, 0], A["x"][bass.ds(j * 2 + 2, 1)].rearrange("o t p d -> p (o t) d")) \
                            .then_inc(x_next, 16)
                sp.wait_ge(unit_done, done_before(NU))
                sp.dma_start(out[bass.ds(j * 2 + 1, 1)].rearrange("o t p d -> p (o t) d"), X[:, 1]).then_inc(x_last, 16)
                sp.wait_ge(x_next, 16)
                sp.sem_clear(range(numbers[0], numbers[-1] + 1))
                sp.sem_inc(pair_done, 1)
                sp.wait_ge(x_last, 16)
                sp.sem_clear(range(x_last.num, x_last.num + 1))

        @block.gpsimd
        def _(pool):
            pool.memset(half[:], -0.5)
            pool.memset(euler[:], float(np.exp(np.float32(1.0))))
            pool.memset(cparts[:], 0.0)
            pool.wait_ge(arrived["small_in"], 16 * NSMALL)
            for c in range(4):
                nc.gpsimd.tensor_scalar(taps[:, c, :], ident[:], conv_w[:, 1, c:c + 1], None, ALU.mult) \
                    .then_inc(taps_done, 1)
                pool.wait_ge(taps_done, c + 1)
            pool.drain().then_inc(setup_done, 1)
            pool.wait_ge(setup_done, 3)

            def prologue(u, stage):
                if u == NU:
                    return
                kind, p = UNITS[u]
                k = kth[u]
                if stage == "guess":
                    pool.wait_ge(g_var.sem, g_var.at(u, 0))
                    g_rsq.by(nc.gpsimd.tensor_tensor(y0, ve, half[:, :, 0], ALU.pow))
                if stage == "rms" and kind == "mamba":
                    pool.wait_ge(r_var.sem, r_var.at(k, 0))
                    r_rsq.by(nc.gpsimd.tensor_tensor(y0, ve, half[:, :, 0], ALU.pow))
                if stage in EXPS and kind == "moe" and UNITS[u - 1][0] == "moe":
                    t = EXPS.index(stage)
                    pool.wait_ge(e_sub.sem, e_sub.at(k, 0))
                    e_exp.by(nc.gpsimd.tensor_tensor(gexp[:, t], euler[:, t], glog[:, t], ALU.pow))

            def hand_over(u, i):
                if u + 1 < NU:
                    prologue(u + 1, stage_at(POOL_STAGES, i, UNITS[u + 1][0]))

            with pool.Fori(0, PAIRS) as j:
                prologue(0, "guess")
                for u, (kind, p) in enumerate(UNITS):
                    k = kth[u]
                    if kind == "ffn":
                        prologue(u + 1, "guess")
                    if kind == "moe":
                        for i in range(MSTEPS):
                            pool.wait_ge(m_hi.sem, m_hi.at(k, i))
                            m_lo.by(nc.gpsimd.tensor_tensor(m_hh[1][:, i % 3, :], m_h[:, i % 3, :],
                                                            m_hh[0][:, i % 3, :].bitcast(F32), ALU.subtract))
                            hand_over(u, i - MOE_LAG * p)
                    if kind == "mha":
                        if k % 2 == 0:
                            for odd in (1, 0):
                                other = a_k[64 * (1 - odd):64 * (1 - odd) + 64, odd::2]
                                a_fill.by(nc.gpsimd.memset(other.bitcast(F32), 0.0))
                                pool.wait_ge(a_fill.sem, a_fill.at(0, 1 - odd))
                        prologue(u + 1, "guess")
                        if k % 2 == 0:
                            a_fill.by(nc.gpsimd.memset(a_v[:, :, :, DH:32], 1.0))
                    if kind == "mamba":
                        n_fill.by(nc.gpsimd.memset(n_xp[:, :, 0:3], 0.0))
                        pool.wait_ge(n_mids.sem, n_mids.at(k, 0))
                        n_bcm.by(nc.gpsimd.tensor_copy(n_bc[32:64], n_mid[64:96]))
                        pool.wait_ge(n_bcm.sem, n_bcm.at(k, 0))
                        pool.wait_ge(n_us.sem, n_us.at(k, 0))
                        n_a1.by(nc.gpsimd.tensor_scalar(n_low[:], n_u[:], -0.5, 1.0, ALU.mult, ALU.add))
                        pool.wait_ge(n_a1.sem, n_a1.at(k, 0))
                        n_lows.by(nc.gpsimd.tensor_tensor(n_low[:], n_low[:], n_u[:], ALU.mult))
                        for n in range(2 * NSTATE):
                            m = n % 2
                            pool.wait_ge(n_scan.sem, n_scan.at(k, n))
                            pool.wait_ge(n_csc.sem, n_csc.at(k, n // 2))
                            if n >= 2:
                                pool.wait_ge(n_ya.sem, n_ya.at(k, n - 2))
                            n_hcs.by(nc.gpsimd.tensor_tensor(n_hc[:, m, :], n_h[:, m, :], n_cs[:, n // 2 % 2, :],
                                                             ALU.mult))
                            if m == 1:
                                hand_over(u, n // 2)
                    unit_end(pool, j, u)

        @block.scalar
        def _(act):
            def arrival(signal):
                act.wait_ge(arrived[signal], 16 * (NSMALL if signal == "small_in" else 1))

            def bias_part(first, src):
                bias_rows = biasw[first:P]
                nc.scalar.activation(bias_rows, src[first:P], ACT.Copy).then_inc(bias_act, 1)

            for n, (signal, dst, src) in enumerate(splits):
                arrival(signal)
                nc.scalar.activation(dst[0], src, ACT.Copy).then_inc(split_done, 1)
                if n == 0:
                    arrival("bias_in")
                    bias_part(0, stage_b)
                if n == 1:
                    act.wait_ge(bias_dve, 1)
                    bias_part(64, rest_b)
                if n == 5:
                    act.wait_ge(bias_dve, 2)
                    bias_part(96, rest_b)
                    nc.scalar.activation(amat[:], amat[:], ACT.Exp).then_inc(amat_done, 1)
                    act.wait_ge(amat_done, 1)
                    nc.scalar.mul(amat[:], amat[:], -1.0).then_inc(amat_done, 1)
            act.wait_ge(split_done, len(splits))
            act.wait_ge(amat_done, 2)
            act.wait_ge(bias_act, 3)
            act.drain().then_inc(setup_done, 1)
            act.wait_ge(setup_done, 3)

            def prologue(j, u, stage):
                if u == NU:
                    return
                kind, p = UNITS[u]
                k = kth[u]
                if stage == "high":
                    act.wait_ge(g_tr.sem, g_tr.at(u, 0))
                    g_xh.by(act.activation(xT[0][:, p, :], bank[:, 7, :], ACT.Copy,
                                           scale=norm_w if kind == "mamba" else 1.0))
                if stage == "exp 0" and kind == "moe" and UNITS[u - 1][0] != "moe":
                    act.wait_ge(e_sub.sem, e_sub.at(k, 0))
                    for t in range(NT):
                        e_exp.by(act.activation(gexp[:, t], glog[:, t], ACT.Exp))
                if stage in HEAD_PARTS and kind == "mha":
                    side, c = divmod(HEAD_PARTS.index(stage), 3)
                    if c == 0:
                        act.wait_ge(a_rotd.sem, a_rotd.at(k, side))
                    else:
                        act.wait_ge(a_res.sem, a_res.at(k, 2 * side + c - 1))
                    if side == 1 and c == 0:
                        act.wait_ge(a_wr.sem, a_wr.at(k, 5))
                    a_prt.by(act.activation(a_parts[:, c, :], a_rot(p)[0], ACT.Copy))

            def ffn(j, u, k):
                p = UNITS[u][1]
                for i in range(STEPS + 1):
                    if i < STEPS:
                        act.wait_ge(f_s1.sem, f_s1.at(k, i))
                        if i >= 4 or p == 1:
                            act.wait_ge(f_s2.sem, f_s2.at(k, i - 4))
                        f_hi.by(act.activation(f_h[0][:, i % 4, :], bank[:, i % 3, :], ACT.Relu))
                    if k == SPLIT_AT[0] and i in SPLIT_AT[1]:
                        e = SPLIT_AT[1].index(i)
                        act.wait_ge(w_in[e % 2].sem, w_in[e % 2].at(0, e // 2))
                        w_hi.by(act.activation(mwf[0][:, e * 6 * P:(e + 1) * 6 * P], w_stage[:, e % 2], ACT.Copy))
                    hand_over(j, u, i - FFN_LAG * p)
                    if p == 1:
                        if i in (2, 4):
                            copy_pT(j, k - 1, i // 2)
                            probs(j, k - 1, i // 2 + 1)
                        if i == 6:
                            copy_pT(j, k - 1, 3)
                    if i in (11, 19):
                        t = (11, 19).index(i)
                        act.wait_ge(f_s2.sem, f_s2.at(k, M1 * t + M1 - 1))
                        f_evh.by(act.activation((f_q, f_k)[t][0][:], bank[:, 3 + t, :], ACT.Copy))
                    if i in (21, 23):
                        probs(j, k, (i - 21) // 2)
                    if i == 23:
                        copy_pT(j, k, 0)
                act.wait_ge(f_s2.sem, f_s2.at(k, STEPS - 1))
                f_evh.by(act.activation(f_vT[:], bank[:, 3, :], ACT.Copy))
                if p == 0:
                    return
                copy_pT(j, k, 1)
                probs(j, k, 2)
                copy_pT(j, k, 2)
                probs(j, k, 3)
                copy_pT(j, k, 3)

            def probs(j, k, qt):
                act.wait_ge(f_max.sem, f_max.at(k, qt))
                if qt >= 2:
                    act.wait_ge(f_ptr.sem, f_ptr.at(k, qt - 2))
                f_prob.by(act.activation(f_p[:, qt % 2, :], bank[:, 5, :], ACT.Exp, bias=f_s[:, 1, qt:qt + 1],
                                         scale=LEAF_SCALE, accum_out=f_s[:, 2, qt:qt + 1]))

            def copy_pT(j, k, qt):
                act.wait_ge(f_ptr.sem, f_ptr.at(k, qt))
                f_pok.by(act.activation(f_pT[:, :, qt * P:(qt + 1) * P],
                                        bank[:, 6, :].rearrange("p (t q) -> p t q", t=NT), ACT.Copy))

            def moe(j, u, k):
                p = UNITS[u][1]
                for i in range(MSTEPS + 1):
                    if i < MSTEPS:
                        act.wait_ge(m_a.sem, m_a.at(k, i))
                        if i >= 2:
                            act.wait_ge(m_ts.sem, m_ts.at(k, i - 2))
                        elif p == 1:
                            act.wait_ge(m_hs.sem, m_hs.at(k, i - 2))
                        m_silu.by(act.activation(m_sl[:, i % 2, :], bank[:, i % 2, :], ACT.Silu))
                    if i >= 1:
                        act.wait_ge(m_hs.sem, m_hs.at(k, i - 1))
                        if i - 1 >= 3 or p == 1:
                            act.wait_ge(m_s2.sem, m_s2.at(k, i - 4))
                        m_hi.by(act.activation(m_hh[0][:, (i - 1) % 3, :], m_h[:, (i - 1) % 3, :], ACT.Copy))
                    hand_over(j, u, i - MOE_LAG * p)
                act.wait_ge(m_s2.sem, m_s2.at(k, MSTEPS - 1))
                m_y.by(act.activation(m_yT[:], bank[:, 6, :], ACT.Copy))

            def mha(j, u, k):
                hand_over(j, u, 5)
                max_rows(k, 0)
                for s_ in range(NS2):
                    g, kt = s_ // (2 * NT), s_ // 2 % NT
                    w = T - kt * P
                    act.wait_ge(a_s2.sem, a_s2.at(k, s_))
                    if s_ >= 4:
                        act.wait_ge(a_pv.sem, a_pv.at(k, (s_ - 4) // 2))
                    b = 2 * (s_ % 2)
                    a_e2.by(act.activation(a_p[:, s_ % 4, :, 0:w], bank[:, b:b + 2, 0:w], ACT.Exp))
                    if s_ % 8 == 3 and g >= 1:
                        heads_out(k, g - 1)
                    for job, n in HEADS_PLAN[s_]:
                        if job == "turn":
                            max_rows(k, n)
                    if s_ > HEAD_LAG + 5:
                        hand_over(j, u, s_ - HEAD_LAG)
                heads_out(k, 3)
                act.wait_ge(a_ctr.sem, a_ctr.at(k, 0))
                a_cok.by(act.activation(a_o[:], bank[:, 0, :], ACT.Copy))

            def max_rows(k, quad):
                act.wait_ge(a_mtr.sem, a_mtr.at(k, quad))
                if quad >= 1:
                    act.wait_ge(a_mwr.sem, a_mwr.at(k, quad - 1))
                b = job_bank(HEADS_JOBS.index(("turn", quad)))
                a_mok.by(act.activation(a_mT, bank[0:12, b, 0:T // 2].bitcast(BF16), ACT.Copy))

            def heads_out(k, g):
                act.wait_ge(a_pv.sem, a_pv.at(k, NT * g + NT - 1))
                if g >= 1:
                    act.wait_ge(a_otr.sem, a_otr.at(k, g - 1))
                a_osb.by(act.activation(a_o[:], bank[:, 6, :], ACT.Copy))

            def mamba(j, u, k):
                for m in range(2):
                    act.wait_ge(n_in.sem, n_in.at(k, m))
                    n_xps.by(act.activation(n_xp[:, m, 3:3 + T], bank[:, m, :], ACT.Copy))
                for m in range(2):
                    act.wait_ge(n_in.sem, n_in.at(k, 2 + m))
                    n_sil.by(act.activation(n_sz[:, m, :], bank[:, 2 + m, :], ACT.Silu))
                for m in range(2):
                    if m == 0:
                        act.wait_ge(n_cvs.sem, n_cvs.at(k, 0))
                        n_sil.by(act.activation(n_xc[:, m, :], n_cv[:, m, :], ACT.Silu))
                    else:
                        act.wait_ge(n_cvp.sem, n_cvp.at(k, 0))
                        n_sil.by(act.activation(n_xc[:, m, :], bank[:, 5, :], ACT.Silu, bias=conv_b[:, 1:2]))
                act.activation(preload, half[:, 0, 0:NT], ACT.Exp)
                act.wait_ge(n_xdb.sem, n_xdb.at(k, 0))
                n_dtc.by(act.activation(n_dtr[:], bank[0:64, 4, :], ACT.Copy))
                n_bc1.by(act.activation(n_bc[64:96], bank[64:96, 4, :], ACT.Copy))
                for m in range(2):
                    act.wait_ge(n_dtp.sem, n_dtp.at(k, m))
                    n_abss.by(act.activation(n_abs[:, m, :], bank[:, m, :], ACT.Abs, bias=b_dt[:, m:m + 1]))
                act.wait_ge(n_abss.sem, n_abss.at(k, 1))
                n_us.by(act.activation(n_u[:], n_abs[:], ACT.Exp, scale=-1.0))
                act.wait_ge(n_us.sem, n_us.at(k, 0))
                n_lns.by(act.activation(n_ln[:], n_u[:], ACT.Ln, bias=1.0))
                for m in range(2):
                    n_poss.by(act.activation(n_pos[:, m, :], bank[:, m, :], ACT.Relu, bias=b_dt[:, m:m + 1]))
                act.wait_ge(n_dts.sem, n_dts.at(k, 0))
                for n in range(NSTATE):
                    for m in range(NHALF):
                        if n >= 1:
                            act.wait_ge(n_scan.sem, n_scan.at(k, 2 * n + m - 2))
                        n_das.by(act.activation(n_da[:, m, :], n_dt[:, m, :], ACT.Exp, scale=amat[:, m, n:n + 1]))
                    act.wait_ge(n_cr.sem, n_cr.at(k, n))
                    if n >= 2:
                        act.wait_ge(n_hcs.sem, n_hcs.at(k, 2 * n - 3))
                    n_csc.by(act.activation(n_cs[:, n % 2, :], bank[:, n % 2, :], ACT.Copy))
                    hand_over(j, u, n)

            def hand_over(j, u, i):
                if u + 1 < NU:
                    prologue(j, u + 1, stage_at(ACT_STAGES, i, UNITS[u + 1][0]))

            with act.Fori(0, PAIRS) as j:
                for stage in ACT_STAGES.values():
                    prologue(j, 0, stage)
                for u, (kind, p) in enumerate(UNITS):
                    {"ffn": ffn, "moe": moe, "mha": mha, "mamba": mamba}[kind](j, u, kth[u])
                    unit_end(act, j, u)

        @block.vector
        def _(dve):
            V = nc.vector
            for n, (_, dst, src) in enumerate(splits):
                dve.wait_ge(split_done, n + 1)
                V.tensor_tensor(dst[1], src, dst[0].bitcast(F32), ALU.subtract).then_inc(low_done, 1)
                if n == 0:
                    dve.wait_ge(bias_act, 1)
                    V.tensor_tensor(rest_b[64:128, :], stage_b[64:128, :], biasw[64:128, :], ALU.subtract) \
                        .then_inc(bias_dve, 1)
                if n == 1:
                    dve.wait_ge(bias_act, 2)
                    V.tensor_tensor(rest_b[96:128, :], rest_b[96:128, :], biasw[96:128, :], ALU.subtract) \
                        .then_inc(bias_dve, 1)
            dve.wait_ge(low_done, len(splits))
            dve.wait_ge(bias_dve, 2)
            V.memset(ve, 1.0).then_inc(setup_done, 1)
            dve.wait_ge(setup_done, 3)

            steps = [0]

            def step(j, ins):
                steps[0] += 1
                ins.then_inc(dve_step, 1)
                dve.wait_ge(dve_step, steps[0])

            def newton(j):
                step(j, V.tensor_tensor(y2, y0, y0, ALU.mult))
                step(j, V.tensor_tensor(y2, y2, ve, ALU.mult))
                step(j, V.tensor_scalar(y2, y2, -0.5, 1.5, ALU.mult, ALU.add))
                step(j, V.tensor_tensor(rstd, y2, y0, ALU.mult))

            def stats(j, src):
                for t in range(NT):
                    ins = V.bn_stats(st[:, t, :], src[:, t, :])
                step(j, ins)
                for t in range(NT):
                    ins = V.bn_aggr(mv[:, t, :], st[:, t, :])
                step(j, ins)

            def prologue(j, u, stage):
                if u == NU:
                    return
                kind, p = UNITS[u]
                k = kth[u]
                if stage == "stats":
                    if u < 2:
                        dve.wait_ge(*((x_first, 16), (x_in, 16))[u])
                    stats(j, X[:, p])
                    g_var.by(V.tensor_scalar(ve, mv[:, :, 1], EPS, None, ALU.add))
                if stage == "rows":
                    dve.wait_ge(g_var.sem, g_var.at(u, 0))
                    dve.wait_ge(g_rsq.sem, g_rsq.at(u, 0))
                    newton(j)
                    for t in range(NT):
                        ins = V.tensor_scalar(xn[:, p, t, :], X[:, p, t, :], mv[:, t, 0:1], rstd[:, t:t + 1],
                                              ALU.subtract, ALU.mult)
                    if kind == "mamba":
                        step(j, ins)
                        stats(j, xn[:, p])
                        step(j, V.tensor_tensor(y2, mv[:, :, 0], mv[:, :, 0], ALU.mult))
                        step(j, V.tensor_tensor(y2, y2, mv[:, :, 1], ALU.add))
                        r_var.by(V.tensor_scalar(ve, y2, EPS, None, ALU.add))
                    else:
                        g_xn.by(ins)
                if stage == "rms" and kind == "mamba":
                    dve.wait_ge(r_rsq.sem, r_rsq.at(k, 0))
                    dve.wait_ge(r_var.sem, r_var.at(k, 0))
                    newton(j)
                    for t in range(NT):
                        ins = V.tensor_scalar(xm[p][:, t, :], xn[:, p, t, :], rstd[:, t:t + 1], None, ALU.mult)
                    g_xn.by(ins)
                if stage == "low":
                    dve.wait_ge(g_xh.sem, g_xh.at(u, 0))
                    g_xl.by(V.scalar_tensor_tensor(xT[1][:, p, :], bank[:, 7, :], norm_w if kind == "mamba" else 1.0,
                                                   xT[0][:, p, :].bitcast(F32), ALU.mult, ALU.subtract))
                if kind == "ffn":
                    if stage == "first":
                        dve.wait_ge(t_sc.sem, t_sc.at(k, 0))
                        t_bit.by(V.tensor_scalar(dbit[:], bank[0:96, 7, :], node_b[0:96], 0.0, ALU.add, ALU.is_ge))
                    if stage in ("second", "third", "fourth"):
                        t = ("second", "third", "fourth").index(stage)
                        dve.wait_ge(t_cnt.sem, t_cnt.at(k, t))
                        t_sel.by(V.tensor_scalar(R[:, p, t, :], bank[:, 7, :], leaf_thr, None, ALU.is_ge))
                if kind == "mha":
                    if stage in HEAD_ROTATIONS:
                        rotate(j, k, p, *divmod(HEAD_ROTATIONS.index(stage), 2))
                    if stage in HEAD_RESIDUALS:
                        residual(k, p, *divmod(HEAD_RESIDUALS.index(stage), 2))
                if kind == "moe":
                    if stage == "first":
                        dve.wait_ge(e_log.sem, e_log.at(k, 0))
                        raw = bank[:, 7, 0:NT * EXPERTS].rearrange("p (t e) -> p t e", t=NT)
                        step(j, V.tensor_reduce(gmax, raw, AX_X, ALU.max))
                        e_sub.by(V.tensor_tensor(glog, raw, per_token(gmax), ALU.subtract))
                    if stage == "fourth":
                        dve.wait_ge(e_exp.sem, e_exp.at(k, NT - 1))
                        scores(j)
                    if stage == "ranks":
                        ranks(j, cmp[p])
                    if stage == "combine":
                        combine(j)
                    if stage == "row":
                        dve.wait_ge(e_tr.sem, e_tr.at(k, 0))
                        e_row.by(V.tensor_copy(R[0:96, p, 0, :], bank[0:96, 7, 0:T // 2].bitcast(BF16)))

            def per_token(v):
                return v.unsqueeze(2).to_broadcast([P, NT, EXPERTS])

            def scores(j):
                step(j, V.tensor_reduce(gsum, gexp, AX_X, ALU.add))
                step(j, V.reciprocal(grec, gsum))
                step(j, V.tensor_tensor(gsc, gexp, per_token(grec), ALU.mult))
                step(j, V.tensor_tensor(gbi, gsc, gate_b[:].unsqueeze(1).to_broadcast([P, NT, EXPERTS]), ALU.add))

            def ranks(j, cmp):
                full = [P, NT, EXPERTS, EXPERTS]
                other = gbi.unsqueeze(2).to_broadcast(full)
                own = gbi.unsqueeze(3).to_broadcast(full)
                V.tensor_tensor(cmp[:, 0], other, own, ALU.is_gt)
                step(j, V.tensor_tensor(cmp[:, 1], other, own, ALU.is_equal))
                step(j, V.tensor_tensor(cmp[:, 1], cmp[:, 1], tri[:].unsqueeze(1).to_broadcast(full), ALU.mult))
                step(j, V.tensor_tensor(cmp[:, 0], cmp[:, 0], cmp[:, 1], ALU.add))
                step(j, V.tensor_reduce(grank, cmp[:, 0], AX_X, ALU.add))

            def combine(j):
                step(j, V.scalar_tensor_tensor(gcmb, grank, 1.5, gsc, ALU.is_lt, ALU.mult))
                step(j, V.tensor_copy(cparts[:, :, 0:8], gcmb))
                step(j, V.tensor_tensor(gr1, gcmb, cparts[:, :, 0:8], ALU.subtract))
                step(j, V.tensor_copy(cparts[:, :, 32:40], gr1))
                step(j, V.tensor_tensor(gr2, gr1, cparts[:, :, 32:40], ALU.subtract))
                e_prt.by(V.tensor_copy(cparts[:, :, 64:72], gr2))

            def add_rows(j, p, src, scale=1.0):
                return V.scalar_tensor_tensor(flat(X[:, p]), src, scale, flat(X[:, p]), ALU.mult, ALU.add)

            def ffn(j, u, k, p):
                for i in range(STEPS):
                    dve.wait_ge(f_hi.sem, f_hi.at(k, i))
                    f_lo.by(V.scalar_tensor_tensor(f_h[1][:, i % 4, :], bank[:, i % 3, :], 0.0,
                                                   f_h[0][:, i % 4, :].bitcast(F32), ALU.max, ALU.subtract))
                    if k == SPLIT_AT[0] and i - 1 in SPLIT_AT[1]:
                        e = SPLIT_AT[1].index(i - 1)
                        dve.wait_ge(w_hi.sem, w_hi.at(0, e))
                        w_lo.by(V.tensor_tensor(mwf[1][:, e * 6 * P:(e + 1) * 6 * P], w_stage[:, e % 2],
                                                mwf[0][:, e * 6 * P:(e + 1) * 6 * P].bitcast(F32), ALU.subtract))
                    if p == 1:
                        if i == 0:
                            rows_of_v(k - 1)
                        if i in (1, 3):
                            score_max(j, k - 1, 2 + i // 2)
                        if i == 7:
                            weighted(j, k - 1, 0)
                    hand_over(j, u, i - FFN_LAG * p)
                    if i in (11, 19):
                        t = (11, 19).index(i)
                        dve.wait_ge(f_evh.sem, f_evh.at(k, t))
                        f_evl.by(V.tensor_tensor((f_q, f_k)[t][1][:], bank[:, 3 + t, :], (f_q, f_k)[t][0][:].bitcast(F32),
                                                 ALU.subtract))
                    if i in (20, 22):
                        score_max(j, k, (i - 20) // 2)
                if p == 0:
                    return
                hand_over(j, u, STEPS - FFN_LAG)
                rows_of_v(k)
                score_max(j, k, 2)
                score_max(j, k, 3)
                weighted(j, k, p)

            def rows_of_v(k):
                dve.wait_ge(f_vtr.sem, f_vtr.at(k, 0))
                f_vok.by(V.tensor_copy(f_v[:], bank[:, 3, :].rearrange("p (t d) -> p t d", t=NT)))

            def weighted(j, k, p):
                dve.wait_ge(f_prob.sem, f_prob.at(k, 3))
                step(j, V.reciprocal(f_s[:, 3, :], f_s[:, 2, :]))
                step(j, V.tensor_scalar(f_s[:, 4, :], f_s[:, 3, :], 0.5, None, ALU.mult))
                dve.wait_ge(f_pv.sem, f_pv.at(k, NT - 1))
                for qt in range(NT):
                    ins = V.scalar_tensor_tensor(X[:, p, qt, :], bank[:, 4, qt * P:(qt + 1) * P], f_s[:, 4, qt:qt + 1],
                                                 X[:, p, qt, :], ALU.mult, ALU.add)
                step(j, ins)

            def score_max(j, k, qt):
                dve.wait_ge(f_sco.sem, f_sco.at(k, qt))
                step(j, V.tensor_reduce(f_s[:, 0, qt:qt + 1], bank[:, 5, :], AX_X, ALU.max))
                f_max.by(V.tensor_scalar(f_s[:, 1, qt:qt + 1], f_s[:, 0, qt:qt + 1], -LEAF_SCALE, None, ALU.mult))

            def moe(j, u, k, p):
                for i in range(MSTEPS):
                    e = i // 2
                    dve.wait_ge(m_b.sem, m_b.at(k, i))
                    dve.wait_ge(m_silu.sem, m_silu.at(k, i))
                    if i >= 3 or p == 1:
                        dve.wait_ge(m_lo.sem, m_lo.at(k, i - 3))
                    if e < EXPERTS:
                        m_ts.by(V.tensor_tensor(m_t[:, i % 2, :], m_sl[:, i % 2, :], bank[:, 2 + i % 2, :], ALU.mult))
                        dve.wait_ge(m_ts.sem, m_ts.at(k, i))
                        dve.wait_ge(m_cr.sem, m_cr.at(k, e))
                        m_hs.by(V.tensor_tensor(m_h[:, i % 3, :], m_t[:, i % 2, :], bank[:, 4 + e % 2, :], ALU.mult))
                    else:
                        m_hs.by(V.tensor_tensor(m_h[:, i % 3, :], m_sl[:, i % 2, :], bank[:, 2 + i % 2, :], ALU.mult))
                    if i == 1 and p == 1:
                        mixed(j, k - 1, 0)
                    hand_over(j, u, i - MOE_LAG * p)
                if p == 1:
                    mixed(j, k, p)

            def mixed(j, k, p):
                dve.wait_ge(m_ytr.sem, m_ytr.at(k, 0))
                m_res.by(add_rows(j, p, bank[:, 7, :], 0.5))
                dve.wait_ge(m_res.sem, m_res.at(k, 0))

            def mha(j, u, k, p):
                V.tensor_tensor(X[:, p], X[:, p], out_b[:].unsqueeze(1).to_broadcast([P, NT, P]), ALU.add)
                hand_over(j, u, 0)
                dve.wait_ge(a_vpr.sem, a_vpr.at(k, 0))
                a_vok.by(V.tensor_copy(a_v[:, :, :, 0:DH], bank[:, 6, :].rearrange("p (t h d) -> p t h d", t=NT, d=DH)))
                hand_over(j, u, 2)
                for n, (job, which) in enumerate(HEADS_PLAN[-1]):
                    head_job(j, k, job, which)
                    if n == 4:
                        hand_over(j, u, 6)
                for s_ in range(NS2):
                    for job, which in HEADS_PLAN[s_]:
                        head_job(j, k, job, which)
                    if s_ >= HEAD_LAG + 7:
                        hand_over(j, u, s_ - HEAD_LAG)
                normalise(j, k, QUADS - 1)
                dve.wait_ge(a_out.sem, a_out.at(k, 0))
                add_rows(j, p, bank[:, 2, :])

            def normalise(j, k, g):
                dve.wait_ge(a_otr.sem, a_otr.at(k, g))
                if g >= 1:
                    dve.wait_ge(a_norm.sem, a_norm.at(k, g - 1))
                src = bank[:, job_bank(HEADS_JOBS.index(("rows", g))), :].rearrange("p (t c w) -> p t c w", t=NT, c=4)
                step(j, V.reciprocal(a_rec[:], src[:, :, :, DH]))
                a_norm.by(V.tensor_tensor(a_rows[:, :, 32 * g:32 * g + 32].rearrange("p t (c d) -> p t c d", d=DH),
                                          src[:, :, :, 0:DH], a_rec[:].unsqueeze(3).to_broadcast([P, NT, 4, DH]),
                                          ALU.mult))

            def rotate(j, k, p, side, c):
                dve.wait_ge(a_rld.sem, a_rld.at(0, 0))
                dve.wait_ge(a_proj.sem, a_proj.at(k, 2 * side + c))
                if side == 1:
                    dve.wait_ge(a_prt.sem, a_prt.at(k, 2))
                full, other = a_rot(p)
                a_took.by(V.scalar_tensor_tensor((full, other)[c], bank[:, 7, :], HEAD_SCALE if side == 0 else 1.0,
                                                 rope[:, c, :], ALU.mult, ALU.mult))
                if c == 1:
                    dve.wait_ge(a_took.sem, a_took.at(k, 2 * side + 1))
                    a_rotd.by(V.tensor_tensor(full, full, other, ALU.add))

            def residual(k, p, side, c):
                dve.wait_ge(a_prt.sem, a_prt.at(k, 3 * side + c))
                a_res.by(V.tensor_tensor(a_rot(p)[0], a_rot(p)[0], a_parts[:, c, :], ALU.subtract))

            def head_job(j, k, job, n):
                if job == "rows":
                    normalise(j, k, n)
                if job == "slot":
                    quad, (qt, h0, nh) = n // NS1, SLOTS_4[n % NS1]
                    w = (qt + 1) * P
                    dve.wait_ge(a_s1.sem, a_s1.at(k, n))
                    src = bank[:, job_bank(HEADS_JOBS.index((job, n))), 0:nh * w].rearrange("p (h w) -> p h w", w=w)
                    a_m1.by(V.tensor_reduce(a_mx[:, quad, qt, h0:h0 + nh], src, AX_X, ALU.max, negate=True))
                    if n % NS1 == NS1 - 1:
                        max_parts(j, k, quad)

            def max_parts(j, k, quad):
                dve.wait_ge(a_m1.sem, a_m1.at(k, quad * NS1 + NS1 - 1))
                step(j, V.tensor_copy(a_mp[:, quad, :, 0, :], a_mx[:, quad]))
                step(j, V.tensor_tensor(a_mr[:], a_mx[:, quad], a_mp[:, quad, :, 0, :], ALU.subtract))
                step(j, V.tensor_copy(a_mp[:, quad, :, 1, :], a_mr[:]))
                step(j, V.tensor_tensor(a_mx[:, quad], a_mr[:], a_mp[:, quad, :, 1, :], ALU.subtract))
                a_mpt.by(V.tensor_copy(a_mp[:, quad, :, 2, :], a_mx[:, quad]))

            def mamba(j, u, k, p):
                V.tensor_tensor(X[:, p], X[:, p], xn[:, p], ALU.add)
                dve.wait_ge(n_fill.sem, n_fill.at(k, 0))
                dve.wait_ge(n_xps.sem, n_xps.at(k, 0))
                step(j, V.tensor_scalar(n_cv[:, 0, :], n_xp[:, 0, 0:T], conv_w[:, 0, 0:1], conv_b[:, 0:1],
                                        ALU.mult, ALU.add))
                for c in range(1, 4):
                    ins = V.scalar_tensor_tensor(n_cv[:, 0, :], n_xp[:, 0, c:c + T], conv_w[:, 0, c:c + 1],
                                                 n_cv[:, 0, :], ALU.mult, ALU.add)
                    if c < 3:
                        step(j, ins)
                n_cvs.by(ins)
                dve.wait_ge(n_bc1.sem, n_bc1.at(k, 0))
                step(j, V.tensor_tensor(n_r[64:96], bank[64:96, 4, :], n_bc[64:96], ALU.subtract))
                n_mids.by(V.tensor_copy(n_mid[64:96], n_r[64:96]))
                dve.wait_ge(n_mids.sem, n_mids.at(k, 0))
                step(j, V.tensor_tensor(n_r[64:96], n_r[64:96], n_mid[64:96], ALU.subtract))
                n_bcp.by(V.tensor_copy(n_bc[0:32], n_r[64:96]))
                dve.wait_ge(n_us.sem, n_us.at(k, 0))
                dve.wait_ge(n_sil.sem, n_sil.at(k, 3))
                step(j, V.tensor_scalar(n_cor[:], n_u[:], 1.0, -1.0, ALU.add, ALU.add))
                step(j, V.tensor_tensor(n_cor[:], n_u[:], n_cor[:], ALU.subtract))
                dve.wait_ge(n_lns.sem, n_lns.at(k, 0))
                step(j, V.tensor_tensor(n_cor[:], n_cor[:], n_ln[:], ALU.add))
                dve.wait_ge(n_lows.sem, n_lows.at(k, 0))
                step(j, V.tensor_tensor(n_cor[:], n_cor[:], n_low[:], ALU.max))
                step(j, V.tensor_tensor(n_cor[:], n_cor[:], n_u[:], ALU.min))
                dve.wait_ge(n_poss.sem, n_poss.at(k, 1))
                n_dts.by(V.tensor_tensor(n_dt[:], n_cor[:], n_pos[:], ALU.add))
                dve.wait_ge(n_dts.sem, n_dts.at(k, 0))
                dve.wait_ge(n_sil.sem, n_sil.at(k, 3))
                n_dtxs.by(V.tensor_tensor(n_dtx[:], n_dt[:], n_xc[:], ALU.mult))
                dve.wait_ge(n_dtxs.sem, n_dtxs.at(k, 0))
                for n in range(NSTATE):
                    dve.wait_ge(n_br.sem, n_br.at(k, n))
                    for m in range(NHALF):
                        i = 2 * n + m
                        if n >= 1:
                            dve.wait_ge(n_scan.sem, n_scan.at(k, i - 2))
                        n_dbs.by(V.tensor_tensor(n_db[:, m, :], n_dtx[:, m, :], bank[:, 4 + n % 2, :], ALU.mult))
                    for m in range(NHALF):
                        i = 2 * n + m
                        dve.wait_ge(n_dbs.sem, n_dbs.at(k, i))
                        dve.wait_ge(n_das.sem, n_das.at(k, i))
                        if n >= 1:
                            dve.wait_ge(n_hcs.sem, n_hcs.at(k, i - 2))
                        n_scan.by(V.tensor_tensor_scan(n_h[:, m, :], n_da[:, m, :], n_db[:, m, :], 0.0,
                                                       ALU.mult, ALU.add))
                    hand_over(j, u, n)
                for at in range(NSTATE, NSTATE + 2):
                    hand_over(j, u, at)
                dve.wait_ge(n_scan.sem, n_scan.at(k, 2 * NSTATE - 1))
                for m in range(2):
                    dve.wait_ge(n_ya.sem, n_ya.at(k, 2 * NSTATE - 2 + m))
                    step(j, V.scalar_tensor_tensor(n_db[:, m, :], n_xc[:, m, :], d_skip[:, m:m + 1], bank[:, 2 + m, :],
                                                   ALU.mult, ALU.add))
                    n_y.by(V.tensor_tensor(n_db[:, m], n_db[:, m], n_sz[:, m], ALU.mult))
                dve.wait_ge(n_o.sem, n_o.at(k, 0))
                add_rows(j, p, bank[:, 6, :])

            def hand_over(j, u, i):
                if u + 1 < NU:
                    prologue(j, u + 1, stage_at(DVE_STAGES, i, UNITS[u + 1][0]))

            with dve.Fori(0, PAIRS) as j:
                steps[0] = 0
                for stage in DVE_STAGES.values():
                    prologue(j, 0, stage)
                for u, (kind, p) in enumerate(UNITS):
                    {"ffn": ffn, "moe": moe, "mha": mha, "mamba": mamba}[kind](j, u, kth[u], p)
                    unit_end(dve, j, u)

        @block.tensor
        def _(pe):
            mm = nc.tensor.matmul
            pe.wait_ge(setup_done, 3)

            def product(dst, w, x, start=True, stop=True):
                mm(dst, w[0], x[0], start=start, stop=False)
                mm(dst, w[0], x[1], start=False, stop=False)
                return mm(dst, w[1], x[0], start=False, stop=stop)

            def xs(p):
                return [xT[0][:, p, :], xT[1][:, p, :]]

            def rows(dst, src, idn):
                for t in range(NT):
                    ins = nc.tensor.transpose(dst(t), src(t), idn)
                return ins

            def back(b, src):
                return rows(lambda t: bank[:, b, t * P:(t + 1) * P], lambda t: src[:, t * P:(t + 1) * P], ident[:])

            def prologue(j, u, stage):
                if u == NU:
                    return
                kind, p = UNITS[u]
                k = kth[u]
                if stage == "turn":
                    pe.wait_ge(g_xn.sem, g_xn.at(u, 0))
                    src = xm[p] if kind == "mamba" else xn[:, p]
                    g_tr.by(rows(lambda t: bank[:, 7, t * P:(t + 1) * P], lambda t: src[:, t, :], ident[:]))
                if kind == "ffn":
                    if stage == "first":
                        pe.wait_ge(g_xl.sem, g_xl.at(u, 0))
                        t_sc.by(product(bank[0:96, 7, :], [rw[0][:, 0:96], rw[1][:, 0:96]], xs(p)))
                    if stage == "second":
                        pe.wait_ge(t_bit.sem, t_bit.at(k, 0))
                        t_cnt.by(mm(bank[:, 7, :], tree[:, 0, :], dbit[:], start=True, stop=True))
                    if stage in ("third", "fourth"):
                        t = ("third", "fourth").index(stage) + 1
                        pe.wait_ge(t_sel.sem, t_sel.at(k, t - 1))
                        t_cnt.by(mm(bank[:, 7, :], tree[:, t, :], dbit[:], start=True, stop=True))
                if kind == "mha" and stage in HEAD_ROTATIONS:
                    n = HEAD_ROTATIONS.index(stage)
                    if n == 0:
                        pe.wait_ge(g_xl.sem, g_xl.at(u, 0))
                    else:
                        pe.wait_ge(a_took.sem, a_took.at(k, n - 1))
                    a_proj.by(product(bank[:, 7, :], [aw[c][:, n, :] for c in range(2)], xs(p)))
                if kind == "moe":
                    if stage == "first":
                        pe.wait_ge(g_xl.sem, g_xl.at(u, 0))
                        for t in range(NT):
                            x = [xT[c][:, p, t * P:(t + 1) * P] for c in range(2)]
                            ins = product(bank[:, 7, t * EXPERTS:(t + 1) * EXPERTS], x,
                                          [rw[0][:, 96:104], rw[1][:, 96:104]])
                        e_log.by(ins)
                    if stage == "weights":
                        pe.wait_ge(e_prt.sem, e_prt.at(k, 0))
                        tr = bank[0:96, 7, 0:T // 2].bitcast(BF16)
                        e_tr.by(rows(lambda t: tr[:, t * P:(t + 1) * P], lambda t: cparts[:, t, :], identb))

            def ready(j, u):
                kind, p = UNITS[u]
                pe.wait_ge(g_xl.sem, g_xl.at(u, 0))

            def ffn(j, u, k, p):
                x = xs(p)
                ready(j, u)
                pe.wait_ge(t_sel.sem, t_sel.at(k, TREES - 1))
                for i in range(STEPS + 2):
                    if i < STEPS:
                        t, m = divmod(i, M1)
                        b = bank[:, i % 3, :]
                        if i >= 3 or p == 1:
                            pe.wait_ge(f_lo.sem, f_lo.at(k, i - 3))
                        product(b, [fw1[c][:, t, m * P:(m + 1) * P] for c in range(2)], x, stop=False)
                        f_s1.by(mm(b, b1w[:, t, m * P:(m + 1) * P], R[:, p, t, :], start=False, stop=True))
                    if i >= 2:
                        i2 = i - 2
                        t, m = divmod(i2, M1)
                        acc = bank[:, 3 + t % 2, :]
                        pe.wait_ge(f_lo.sem, f_lo.at(k, i2))
                        if i2 == 2 * M1:
                            pe.wait_ge(f_evl.sem, f_evl.at(k, 0))
                        if i2 == 0 and p == 1:
                            pe.wait_ge(f_vok.sem, f_vok.at(k - 1, 0))
                        if m == 0:
                            mm(acc, b2w[:, t, :], R[:, p, t, :], start=True, stop=False)
                        f_s2.by(product(acc, [fw2[c][:, t, m, :] for c in range(2)],
                                        [f_h[c][:, i2 % 4, :] for c in range(2)], start=False, stop=m == M1 - 1))
                    if p == 1 and i < FFN_LAG + 1:
                        attend(j, k - 1, ATTEND_AT.get(i, ()))
                    hand_over(j, u, i - FFN_LAG * p)
                    if i in (21, 23):
                        score(j, k, (i - 21) // 2)
                    if i == 24:
                        turn(j, k, 0)
                if p == 1:
                    attend(j, k, [item for at in sorted(ATTEND_AT) for item in ATTEND_AT[at]])

            def attend(j, k, items):
                for what, qt in items:
                    if what == "values":
                        pe.wait_ge(f_evh.sem, f_evh.at(k, 2))
                        f_vtr.by(back(3, f_vT))
                    else:
                        {"score": score, "turn": turn, "weigh": weigh}[what](j, k, qt)

            def score(j, k, qt):
                if qt == 0:
                    pe.wait_ge(f_evl.sem, f_evl.at(k, 1))
                else:
                    pe.wait_ge(f_prob.sem, f_prob.at(k, qt - 1))
                f_sco.by(product(bank[:, 5, :], [f_q[c][:, qt * P:(qt + 1) * P] for c in range(2)],
                                 [f_k[c][:] for c in range(2)]))

            def turn(j, k, qt):
                pe.wait_ge(f_prob.sem, f_prob.at(k, qt))
                if qt:
                    pe.wait_ge(f_pok.sem, f_pok.at(k, qt - 1))
                f_ptr.by(rows(lambda t: bank[:, 6, t * P:(t + 1) * P],
                              lambda t: f_p[:, qt % 2, t * P:(t + 1) * P], ident[:]))

            def weigh(j, k, qt):
                pe.wait_ge(f_pok.sem, f_pok.at(k, qt))
                pe.wait_ge(f_vok.sem, f_vok.at(k, 0))
                for kt in range(NT):
                    ins = mm(bank[:, 4, qt * P:(qt + 1) * P], f_pT[:, kt, qt * P:(qt + 1) * P], f_v[:, kt, :],
                             start=kt == 0, stop=kt == NT - 1)
                f_pv.by(ins)

            def moe(j, u, k, p):
                x = xs(p)
                ready(j, u)
                if k == 0:
                    pe.wait_ge(w_lo.sem, w_lo.at(0, EXPERTS - 1))
                for i in range(MSTEPS + 3):
                    if i < MSTEPS:
                        e, m = divmod(i, 2)
                        if i >= 2:
                            pe.wait_ge(m_ts.sem, m_ts.at(k, i - 2))
                        elif p == 1:
                            pe.wait_ge(m_hs.sem, m_hs.at(k, i - 2))
                        m_a.by(product(bank[:, i % 2, :], [mw[c][:, e, m, :] for c in range(2)], x))
                        m_b.by(product(bank[:, 2 + i % 2, :], [mw[c][:, e, 2 + m, :] for c in range(2)], x))
                        if m == 0 and e < EXPERTS:
                            if e == 0:
                                pe.wait_ge(e_row.sem, e_row.at(k, 0))
                            if e >= 2:
                                pe.wait_ge(m_hs.sem, m_hs.at(k, i - 3))
                            m_cr.by(mm(bank[:, 4 + e % 2, :], pick[:, e:e + 1].to_broadcast([96, P]), R[0:96, p, 0, :],
                                       start=True, stop=True))
                    if i >= 3:
                        i2 = i - 3
                        e, m = divmod(i2, 2)
                        pe.wait_ge(m_lo.sem, m_lo.at(k, i2))
                        if i2 == 0 and p == 1:
                            pe.wait_ge(m_y.sem, m_y.at(k - 1, 0))
                        m_s2.by(product(bank[:, 6, :], [mw[c][:, e, 4 + m, :] for c in range(2)],
                                        [m_hh[c][:, i2 % 3, :] for c in range(2)], start=i2 == 0, stop=i2 == MSTEPS - 1))
                    hand_over(j, u, i - MOE_LAG * p)
                    if i == 1 and p == 1:
                        rows_of_y(k - 1)
                if p == 1:
                    rows_of_y(k)

            def rows_of_y(k):
                pe.wait_ge(m_y.sem, m_y.at(k, 0))
                m_ytr.by(back(7, m_yT))

            def mha(j, u, k, p):
                x = xs(p)
                ready(j, u)
                for t in range(NT):
                    ins = product(bank[:, 6, t * P:(t + 1) * P], [xT[c][:, p, t * P:(t + 1) * P] for c in range(2)],
                                  [aw[c][:, 4, :] for c in range(2)])
                a_vpr.by(ins)
                pe.wait_ge(a_fill.sem, a_fill.at(0, 1))
                rows_of_half(k, 0)
                for n, (job, which) in enumerate(HEADS_PLAN[-1]):
                    head_job(k, job, which)
                    if n == 1:
                        hand_over(j, u, 4)
                for s_ in range(NS2 + 3):
                    if s_ < NS2:
                        g, kt, pair = s_ // (2 * NT), s_ // 2 % NT, s_ % 2
                        w = T - kt * P
                        if s_ % STEPS_4 == 0:
                            pe.wait_ge(a_mld[g].sem, a_mld[g].at(k, 1))
                        if s_ >= 2:
                            pe.wait_ge(a_e2.sem, a_e2.at(k, s_ - 2))
                        for n in range(2):
                            h = 4 * g + 2 * pair + n
                            b = 2 * (s_ % 2) + n
                            mm(bank[:, b, 0:w], a_k[:, h, kt * P:(kt + 1) * P], a_q[:, h // 2, kt * P:T],
                               start=True, stop=False)
                            ins = mm(bank[:, b, 0:P], identb, mask_kq, start=False, stop=True)
                        a_s2.by(ins)
                        for job, which in HEADS_PLAN[s_]:
                            head_job(k, job, which)
                    if s_ >= 3 and s_ % 2 == 1:
                        q_ = (s_ - 3) // 2
                        g, kt = divmod(q_, NT)
                        pe.wait_ge(a_e2.sem, a_e2.at(k, 2 * q_ + 1))
                        if kt == 0 and g >= 1:
                            pe.wait_ge(a_osb.sem, a_osb.at(k, g - 1))
                        if q_ == 0:
                            pe.wait_ge(a_vok.sem, a_vok.at(k, 0))
                            pe.wait_ge(a_fill.sem, a_fill.at(0, 2))
                        for c in range(4):
                            ring = (2 * q_ + c // 2) % 4
                            ins = mm(bank[32 * c:32 * c + 32, 6, kt * P:T], a_v[:, kt, 4 * g + c, :],
                                     a_p[:, ring, c % 2, 0:T - kt * P], start=kt == 0, stop=kt == NT - 1)
                        a_pv.by(ins)
                    if s_ > HEAD_LAG + 6:
                        hand_over(j, u, s_ - HEAD_LAG)
                head_job(k, "rows", QUADS - 1)
                pe.wait_ge(a_norm.sem, a_norm.at(k, 3))
                a_ctr.by(rows(lambda t: bank[:, 0, t * P:(t + 1) * P], lambda t: a_rows[:, t, :], ident[:]))
                pe.wait_ge(a_cok.sem, a_cok.at(k, 0))
                for t in range(NT):
                    ins = mm(bank[:, 2, t * P:(t + 1) * P], a_o[:, t * P:(t + 1) * P], owT[:], start=True, stop=True)
                a_out.by(ins)

            def rows_of_half(k, n):
                pe.wait_ge(a_ldq[n].sem, a_ldq[n].at(k, 0))
                pe.wait_ge(a_ldk[n].sem, a_ldk[n].at(k, 1))

            def bank_free(k, i):
                if i < RING_OF_4:
                    i -= 2
                if i >= 2:
                    job, n = HEADS_JOBS[i - 2]
                    signal = {"slot": a_m1, "turn": a_mok, "rows": a_norm}[job]
                    pe.wait_ge(signal.sem, signal.at(k, n))

            def head_job(k, job, n):
                i = HEADS_JOBS.index((job, n))
                b = job_bank(i)
                bank_free(k, i)
                if job == "slot":
                    quad, (qt, h0, nh) = n // NS1, SLOTS_4[n % NS1]
                    if quad == 2 and n % NS1 == 0:
                        rows_of_half(k, 1)
                    w = (qt + 1) * P
                    for c in range(nh):
                        h = 4 * quad + h0 + c
                        mm(bank[:, b, c * w:(c + 1) * w], a_q[:, h // 2, qt * P:(qt + 1) * P], a_k[:, h, 0:w],
                           start=True, stop=False)
                        ins = mm(bank[:, b, c * w + qt * P:(c + 1) * w], identb, mask_qk, start=False, stop=True)
                    a_s1.by(ins)
                if job == "turn":
                    pe.wait_ge(a_mpt.sem, a_mpt.at(k, n))
                    tr = bank[0:12, b, 0:T // 2].bitcast(BF16)
                    a_mtr.by(rows(lambda t: tr[:, t * P:(t + 1) * P], lambda t: flat(a_mp[:, n, t]), identb))
                if job == "rows":
                    pe.wait_ge(a_osb.sem, a_osb.at(k, n))
                    a_otr.by(back(b, a_o))

            def mamba(j, u, k, p):
                x = xs(p)
                ready(j, u)
                for n in range(4):
                    n_in.by(product(bank[:, n, :], [win[c][:, n, :] for c in range(2)], x))
                pe.wait_ge(n_xps.sem, n_xps.at(k, 1))
                pe.wait_ge(n_fill.sem, n_fill.at(k, 0))
                for c in range(4):
                    ins = mm(bank[:, 5, :], taps[:, c, :], n_xp[:, 1, c:c + T], start=c == 0, stop=c == 3)
                n_cvp.by(ins)
                for m in range(2):
                    pe.wait_ge(n_sil.sem, n_sil.at(k, 2 + m))
                    ins = mm(bank[0:96, 4, :], wx[:, m, :], n_xc[:, m, :], start=m == 0, stop=m == 1)
                n_xdb.by(ins)
                pe.wait_ge(n_dtc.sem, n_dtc.at(k, 0))
                for m in range(2):
                    n_dtp.by(mm(bank[:, m, :], wdt[:, m, :], n_dtr[:], start=True, stop=True))
                pe.wait_ge(n_bcp.sem, n_bcp.at(k, 0))
                pe.wait_ge(n_bcm.sem, n_bcm.at(k, 0))
                pe.wait_ge(n_poss.sem, n_poss.at(k, 1))
                pe.wait_ge(n_abss.sem, n_abss.at(k, 1))
                for n in range(NSTATE + 2):
                    if n < NSTATE:
                        if n >= 2:
                            pe.wait_ge(n_dbs.sem, n_dbs.at(k, 2 * n - 3))
                        n_br.by(mm(bank[:, 4 + n % 2, :], pick[:, n:n + 1].to_broadcast([96, P]), n_bc[:],
                                   start=True, stop=True))
                        if n >= 2:
                            pe.wait_ge(n_csc.sem, n_csc.at(k, n - 2))
                        n_cr.by(mm(bank[:, n % 2, :], pick[:, 16 + n:17 + n].to_broadcast([96, P]), n_bc[:],
                                   start=True, stop=True))
                    if n >= 2:
                        for m in range(2):
                            pe.wait_ge(n_hcs.sem, n_hcs.at(k, 2 * n - 4 + m))
                            n_ya.by(mm(bank[:, 2 + m, :], ident[:], n_hc[:, m, :], start=n == 2, stop=n == NSTATE + 1))
                    hand_over(j, u, n)
                hand_over(j, u, NSTATE + 2)
                pe.wait_ge(n_y.sem, n_y.at(k, 1))
                for t in range(NT):
                    for m in range(2):
                        ins = mm(bank[:, 6, t * P:(t + 1) * P], n_db[:, m, t * P:(t + 1) * P], wout[:, m, :],
                                 start=m == 0, stop=m == 1)
                n_o.by(ins)

            def hand_over(j, u, i):
                if u + 1 < NU:
                    prologue(j, u + 1, stage_at(PE_STAGES, i, UNITS[u + 1][0]))

            with pe.Fori(0, PAIRS) as j:
                for stage in PE_STAGES.values():
                    prologue(j, 0, stage)
                for u, (kind, p) in enumerate(UNITS):
                    {"ffn": ffn, "moe": moe, "mha": mha, "mamba": mamba}[kind](j, u, kth[u], p)
                    unit_end(pe, j, u)

        for signal in signals:
            signal.whole()


def constants():
    f, half = np.float32, P // 2
    pos = np.arange(T, dtype=f)
    freqs = (f(1.0) / f(10000.0) ** (np.arange(half, dtype=f) / f(half))).astype(f)
    angle = pos[:, None] * freqs[None, :]
    sin, cos = np.sin(angle).astype(f).T, np.cos(angle).astype(f).T
    rope = np.stack([np.concatenate([cos, cos]), np.concatenate([-sin, sin])], 1)
    eye = np.eye(P, dtype=f)
    later = np.arange(P)[None, :] > np.arange(P)[:, None]
    mask_qk = np.where(later, f(-1e9), f(0))
    mask_kq = np.where(later.T, f(-1e9), f(0))
    path = np.zeros((LEAVES, LEAVES), f)
    depth = LEAVES.bit_length() - 1
    path[LEAVES - 1] = -depth
    for leaf in range(LEAVES):
        node = leaf + LEAVES - 1
        while node:
            up = (node - 1) // 2
            path[up, leaf] = 1 if node == 2 * up + 2 else -1
            path[LEAVES - 1, leaf] += node == 2 * up + 1
            node = up
    tree = np.zeros((96, TREES, P), f)
    thr = np.full(P, -0.5, f)
    thr[0:32] = 0.5
    for t in range(TREES):
        tree[32 * t:32 * t + LEAVES, t, 0:LEAVES] = -path
        for c in range(1, 4):
            tree[32 * t:32 * t + LEAVES, t, 32 * c:32 * c + LEAVES] = path
    big = np.zeros((P, TREES * (M1 * P + P)), f)
    for t in range(TREES):
        for leaf in range(LEAVES):
            big[leaf, t * M1 * P + leaf * LEAF_W:t * M1 * P + (leaf + 1) * LEAF_W] = -2.0 ** 100
    pick = np.zeros((96, 32), f)
    for c in range(3):
        pick[32 * c:32 * c + 32] = np.eye(32, dtype=f)
    tri = np.broadcast_to(np.tril(np.ones((EXPERTS, EXPERTS), f), -1), (P, EXPERTS, EXPERTS))
    bf = np.dtype("bfloat16")

    def parts(v):
        got = []
        for _ in range(3):
            got.append(v.astype(bf).astype(f))
            v = v - got[-1]
        return got
    slopes = np.array([2.0 ** (-8.0 * (i + 1) / HEADS) for i in range(HEADS)], f)
    q_rows, k_rows = np.zeros((2, 16, HEADS, T), f)
    k_rows[0:3] = 1
    even = pos - pos % 2
    for n, part in enumerate(parts(slopes)):
        for c, v in enumerate((even, pos - even)):
            q_rows[3 + 2 * n + c] = part[:, None]
            k_rows[3 + 2 * n + c] = v[None, :]
    for n, part in enumerate(parts(-slopes[:, None] * pos[None, :])):
        q_rows[9 + n] = part
        k_rows[9 + n] = 1

    def by_parity(rows):
        return rows.reshape(16, HEADS // 2, 2, T).transpose(0, 2, 1, 3).astype(bf)
    return {"rope": rope, "ident": eye, "tri": tri,
            "cbf": np.stack([eye, mask_qk, mask_kq], 1).astype(bf), "tree": tree.astype(bf), "bias": big,
            "pick": pick.astype(bf), "q_rows": by_parity(q_rows), "k_rows": by_parity(k_rows)}, thr


def layouts(a):
    const, thr = constants()
    by_dim = np.arange(P).reshape(HEADS // 2, 2, DH).transpose(1, 2, 0).reshape(-1)
    f = np.float32

    def zeros(*shape):
        return np.zeros(shape, f)
    d = dict(const)
    d["rope"] = const["rope"][by_dim]
    d["x"] = np.concatenate([a["L0_attn_x"].reshape(BATCHES, NT, P, P), zeros(1, NT, P, P)])
    fw1, fw2, bias = zeros(P, TREES, M1 * P), zeros(P, TREES, M1, P), const["bias"]
    rw, col = zeros(P, 96 + EXPERTS), zeros(P, 20)
    for t, n in enumerate("qkv"):
        fw1[:, t] = a[f"L0_ffn_{n}_w1"].transpose(1, 0, 2).reshape(P, -1)
        fw2[:, t] = a[f"L0_ffn_{n}_w2"].reshape(M1, P, P).transpose(1, 0, 2)
        rw[:, 32 * t:32 * t + LEAVES - 1] = a[f"L0_ffn_{n}_node_w"].T
        col[32 * t:32 * t + LEAVES - 1, 1] = a[f"L0_ffn_{n}_node_b"]
        for c in range(1, 4):
            for leaf in range(LEAVES):
                at = t * M1 * P + leaf * LEAF_W
                bias[32 * c + leaf, at:at + LEAF_W] = a[f"L0_ffn_{n}_b1"][leaf]
            at = TREES * M1 * P + t * P
            bias[32 * c:32 * c + LEAVES, at:at + P] = a[f"L0_ffn_{n}_b2"]
    rw[:, 96:] = a["L1_ffn_gate_w"].T
    mw = zeros(P, MLPS, 6, P)
    for e in range(MLPS):
        w1, w2, w3 = (a[f"L1_ffn_w{n}"][e] if e < EXPERTS else a[f"L1_ffn_sw{n}"] for n in (1, 2, 3))
        mw[:, e, 0:2] = w1.T.reshape(P, 2, P)
        mw[:, e, 2:4] = w3.T.reshape(P, 2, P)
        mw[:, e, 4:6] = w2.T.reshape(2, P, P).transpose(1, 0, 2)
    wq, wk, wv = (a[f"L0_attn_w{n}"].T for n in "qkv")
    d["aw"] = np.stack([wq[:, by_dim], np.roll(wq, P // 2, 1)[:, by_dim], wk[:, by_dim],
                        np.roll(wk, P // 2, 1)[:, by_dim], wv], 1)
    d["owT"] = a["L0_attn_out_w"].T
    d["out_b"] = np.broadcast_to(a["L0_attn_out_b"], (P, P))
    d["win"] = a["L1_attn_W_in"].reshape(P, 4, P)
    d["wx"] = a["L1_attn_W_x"].reshape(NHALF, P, 96).transpose(1, 0, 2)
    d["wdt"] = a["L1_attn_W_dt"].reshape(64, NHALF, P)
    d["wout"] = a["L1_attn_W_out"].reshape(NHALF, P, P).transpose(1, 0, 2)
    d["a_log"] = a["L1_attn_A_log"].reshape(NHALF, P, NSTATE).transpose(1, 0, 2)
    col[:, 0], col[:, 2] = thr, a["L1_attn_norm_w"]
    col[:, 5:13] = a["L1_attn_conv_w"].reshape(NHALF, P, 4).transpose(1, 0, 2).reshape(P, 8)
    for at, name in ((13, "conv_b"), (15, "b_dt"), (17, "D")):
        col[:, at:at + 2] = a[f"L1_attn_{name}"].reshape(NHALF, P).T
    d["gate_b"] = np.broadcast_to(a["L1_ffn_gate_bias"], (P, EXPERTS))
    d.update(fw1=fw1.reshape(P, -1), fw2=fw2.reshape(P, -1), bias=bias, rw=rw, col=col, mw=mw.reshape(P, -1))
    d["aw"], d["win"] = d["aw"].reshape(P, -1), d["win"].reshape(P, -1)
    return d


def kernel(**inputs):
    import numpy as _np
    import concourse.bacc as _bacc
    from concourse import mybir as _mybir
    from concourse.bass_utils import run_bass_kernel_spmd as _run

    nc = _bacc.Bacc("TRN2", target_bir_lowering=False, num_devices=1)
    arrays, args = {}, {}
    for name, a in layouts({n: _np.asarray(v) for n, v in inputs.items()}).items():
        a = _np.ascontiguousarray(a)
        arrays[f"in_{name}_dram"] = a
        args[name] = nc.dram_tensor(f"in_{name}_dram", a.shape, _mybir.dt.from_np(a.dtype), kind="ExternalInput").ap()
    out = nc.dram_tensor("out_dram", (BATCHES, NT, P, P), F32, kind="ExternalOutput").ap()
    program(nc, args, out)
    r = _run(nc, [arrays], core_ids=[0])
    return r.results[0]["out_dram"].reshape(BATCHES, T, P)
```
